# Optimizing a Trainium2 kernel written in Bass

```python
import numpy as np
import jax
import jax.numpy as jnp

def _softmax(x, axis=-1):
    return jax.nn.softmax(x, axis=axis)

def _gelu(x):
    return jax.nn.gelu(x, approximate=True)

def _silu(x):
    return jax.nn.silu(x)

def _sigmoid(x):
    return jax.nn.sigmoid(x)

def _layernorm(x, axis=-1, eps=1e-05):
    m = jnp.mean(x, axis=axis, keepdims=True)
    v = jnp.var(x, axis=axis, keepdims=True)
    return (x - m) / jnp.sqrt(v + eps)

def _scatter_add(tgt, idx, src, axis=0):
    return tgt.at[idx].add(src)

def _segment_sum(src, seg, n):
    return jax.ops.segment_sum(src, seg, n)
kernel_name = 'mk_gps_d1_gnn_r8_c4d255'

def setup_inputs(seed: int=0):
    np.random.seed(seed)
    _w = jnp.asarray

    def _rec_inputs():
        import jax
        import jax.numpy as jnp
        _gk = jax.random.key(seed)
        x = -0.0003713 + 1 * jax.random.normal(jax.random.fold_in(_gk, 1), (6250, 256), jnp.float32)
        _s = jax.random.randint(jax.random.fold_in(_gk, 2), (100000,), 0, 6250, jnp.int32)
        _d = jax.random.randint(jax.random.fold_in(_gk, 3), (100000,), 0, 6250, jnp.int32)
        _loop = jnp.arange(6250, dtype=jnp.int32)
        src = jnp.concatenate([_s, _d, _loop])
        dst = jnp.concatenate([_d, _s, _loop])
        _o = jnp.argsort(dst, stable=True)
        src = src[_o]
        dst = dst[_o]
        edge_attr_16 = -0.00010739 + 0.99994 * jax.random.normal(jax.random.fold_in(_gk, 12), (206250, 16), jnp.float32)
        edge_attr_4 = jax.random.uniform(jax.random.fold_in(_gk, 13), (206250, 4), jnp.float32, 0.0, 1)
        return (x, src, dst, edge_attr_16, edge_attr_4)
    x, src, dst, edge_attr_16, edge_attr_4 = _rec_inputs()

    def _L0_gnn_setup():
        import jax, jax.numpy as jnp
        import numpy as np
        N = 6250
        E = 100000
        IN_DIM = 256
        H = 8
        D = 32
        T = 4
        F = 16
        NEG_SLOPE = 0.2
        key = jax.random.key(seed)
        ks = jax.random.split(key, 9)
        feat = jax.random.normal(ks[0], (N, IN_DIM), dtype=jnp.float32)
        e_pro = jax.random.normal(ks[1], (E, F), dtype=jnp.float32)
        mask = jax.random.uniform(ks[2], (E, T), dtype=jnp.float32)
        W_n = jax.random.normal(ks[3], (IN_DIM, H * D), dtype=jnp.float32) * (1.0 / np.sqrt(IN_DIM))
        attn_l = jax.random.normal(ks[4], (H, D, T), dtype=jnp.float32) * 0.1
        attn_r = jax.random.normal(ks[5], (H, D, T), dtype=jnp.float32) * 0.1
        attn_m = jax.random.normal(ks[6], (H, F, T), dtype=jnp.float32) * 0.1
        src = jax.random.randint(ks[7], (E,), 0, N, dtype=jnp.int32)
        dst = jax.random.randint(ks[8], (E,), 0, N, dtype=jnp.int32)
        return {'feat': feat, 'e_pro': e_pro, 'mask': mask, 'W_n': W_n, 'attn_l': attn_l, 'attn_r': attn_r, 'attn_m': attn_m, 'src': src, 'dst': dst}
    _L0_gnn_all = _L0_gnn_setup()
    _L0_gnn_in = {k: v for k, v in _L0_gnn_all.items() if k in ('W_n', 'attn_l', 'attn_r', 'attn_m')}
    del _L0_gnn_all

    def _L0_mix_setup():
        import jax, jax.numpy as jnp
        import numpy as np
        HEADS = 8
        DIM_HEAD = 32
        SCALE = DIM_HEAD ** (-0.5)
        EPS = 1e-05

        def _layernorm_gamma(x, gamma):
            mu = jnp.mean(x, axis=-1, keepdims=True)
            var = jnp.var(x, axis=-1, keepdims=True)
            return (x - mu) * jax.lax.rsqrt(var + EPS) * gamma
        key = jax.random.key(seed)
        k1, k2, k3 = jax.random.split(key, 3)
        B, N, D = (8, 2048, 256)
        hidden = HEADS * DIM_HEAD
        x = jax.random.normal(k1, (B, N, D), dtype=jnp.float32)
        Wqkv = jax.random.normal(k2, (D, 3 * hidden), dtype=jnp.float32) * D ** (-0.5)
        Wout = jax.random.normal(k3, (hidden, D), dtype=jnp.float32) * hidden ** (-0.5)
        gamma = jnp.ones((D,), dtype=jnp.float32)
        return {'x': x, 'Wqkv': Wqkv, 'Wout': Wout, 'gamma': gamma}
    _L0_mix_all = _L0_mix_setup()
    _L0_mix_in = {k: v for k, v in _L0_mix_all.items() if k in ('Wqkv', 'Wout', 'gamma')}
    del _L0_mix_all

    def _L0_ffn_setup():
        import jax, jax.numpy as jnp
        import numpy as np
        BN_EPS = 0.001

        def _bn(h, g, b, m, v):
            return g * (h - m) * jax.lax.rsqrt(v + BN_EPS) + b
        key = jax.random.key(seed)
        ks = jax.random.split(key, 8)
        B, F, Df = (256, 64, 256)
        E, H, D = (8, 256, 256)
        s1 = 1.0 / np.sqrt(Df)
        s2 = 1.0 / np.sqrt(H)
        return {'x': jax.random.normal(ks[0], (B, F, Df), jnp.float32), 'Wr': jax.random.normal(ks[1], (Df, E), jnp.float32) * s1, 'br': jnp.zeros((E,), jnp.float32), 'W1': jax.random.normal(ks[2], (E, Df, H), jnp.float32) * s1, 'b1': jnp.zeros((E, H), jnp.float32), 'g1': jnp.ones((E, H), jnp.float32), 'be1': jnp.zeros((E, H), jnp.float32), 'm1': jnp.zeros((E, H), jnp.float32), 'v1': jnp.ones((E, H), jnp.float32), 'W2': jax.random.normal(ks[3], (E, H, H), jnp.float32) * s2, 'b2': jnp.zeros((E, H), jnp.float32), 'g2': jnp.ones((E, H), jnp.float32), 'be2': jnp.zeros((E, H), jnp.float32), 'm2': jnp.zeros((E, H), jnp.float32), 'v2': jnp.ones((E, H), jnp.float32), 'Wo': jax.random.normal(ks[4], (E, H, D), jnp.float32) * s2, 'bo': jnp.zeros((E, D), jnp.float32)}
    _L0_ffn_all = _L0_ffn_setup()
    _L0_ffn_in = {k: v for k, v in _L0_ffn_all.items() if k in ('Wr', 'br', 'W1', 'b1', 'g1', 'be1', 'm1', 'v1', 'W2', 'b2', 'g2', 'be2', 'm2', 'v2', 'Wo', 'bo')}
    del _L0_ffn_all
    return {'x': x, 'src': src, 'dst': dst, 'edge_attr_16': edge_attr_16, 'edge_attr_4': edge_attr_4, 'L0_gnn_W_n': _L0_gnn_in['W_n'], 'L0_gnn_attn_l': _L0_gnn_in['attn_l'], 'L0_gnn_attn_r': _L0_gnn_in['attn_r'], 'L0_gnn_attn_m': _L0_gnn_in['attn_m'], 'L0_mix_Wqkv': _L0_mix_in['Wqkv'], 'L0_mix_Wout': _L0_mix_in['Wout'], 'L0_mix_gamma': _L0_mix_in['gamma'], 'L0_ffn_Wr': _L0_ffn_in['Wr'], 'L0_ffn_br': _L0_ffn_in['br'], 'L0_ffn_W1': _L0_ffn_in['W1'], 'L0_ffn_b1': _L0_ffn_in['b1'], 'L0_ffn_g1': _L0_ffn_in['g1'], 'L0_ffn_be1': _L0_ffn_in['be1'], 'L0_ffn_m1': _L0_ffn_in['m1'], 'L0_ffn_v1': _L0_ffn_in['v1'], 'L0_ffn_W2': _L0_ffn_in['W2'], 'L0_ffn_b2': _L0_ffn_in['b2'], 'L0_ffn_g2': _L0_ffn_in['g2'], 'L0_ffn_be2': _L0_ffn_in['be2'], 'L0_ffn_m2': _L0_ffn_in['m2'], 'L0_ffn_v2': _L0_ffn_in['v2'], 'L0_ffn_Wo': _L0_ffn_in['Wo'], 'L0_ffn_bo': _L0_ffn_in['bo']}

def reference(x, src, dst, edge_attr_16, edge_attr_4, L0_gnn_W_n, L0_gnn_attn_l, L0_gnn_attn_r, L0_gnn_attn_m, L0_mix_Wqkv, L0_mix_Wout, L0_mix_gamma, L0_ffn_Wr, L0_ffn_br, L0_ffn_W1, L0_ffn_b1, L0_ffn_g1, L0_ffn_be1, L0_ffn_m1, L0_ffn_v1, L0_ffn_W2, L0_ffn_b2, L0_ffn_g2, L0_ffn_be2, L0_ffn_m2, L0_ffn_v2, L0_ffn_Wo, L0_ffn_bo):
    import jax
    import jax.numpy as jnp

    def _L0_gnn_ref(feat, e_pro, mask, W_n, attn_l, attn_r, attn_m, src, dst):
        import jax, jax.numpy as jnp
        import numpy as np
        N = 6250
        E = 100000
        IN_DIM = 256
        H = 8
        D = 32
        T = 4
        F = 16
        NEG_SLOPE = 0.2
        feat_src = (feat @ W_n).reshape(N, H, D)
        el = jnp.einsum('nhd,hdt->nht', feat_src, attn_l)
        er = jnp.einsum('nhd,hdt->nht', feat_src, attn_r)
        em = jnp.einsum('ef,hft->eht', e_pro, attn_m)
        left = jnp.einsum('eht,et->eh', el[src], mask)
        right = jnp.einsum('eht,et->eh', er[dst], mask)
        em_e = jnp.einsum('eht,et->eh', em, mask)
        e = (left + right + em_e) / 3.0
        e = jnp.where(e > 0, e, NEG_SLOPE * e)
        e_max = jax.ops.segment_max(e, dst, num_segments=N)
        e_exp = jnp.exp(e - e_max[dst])
        e_sum = jax.ops.segment_sum(e_exp, dst, num_segments=N)
        a = e_exp / e_sum[dst]
        msg = feat_src[src] * a[:, :, None]
        rst = jax.ops.segment_sum(msg, dst, num_segments=N)
        return rst.reshape(N, H * D)

    def _L0_mix_ref(x, Wqkv, Wout, gamma):
        import jax, jax.numpy as jnp
        import numpy as np
        HEADS = 8
        DIM_HEAD = 32
        SCALE = DIM_HEAD ** (-0.5)
        EPS = 1e-05

        def _layernorm_gamma(x, gamma):
            mu = jnp.mean(x, axis=-1, keepdims=True)
            var = jnp.var(x, axis=-1, keepdims=True)
            return (x - mu) * jax.lax.rsqrt(var + EPS) * gamma
        B, N, D = x.shape
        qkv = x @ Wqkv
        q, k, v = jnp.split(qkv, 3, axis=-1)

        def to_heads(t):
            return t.reshape(B, N, HEADS, DIM_HEAD).transpose(0, 2, 1, 3)
        q, k, v = map(to_heads, (q, k, v))
        q = jax.nn.softmax(q, axis=-1) * SCALE
        k = jax.nn.softmax(k, axis=2)
        context = jnp.einsum('bhnd,bhne->bhde', k, v)
        out = jnp.einsum('bhde,bhnd->bhne', context, q)
        out = out.transpose(0, 2, 1, 3).reshape(B, N, HEADS * DIM_HEAD)
        out = out @ Wout
        return _layernorm_gamma(out, gamma)

    def _L0_ffn_ref(x, Wr, br, W1, b1, g1, be1, m1, v1, W2, b2, g2, be2, m2, v2, Wo, bo):
        import jax, jax.numpy as jnp
        import numpy as np
        BN_EPS = 0.001

        def _bn(h, g, b, m, v):
            return g * (h - m) * jax.lax.rsqrt(v + BN_EPS) + b
        feat = jnp.mean(x, axis=0)
        w = jax.nn.softmax(feat @ Wr + br, axis=-1)
        h = jnp.einsum('bfd,edh->bfeh', x, W1) + b1
        h = jax.nn.relu(_bn(h, g1, be1, m1, v1))
        h = jnp.einsum('bfeh,ehk->bfek', h, W2) + b2
        h = jax.nn.relu(_bn(h, g2, be2, m2, v2))
        y = jnp.einsum('bfeh,ehd->bfed', h, Wo) + bo
        return jnp.einsum('bfed,fe->bfd', y, w)
    xn = _layernorm(x, axis=-1)
    x = x + _L0_gnn_ref(xn, edge_attr_16, edge_attr_4, L0_gnn_W_n, L0_gnn_attn_l, L0_gnn_attn_r, L0_gnn_attn_m, src, dst) + _L0_mix_ref(xn[None], L0_mix_Wqkv, L0_mix_Wout, L0_mix_gamma)[0]
    x = x + _L0_ffn_ref(_layernorm(x, axis=-1)[None], L0_ffn_Wr, L0_ffn_br, L0_ffn_W1, L0_ffn_b1, L0_ffn_g1, L0_ffn_be1, L0_ffn_m1, L0_ffn_v1, L0_ffn_W2, L0_ffn_b2, L0_ffn_g2, L0_ffn_be2, L0_ffn_m2, L0_ffn_v2, L0_ffn_Wo, L0_ffn_bo)[0]
    return x

_drawn_inputs = setup_inputs


def setup_inputs(seed=0):
    import zlib

    import numpy as np

    out = dict(_drawn_inputs(seed))
    spreads = {'L0_mix_gamma': (1.0, 0.2),
     'L0_ffn_br': (0.0, 0.341),
     'L0_ffn_b1': (0.0, 0.407),
     'L0_ffn_g1': (1.0, 0.2),
     'L0_ffn_be1': (0.0, 0.422),
     'L0_ffn_m1': (0.0, 0.403),
     'L0_ffn_v1': (1.0, 0.6),
     'L0_ffn_b2': (0.0, 0.287),
     'L0_ffn_g2': (1.0, 0.2),
     'L0_ffn_be2': (0.0, 0.307),
     'L0_ffn_m2': (0.0, 0.296),
     'L0_ffn_v2': (1.0, 0.6),
     'L0_ffn_bo': (0.0, 0.1)}
    factors = {'edge_attr_16': 3.168,
     'edge_attr_4': 2.792,
     'L0_gnn_attn_r': 3.562,
     'L0_gnn_attn_m': 3.044}
    for name, (base, spread) in spreads.items():
        noise = np.random.default_rng([zlib.crc32(name.encode()), seed]).standard_normal(out[name].shape)
        drawn = base * np.exp(spread * noise) if base else spread * noise
        out[name] = jnp.asarray(drawn.astype(out[name].dtype))
    for name, factor in factors.items():
        out[name] = (out[name] * factor).astype(out[name].dtype)
    return out
```

```python
from contextlib import ExitStack

import concourse.bass as bass
from concourse import mybir

F32 = mybir.dt.float32
BF16 = mybir.dt.bfloat16
I32 = mybir.dt.int32
U16 = mybir.dt.uint16
ALU = mybir.AluOpType
ACT = mybir.ActivationFunctionType
AX_X = mybir.AxisListType.X
RMAX = bass.bass_isa.ReduceOp.max

P = 128
N = 6250
NT = -(-N // P)
NP = NT * P
LAST = N - (NT - 1) * P
D = 256
KD = D // P
H = 8
DH = D // H
T = 4
HT = H * T
F = 16
E = 206250
C = 8
GE = C * P
G = -(-E // GE)
EP = G * GE
PAD_DST = 8191
V = G + NT - 1
VP = 2 * P
ROW = D + HT
HW = DH + 1
SUMS = H * HW + H
SLOTS = 4
NEG = -1.0e30
SLOPE = 0.2
LN_EPS = 1e-5
BN_EPS = 1e-3
SCALE = DH ** -0.5
X = 8
EL = EP // P


class Kit:

    def __init__(self, nc, ctx):
        self.nc, self.ctx = nc, ctx

    def sb(self, name, shape, dt=F32):
        return self.ctx.enter_context(self.nc.sbuf_tensor(name, shape, dt))

    def ps(self, name, shape, dt=F32):
        return self.ctx.enter_context(self.nc.psum_tensor(name, shape, dt))

    def sem(self, name):
        return self.ctx.enter_context(self.nc.semaphore(name))


def row_of(t, n=1):
    return bass.ds(t, n)


def settle(eng):
    eng.nop(nofuse=True)


def later(t):
    return not (isinstance(t, int) and t < 2)


def tiles(eng, body, follow=None):

    def step(t, s):
        body(t, s)
        if follow is not None and not (isinstance(t, int) and t == 0):
            follow(t - 1, 1 - s)

    for t in range(3):
        step(t, t % 2)
    with eng.Fori(0, (NT - 3) // 2) as k:
        for u in (0, 1):
            step(k * 2 + (3 + u), (3 + u) % 2)
    if follow is not None:
        follow(NT - 1, (NT - 1) % 2)


def phase_nodes(nc, io, scr):
    with ExitStack() as ctx:
        kit = Kit(nc, ctx)
        sb, ps, sem = kit.sb, kit.ps, kit.sem
        wcat = sb("wcat", [P, KD, D + 2 * HT])
        wqkv = sb("wqkv", [P, KD, 3 * D])
        wnT = sb("wnT", [P, KD, D])
        wout = sb("wout", [P, KD, D])
        bd = sb("bd", [P, KD, 2 * HT])
        gamma = sb("gamma", [P, D])
        ident = sb("ident", [P, P])
        eps = sb("eps", [P, 1])
        xin = sb("xin", [P, 2, D])
        st = sb("st", [P, 2, 6])
        mv = sb("mv", [P, 2, 2])
        rstd = sb("rstd", [P, 2, 1])
        xn = sb("xn", [P, 2, D])
        xnT = sb("xnT", [P, 2, KD, P])
        trow = sb("trow", [P, 2, D + 2 * HT])
        er3 = sb("er3", [P, 2, 3 * HT], BF16)
        er_a = sb("er_a", [P, 2, HT])
        er_b = sb("er_b", [P, 2, HT])
        ktile = sb("ktile", [P, NT, D])
        vtile = sb("vtile", [P, NT, D])
        qtile = sb("qtile", [P, NT, D])
        real = sb("real", [P, NT])
        kmax = sb("kmax", [P, D])
        kmaxb = sb("kmaxb", [P, D])
        kexp = sb("kexp", [P, 2, D])
        ctx_sb = sb("ctx_sb", [P, KD, P])
        ctxT = sb("ctxT", [P, KD, P])
        rsum = sb("rsum", [P, KD])
        mixw = sb("mixw", [P, KD, D])
        qmax = sb("qmax", [P, H])
        qsm = sb("qsm", [P, 2, D])
        qsum = sb("qsum", [P, H])
        qT = sb("qT", [P, 2, KD, P])
        xre = sb("xre", [P, 2, D])
        mixo = sb("mixo", [P, 2, D])
        mixf = sb("mixf", [P, 2, D])

        ps_tr = [ps(f"ps_tr{i}", [P, KD, P]) for i in range(2)]
        ps_ft = [ps(f"ps_ft{i}", [P, 512]) for i in range(2)]
        ps_qk = [ps(f"ps_qk{i}", [P, 512]) for i in range(2)]
        ps_v = [ps(f"ps_v{i}", [P, 512]) for i in range(2)]

        weights_in = sem("n_weights_in")
        blocks_in = sem("n_blocks_in")
        zeroed = sem("n_zeroed")
        ident_ok = sem("n_ident_ok")
        pool_step = sem("n_pool_step")
        eps_ok = sem("n_eps_ok")
        attn_w = sem("n_attn_w")
        attn_wc = sem("n_attn_wc")
        x_in = [sem(f"n_x_in{i}") for i in range(2)]
        stats = sem("n_stats")
        var_ok = sem("n_var_ok")
        std = sem("n_std")
        rstd_ok = sem("n_rstd_ok")
        xn_ok = sem("n_xn_ok")
        xnT_ps = sem("n_xnT_ps")
        xnT_ok = sem("n_xnT_ok")
        proj = sem("n_proj")
        trow_ok = sem("n_trow_ok")
        kept = sem("n_kept")
        ermax = sem("n_ermax")
        er_hi = sem("n_er_hi")
        er_r1 = sem("n_er_r1")
        er_mid = sem("n_er_mid")
        er_r2 = sem("n_er_r2")
        er_ok = sem("n_er_ok")
        table_out = [sem(f"n_table_out{i}") for i in range(2)]
        kmax_ok = sem("n_kmax_ok")
        kmaxb_ok = sem("n_kmaxb_ok")
        ksub = sem("n_ksub")
        kexp_ok = sem("n_kexp_ok")
        ctx_mm = sem("n_ctx_mm")
        ctx_z = sem("n_ctx_z")
        ctx_c = sem("n_ctx_c")
        ctxT_ps = sem("n_ctxT_ps")
        ctxT_ok = sem("n_ctxT_ok")
        mix_mm = sem("n_mix_mm")
        mixw_ok = sem("n_mixw_ok")
        rsum_ok = sem("n_rsum_ok")
        qmax_ok = sem("n_qmax_ok")
        qsub = sem("n_qsub")
        qexp = sem("n_qexp")
        qsum_ok = sem("n_qsum_ok")
        qrec = sem("n_qrec")
        qsm_ok = sem("n_qsm_ok")
        qT_ps = sem("n_qT_ps")
        qT_ok = sem("n_qT_ok")
        out_mm = sem("n_out_mm")
        xre_in = [sem(f"n_xre_in{i}") for i in range(2)]
        ln_st = sem("n_ln_st")
        ln_var = sem("n_ln_var")
        ln_std = sem("n_ln_std")
        ln_rstd = sem("n_ln_rstd")
        ln_n = sem("n_ln_n")
        ln_g = sem("n_ln_g")
        mixf_ok = sem("n_mixf_ok")
        mix_out = [sem(f"n_mix_out{i}") for i in range(2)]

        block = ctx.enter_context(nc.Block())

        @block.sync
        def _(sp):
            loads = [
                (wcat[:, :, 0:D], io["W_n"].rearrange("(c p) n -> p c n", p=P)),
                (wnT[:, :, :], io["W_nT"].rearrange("(c p) n -> p c n", p=P)),
                (wqkv[:, :, :], io["Wqkv"].rearrange("(c p) n -> p c n", p=P)),
                (wout[:, :, :], io["Wout"].rearrange("(c p) n -> p c n", p=P)),
                (gamma[:, :], io["gamma"].rearrange("(a n) -> a n", a=1).broadcast_to([P, D])),
            ]
            for dst, src in loads:
                sp.dma_start(dst, src).then_inc(weights_in, 16)
            sp.wait_ge(zeroed, 1)
            for h in range(H):
                rows = slice(DH * (h % 4), DH * (h % 4) + DH)
                for side, name in enumerate(("attn_l", "attn_r")):
                    sp.dma_start(bd[rows, h // 4, HT * side + T * h:HT * side + T * h + T],
                                 io[name][h]).then_inc(blocks_in, 16)

            def load_x(t, s):
                if later(t):
                    sp.wait_ge(xn_ok, t - 1)
                sp.dma_start(xin[:, s, :], io["x"][row_of(t), :, :].rearrange("a p n -> (a p) n")) \
                    .then_inc(x_in[s], 16)

            tiles(sp, load_x)

            def reload(t, s):
                if later(t):
                    sp.wait_ge(mixf_ok, t - 1)
                sp.dma_start(xre[:, s, :], io["x"][row_of(t), :, :].rearrange("a p n -> (a p) n")) \
                    .then_inc(xre_in[s], 16)

            tiles(sp, reload)

        @block.gpsimd
        def _(pool):
            pool.memset(bd[:, :, :], 0.0).then_inc(zeroed, 1)
            pool.memset(ident[:, :], 0.0).then_inc(pool_step, 1)
            pool.memset(real[:, :], 1.0).then_inc(pool_step, 1)
            pool.memset(eps[:, :], LN_EPS).then_inc(eps_ok, 1)
            pool.wait_ge(pool_step, 2)
            pool.affine_select(out=ident[:, :], in_=ident[:, :], compare_op=ALU.not_equal, fill=1.0,
                               base=0, pattern=[[-1, P]], channel_multiplier=1).then_inc(ident_ok, 1)
            pool.affine_select(out=real[:, NT - 1:NT], in_=real[:, NT - 1:NT], compare_op=ALU.is_ge,
                               fill=0.0, base=LAST - 1, pattern=[[0, 1]],
                               channel_multiplier=-1).then_inc(ident_ok, 1)

            def store_table(t, s):
                pool.wait_ge(trow_ok, t + 1)
                pool.wait_ge(er_ok, t + 1)
                pool.wait_ge(ident_ok, 2)
                pool.dma_start(scr["table"][row_of(t), :, :].rearrange("a p n -> (a p) n"),
                               trow[:, s, 0:ROW]).then_inc(table_out[s], 16)
                pool.dma_start(scr["er"][row_of(t), :, :].rearrange("a p n -> (a p) n"),
                               er3[:, s, :]).then_inc(table_out[s], 16)

            tiles(pool, store_table)
            pool.wait_ge(kmax_ok, NT)
            pool.partition_all_reduce(kmaxb[:, :], kmax[:, :], P, RMAX).then_inc(kmaxb_ok, 1)

            def store_mix(t, s):
                pool.wait_ge(mixf_ok, t + 1)
                pool.wait_ge(ident_ok, 2)
                pool.dma_start(scr["xmix"][row_of(t), :, :].rearrange("a p n -> (a p) n"),
                               mixf[:, s, :]).then_inc(mix_out[s], 16)

            tiles(pool, store_mix)
            pool.wait_ge(table_out[0], 32 * ((NT + 1) // 2))
            pool.wait_ge(table_out[1], 32 * (NT // 2))
            pool.wait_ge(mix_out[0], 16 * ((NT + 1) // 2))
            pool.wait_ge(mix_out[1], 16 * (NT // 2))

        @block.scalar
        def _(act):
            act.wait_ge(attn_w, 1)
            for k in range(KD):
                act.copy(wcat[:, k, D:D + 2 * HT], ps_ft[k][:, 0:2 * HT]).then_inc(attn_wc, 1)
            act.wait_ge(eps_ok, 1)

            def turn(t, s):
                act.wait_ge(var_ok, t + 1)
                act.activation(rstd[:, s, :], mv[:, s, 1:2], ACT.Sqrt, bias=eps[:, 0:1]).then_inc(std, 1)
                act.wait_ge(xnT_ps, t + 1)
                if later(t):
                    act.wait_ge(proj, t - 1)
                act.copy(xnT[:, s, :, :], ps_tr[s][:, :, :]).then_inc(xnT_ok, 1)

            def keep(t, s):
                act.wait_ge(proj, t + 1)
                if later(t):
                    act.wait_ge(er_ok, t - 1)
                    act.wait_ge(table_out[s], (t - s) * 16)
                act.copy(trow[:, s, :], ps_ft[s][:, 0:D + 2 * HT]).then_inc(trow_ok, 1)
                act.copy(qtile[:, row_of(t), :].rearrange("p a n -> p (a n)"),
                         ps_qk[s][:, 0:D]).then_inc(kept, 1)
                act.copy(ktile[:, row_of(t), :].rearrange("p a n -> p (a n)"),
                         ps_qk[s][:, D:2 * D]).then_inc(kept, 1)
                act.copy(vtile[:, row_of(t), :].rearrange("p a n -> p (a n)"),
                         ps_v[s][:, 0:D]).then_inc(kept, 1)

            tiles(act, turn, keep)

            def exp_k(t, s):
                act.wait_ge(ksub, t + 1)
                act.activation(kexp[:, s, :], kexp[:, s, :], ACT.Exp).then_inc(kexp_ok, 1)

            tiles(act, exp_k)

            def soften(t, s):
                act.wait_ge(qsub, t + 1)
                act.activation(qsm[:, s, :], qsm[:, s, :], ACT.Exp).then_inc(qexp, 1)
                act.wait_ge(qT_ps, t + 1)
                if later(t):
                    act.wait_ge(out_mm, t - 1)
                act.copy(qT[:, s, :, :], ps_tr[s][:, :, :]).then_inc(qT_ok, 1)

            def deviate(t, s):
                act.wait_ge(ln_var, t + 1)
                act.activation(rstd[:, s, :], mv[:, s, 1:2], ACT.Sqrt, bias=eps[:, 0:1]).then_inc(ln_std, 1)

            tiles(act, soften, deviate)

        @block.vector
        def _(dve):
            def norm(t, s):
                dve.wait_ge(x_in[s], (t - s) * 8 + 16)
                dve.bn_stats(st[:, s, :], xin[:, s, :]).then_inc(stats, 1)
                dve.wait_ge(stats, t + 1)
                settle(dve)
                dve.bn_aggr(mv[:, s, :], st[:, s, :]).then_inc(var_ok, 1)
                dve.wait_ge(std, t + 1)
                dve.reciprocal(rstd[:, s, :], rstd[:, s, :]).then_inc(rstd_ok, 1)
                dve.wait_ge(rstd_ok, t + 1)
                if later(t):
                    dve.wait_ge(xnT_ps, t - 1)
                dve.tensor_scalar(xn[:, s, :], xin[:, s, :], mv[:, s, 0:1], rstd[:, s, 0:1],
                                  ALU.subtract, ALU.mult).then_inc(xn_ok, 1)

            def split(t, s):
                dve.wait_ge(trow_ok, t + 1)
                if later(t):
                    dve.wait_ge(table_out[s], (t - s) * 16)
                er = trow[:, s, ROW:ROW + HT]
                dve.tensor_copy(er3[:, s, 0:HT], er).then_inc(er_hi, 1)
                dve.wait_ge(er_hi, t + 1)
                dve.tensor_tensor(er_a[:, s, :], er, er3[:, s, 0:HT], ALU.subtract).then_inc(er_r1, 1)
                dve.wait_ge(er_r1, t + 1)
                dve.tensor_copy(er3[:, s, HT:2 * HT], er_a[:, s, :]).then_inc(er_mid, 1)
                dve.wait_ge(er_mid, t + 1)
                dve.tensor_tensor(er_b[:, s, :], er_a[:, s, :], er3[:, s, HT:2 * HT],
                                  ALU.subtract).then_inc(er_r2, 1)
                dve.wait_ge(er_r2, t + 1)
                dve.tensor_copy(er3[:, s, 2 * HT:3 * HT], er_b[:, s, :]).then_inc(er_ok, 1)
                kk = ktile[:, row_of(t), :].rearrange("p a n -> p (a n)")
                dve.wait_ge(kept, t * 3 + 2)
                if isinstance(t, int) and t == 0:
                    dve.tensor_copy(kmax[:, :], kk).then_inc(kmax_ok, 1)
                else:
                    dve.wait_ge(kmax_ok, t)
                    dve.tensor_tensor(kmax[:, :], kmax[:, :], kk, ALU.max).then_inc(kmax_ok, 1)

            tiles(dve, norm, split)
            dve.wait_ge(kmaxb_ok, 1)

            def sub_k(t, s):
                dve.wait_ge(kept, 3 * NT)
                if later(t):
                    dve.wait_ge(ctx_mm, t - 1)
                dve.tensor_tensor(kexp[:, s, :], ktile[:, row_of(t), :].rearrange("p a n -> p (a n)"),
                                  kmaxb[:, :], ALU.subtract).then_inc(ksub, 1)

            tiles(dve, sub_k)

            dve.memset(ctx_sb[:, :, :], 0.0).then_inc(ctx_z, 1)
            dve.wait_ge(ctx_mm, NT)
            dve.wait_ge(ctx_z, 1)
            for c in range(KD):
                for j in range(4):
                    r = slice(DH * j, DH * j + DH)
                    dve.tensor_copy(ctx_sb[r, c, DH * j:DH * j + DH],
                                    ps_ft[c][r, P * c + DH * j:P * c + DH * j + DH]).then_inc(ctx_c, 1)
                dve.reciprocal(rsum[:, c:c + 1], ps_ft[c][:, D:D + 1]).then_inc(rsum_ok, 1)
            dve.wait_ge(ctxT_ps, 1)
            dve.tensor_copy(ctxT[:, :, :], ps_tr[0][:, :, :]).then_inc(ctxT_ok, 1)
            dve.wait_ge(mix_mm, 1)
            dve.wait_ge(rsum_ok, 2)
            for c in range(KD):
                dve.tensor_scalar(mixw[:, c, :], ps_qk[c][:, 0:D], rsum[:, c:c + 1], SCALE,
                                  ALU.mult, ALU.mult).then_inc(mixw_ok, 1)

            def soften(t, s):
                q = qtile[:, row_of(t), :].rearrange("p a (h d) -> p (a h) d", h=H)
                qs = qsm[:, s, :].rearrange("p (h d) -> p h d", h=H)
                dve.tensor_reduce(qmax[:, :], q, AX_X, ALU.max).then_inc(qmax_ok, 1)
                dve.wait_ge(qmax_ok, t + 1)
                if later(t):
                    dve.wait_ge(qT_ps, t - 1)
                dve.tensor_tensor(qs, q, qmax[:, :].unsqueeze(2).broadcast_to([P, H, DH]),
                                  ALU.subtract).then_inc(qsub, 1)
                dve.wait_ge(qexp, t + 1)
                dve.tensor_reduce(qsum[:, :], qs, AX_X, ALU.add).then_inc(qsum_ok, 1)
                dve.wait_ge(qsum_ok, t + 1)
                dve.reciprocal(qsum[:, :], qsum[:, :]).then_inc(qrec, 1)
                dve.wait_ge(qrec, t + 1)
                dve.tensor_tensor(qs, qs, qsum[:, :].unsqueeze(2).broadcast_to([P, H, DH]),
                                  ALU.mult).then_inc(qsm_ok, 1)

            def finish(t, s):
                dve.wait_ge(out_mm, t + 1)
                dve.bn_stats(st[:, s, :], ps_v[s][:, 0:D]).then_inc(ln_st, 1)
                dve.wait_ge(ln_st, t + 1)
                settle(dve)
                dve.bn_aggr(mv[:, s, :], st[:, s, :]).then_inc(ln_var, 1)
                dve.wait_ge(ln_std, t + 1)
                dve.reciprocal(rstd[:, s, :], rstd[:, s, :]).then_inc(ln_rstd, 1)
                dve.wait_ge(ln_rstd, t + 1)
                dve.tensor_scalar(mixo[:, s, :], ps_v[s][:, 0:D], mv[:, s, 0:1], rstd[:, s, 0:1],
                                  ALU.subtract, ALU.mult).then_inc(ln_n, 1)
                dve.wait_ge(ln_n, t + 1)
                dve.tensor_tensor(mixo[:, s, :], mixo[:, s, :], gamma[:, :], ALU.mult).then_inc(ln_g, 1)
                dve.wait_ge(ln_g, t + 1)
                if later(t):
                    dve.wait_ge(mix_out[s], (t - s) * 8)
                dve.wait_ge(xre_in[s], (t - s) * 8 + 16)
                dve.tensor_tensor(mixf[:, s, :], mixo[:, s, :], xre[:, s, :],
                                  ALU.add).then_inc(mixf_ok, 1)

            tiles(dve, soften, finish)

        @block.tensor
        def _(pe):
            pe.wait_ge(weights_in, 16 * 5)
            pe.wait_ge(blocks_in, 16 * 2 * H)
            for k in range(KD):
                for c in range(KD):
                    last = pe.matmul(ps_ft[k][:, 0:2 * HT], wnT[:, c, k * P:k * P + P], bd[:, c, :],
                                     start=(c == 0), stop=(c == KD - 1))
            last.then_inc(attn_w, 1)
            pe.wait_ge(attn_wc, KD)
            pe.wait_ge(ident_ok, 2)

            def turn(t, s):
                pe.wait_ge(xn_ok, t + 1)
                if later(t):
                    pe.wait_ge(xnT_ok, t - 1)
                for k in range(KD):
                    last = pe.transpose(ps_tr[s][:, k, :], xn[:, s, k * P:k * P + P], ident[:, :])
                last.then_inc(xnT_ps, 1)

            def project(t, s):
                pe.wait_ge(xnT_ok, t + 1)
                if later(t):
                    pe.wait_ge(kept, (t - 1) * 3)
                for k in range(KD):
                    pe.matmul(ps_ft[s][:, 0:D + 2 * HT], xnT[:, s, k, :], wcat[:, k, :],
                              start=(k == 0), stop=(k == KD - 1))
                for k in range(KD):
                    pe.matmul(ps_qk[s][:, :], xnT[:, s, k, :], wqkv[:, k, 0:2 * D],
                              start=(k == 0), stop=(k == KD - 1))
                for k in range(KD):
                    last = pe.matmul(ps_v[s][:, 0:D], xnT[:, s, k, :], wqkv[:, k, 2 * D:3 * D],
                                     start=(k == 0), stop=(k == KD - 1))
                last.then_inc(proj, 1)

            tiles(pe, turn, project)
            pe.wait_ge(kept, 3 * NT)
            pe.wait_ge(kmax_ok, NT)
            pe.wait_ge(trow_ok, NT)

            def context(t, s, start, stop):
                pe.wait_ge(kexp_ok, t + 1)
                for c in range(KD):
                    pe.matmul(ps_ft[c][:, 0:D], kexp[:, s, c * P:c * P + P],
                              vtile[:, row_of(t), :].rearrange("p a n -> p (a n)"),
                              start=start, stop=stop, skip_group_check=True)
                for c in range(KD):
                    last = pe.matmul(ps_ft[c][:, D:D + 1], kexp[:, s, c * P:c * P + P],
                                     real[:, row_of(t)], start=False, stop=stop, skip_group_check=True)
                last.then_inc(ctx_mm, 1)

            context(0, 0, True, False)
            with pe.Fori(0, (NT - 3) // 2) as k:
                for u in (0, 1):
                    context(k * 2 + (1 + u), (1 + u) % 2, False, False)
            context(NT - 2, 1, False, False)
            context(NT - 1, 0, False, True)

            pe.wait_ge(ctx_c, 2 * 4)
            for c in range(KD):
                last = pe.transpose(ps_tr[0][:, c, :], ctx_sb[:, c, :], ident[:, :])
            last.then_inc(ctxT_ps, 1)
            pe.wait_ge(ctxT_ok, 1)
            for c in range(KD):
                last = pe.matmul(ps_qk[c][:, 0:D], ctxT[:, c, :], wout[:, c, :], start=True, stop=True)
            last.then_inc(mix_mm, 1)
            pe.wait_ge(mixw_ok, KD)

            def turn_q(t, s):
                pe.wait_ge(qsm_ok, t + 1)
                if later(t):
                    pe.wait_ge(qT_ok, t - 1)
                for k in range(KD):
                    last = pe.transpose(ps_tr[s][:, k, :], qsm[:, s, k * P:k * P + P], ident[:, :])
                last.then_inc(qT_ps, 1)

            def attend(t, s):
                pe.wait_ge(qT_ok, t + 1)
                if later(t):
                    pe.wait_ge(ln_n, t - 1)
                for k in range(KD):
                    last = pe.matmul(ps_v[s][:, 0:D], qT[:, s, k, :], mixw[:, k, :],
                                     start=(k == 0), stop=(k == KD - 1))
                last.then_inc(out_mm, 1)

            tiles(pe, turn_q, attend)


def phase_edge_tables(nc, io, scr):
    with ExitStack() as ctx:
        kit = Kit(nc, ctx)
        sb, sem = kit.sb, kit.sem
        d_em = sb("d_em", [P, EL], I32)
        dn_em = sb("dn_em", [P, EL], I32)
        d_lin = sb("d_lin", [P, EL], I32)
        dp_lin = sb("dp_lin", [P, EL], I32)
        dm = sb("dm", [P, EL // C, 2 * C])
        d16 = sb("d16", [P, EL], U16)
        same = sb("same", [P, EL])
        pen = sb("pen", [P, EL], BF16)
        gf = sb("gf", [P, G - 1], I32)
        gt = sb("gt", [P, G - 1], I32)
        gidx = sb("gidx", [P, G - 1], I32)
        gb = sb("gb", [P, G - 1])
        vcol = sb("vcol", [P, 2], I32)
        vf = sb("vf", [P, 2])
        cmp = sb("cmp", [P, 2, G - 1])
        gt_f = sb("gt_f", [P, 2, 2])
        gt_i = sb("gt_i", [P, 2, 2], I32)
        loaded = sem("e_loaded")
        iotas = sem("e_iotas")
        step = sem("e_step")
        dm_ok = sem("e_dm_ok")
        d16_ok = sem("e_d16_ok")
        pen_ok = sem("e_pen_ok")
        visits_ok = sem("e_visits_ok")
        stored = sem("e_stored")
        block = ctx.enter_context(nc.Block())

        @block.sync
        def _(sp):
            for dst, name in ((d_em, "dst_em"), (dn_em, "dst_next_em"), (d_lin, "dst_lin"), (dp_lin, "dst_prev_lin")):
                sp.dma_start(dst[:, :], io[name].rearrange("(p n) -> p n", p=P)).then_inc(loaded, 16)
            sp.dma_start(gf[:, :], io["group_first"].rearrange("(a n) -> a n", a=1).broadcast_to([P, G - 1])) \
                .then_inc(loaded, 16)
            sp.wait_ge(dm_ok, 2)
            sp.dma_start(scr["dm"].rearrange("g p c -> (g p c)").rearrange("(q n) -> q n", q=P),
                         dm[:, :, :].rearrange("p a b -> p (a b)")).then_inc(stored, 16)
            sp.wait_ge(d16_ok, 1)
            sp.dma_start(scr["dst16"].rearrange("(p n) -> p n", p=P), d16[:, :]).then_inc(stored, 16)
            sp.wait_ge(pen_ok, 1)
            sp.dma_start(scr["pen"][0:EP].rearrange("(p n) -> p n", p=P), pen[:, :]).then_inc(stored, 16)
            sp.dma_start(scr["pen"][EP:EP + 1].rearrange("(p n) -> p n", p=1), pen[0:1, 0:1]).then_inc(stored, 16)
            sp.wait_ge(visits_ok, 1)
            for k in range(2):
                sp.dma_start(scr["visit_group"][k * P:(k + 1) * P].rearrange("(p a) -> p a", a=1),
                             gt_i[:, 0, k:k + 1]).then_inc(stored, 16)
                sp.dma_start(scr["visit_tile"][k * P:(k + 1) * P].rearrange("(p a) -> p a", a=1),
                             gt_i[:, 1, k:k + 1]).then_inc(stored, 16)
                sp.dma_start(scr["visit_tile_f"][k * P:(k + 1) * P].rearrange("(p a) -> p a", a=1),
                             gt_f[:, 1, k:k + 1]).then_inc(stored, 16)
            sp.wait_ge(stored, 16 * 10)

        @block.gpsimd
        def _(pool):
            pool.iota(gidx[:, :], pattern=[[1, G - 1]], base=1, channel_multiplier=0).then_inc(iotas, 1)
            pool.iota(vcol[:, :], pattern=[[P, 2]], base=0, channel_multiplier=1).then_inc(iotas, 1)

        @block.vector
        def _(dve):
            dve.wait_ge(loaded, 16 * 5)
            em = d_em[:, :].rearrange("p (a b) -> p a b", b=C)
            dve.tensor_copy(dm[:, :, 0:C], em).then_inc(dm_ok, 1)
            dve.tensor_tensor(dm[:, :, C:2 * C], em, dn_em[:, :].rearrange("p (a b) -> p a b", b=C),
                              ALU.not_equal).then_inc(dm_ok, 1)
            dve.tensor_copy(d16[:, :], d_lin[:, :]).then_inc(d16_ok, 1)
            dve.tensor_tensor(same[:, :], d_lin[:, :], dp_lin[:, :], ALU.not_equal).then_inc(step, 1)
            dve.wait_ge(step, 1)
            dve.tensor_scalar(pen[:, :], same[:, :], NEG, None, ALU.mult).then_inc(pen_ok, 1)
            dve.tensor_single_scalar(gt[:, :], gf[:, :], 7, ALU.arith_shift_right).then_inc(step, 1)
            dve.wait_ge(iotas, 2)
            dve.wait_ge(step, 2)
            dve.tensor_tensor(gb[:, :], gt[:, :], gidx[:, :], ALU.add).then_inc(step, 1)
            dve.tensor_copy(vf[:, :], vcol[:, :]).then_inc(step, 1)
            dve.wait_ge(step, 4)
            for k in range(2):
                dve.tensor_scalar(cmp[:, k, :], gb[:, :], vf[:, k:k + 1], None, ALU.is_le).then_inc(step, 1)
            dve.wait_ge(step, 6)
            dve.tensor_reduce(gt_f[:, 0, :], cmp[:, :, :], AX_X, ALU.add).then_inc(step, 1)
            dve.wait_ge(step, 7)
            dve.tensor_tensor(gt_f[:, 1, :], vf[:, :], gt_f[:, 0, :], ALU.subtract).then_inc(step, 1)
            dve.wait_ge(step, 8)
            dve.tensor_copy(gt_i[:, :, :], gt_f[:, :, :]).then_inc(visits_ok, 1)


def phase_edges(nc, io, scr):
    with ExitStack() as ctx:
        kit = Kit(nc, ctx)
        sb, ps, sem = kit.sb, kit.ps, kit.sem
        vg = sb("vg", [1, VP], I32)
        vt = sb("vt", [1, VP], I32)
        tvb = sb("tvb", [P, VP + 1])
        tbase = sb("tbase", [P, VP])
        nodeid = sb("nodeid", [P, VP])
        fresh = sb("fresh", [P, VP])
        iota_i = sb("iota_i", [P, P], I32)
        iota_f = sb("iota_f", [P, P])
        pcol_i = sb("pcol_i", [P, 1], I32)
        pcol = sb("pcol", [P, 1])
        ident = sb("ident2", [P, P])
        bdm = sb("bdm", [P, C * HT])
        idx = sb("idx", [P, SLOTS, C], I32)
        a4 = sb("a4", [P, SLOTS, C * T])
        a16 = sb("a16", [P, SLOTS, P])
        dme = sb("dme", [P, SLOTS, 2 * C])
        d16r = sb("d16r", [P, SLOTS, GE], U16)
        penr = sb("penr", [H, SLOTS, GE + 1], BF16)
        er3 = sb("er3e", [P, SLOTS, 3 * HT], BF16)
        gat = sb("gat", [P, SLOTS, C, ROW])
        ohT = sb("ohT", [P, 2, GE], BF16)
        iotat = sb("iotat", [P, 2, P])
        oh = sb("oh", [P, 2, C, P])
        z = sb("z", [P, 2, C * HT])
        zm = sb("zm", [P, 2, C * HT])
        lg = sb("lg", [P, 2, C * H])
        lg3 = sb("lg3", [P, 2, C * H])
        e = sb("e", [P, 2, C * H])
        runf = sb("runf", [H, 2, GE])
        runm = sb("runm", [H, 2, GE])
        dlt = sb("dlt", [P, 2, C * H])
        msg = sb("msg", [P, 2, C, SUMS])
        acc = sb("acc", [P, 2, SUMS])
        absn = sb("absn", [P, 2, H])
        mg = sb("mg", [P, 2, H])
        ma = sb("ma", [P, 2, H])
        dd = sb("dd", [P, 2, 2, H])
        sc = sb("sc", [P, 2, 2, H])
        tmp = sb("tmp", [P, 2, H * HW])

        ps_z = [ps(f"ps_z{i}", [P, 512]) for i in range(2)]
        ps_e = ps("ps_e", [P, 1024])
        ps_m = ps("ps_m", [P, 512])
        ps_s = [ps(f"ps_s{i}", [P, 512]) for i in range(2)]

        tables_in = sem("g_tables_in")
        blocks_in = sem("g_blocks_in")
        pool_step = sem("g_pool_step")
        zeroed = sem("g_zeroed")
        pool_ok = sem("g_pool_ok")
        setup = sem("g_setup")
        setup_ok = sem("g_setup_ok")
        in_ = [sem(f"g_in{i}") for i in range(SLOTS)]
        gathered = [sem(f"g_gathered{i}") for i in range(SLOTS)]
        ohT_ok = sem("g_ohT_ok")
        iotat_ok = sem("g_iotat_ok")
        oh_ok = sem("g_oh_ok")
        z_mm = sem("g_z_mm")
        z_ok = sem("g_z_ok")
        zm_ok = sem("g_zm_ok")
        lg_ok = sem("g_lg_ok")
        lg3_ok = sem("g_lg3_ok")
        e_ok = sem("g_e_ok")
        eT_ps = sem("g_eT_ps")
        runf_ok = sem("g_runf_ok")
        runm_ok = sem("g_runm_ok")
        m_ps = sem("g_m_ps")
        dlt_ok = sem("g_dlt_ok")
        mend_ok = sem("g_mend_ok")
        p_ok = sem("g_p_ok")
        msg_ok = sem("g_msg_ok")
        sums = sem("g_sums")
        small = sem("g_small")
        dd_ok = sem("g_dd_ok")
        sc_ok = sem("g_sc_ok")
        merge = sem("g_merge")
        acc_ok = sem("g_acc_ok")
        acc_out = [sem(f"g_acc_out{i}") for i in range(2)]
        LOADS = 7

        block = ctx.enter_context(nc.Block())

        def tail(eng, body, last):
            body(0, 0)
            body(1, 1)
            with eng.Fori(0, (V - 2) // SLOTS) as k:
                for u in range(SLOTS):
                    body(k * SLOTS + (2 + u), (2 + u) % SLOTS)
            if last is not None:
                last()

        @block.sync
        def _(sp):
            sp.dma_start(vg[:, :], scr["visit_group"].rearrange("(a n) -> a n", a=1)).then_inc(tables_in, 16)
            sp.dma_start(vt[:, :], scr["visit_tile"].rearrange("(a n) -> a n", a=1)).then_inc(tables_in, 16)
            sp.dma_start(tvb[:, 1:VP + 1], scr["visit_tile_f"].rearrange("(a n) -> a n", a=1)
                         .broadcast_to([P, VP])).then_inc(tables_in, 16)
            sp.wait_ge(zeroed, 1)
            for c in range(C):
                sp.dma_start(bdm[F * c:F * c + F, HT * c:HT * c + HT].rearrange("f (h t) -> f h t", h=H),
                             io["attn_m"].rearrange("h f t -> f h t")).then_inc(blocks_in, 16)
            sp.wait_ge(tables_in, 48)

            def loads(g, t, s, before):
                before()
                sp.dma_start(idx[:, s, :], io["src"][row_of(g), :, :].rearrange("a p c -> (a p) c")).then_inc(in_[s], 16)
                sp.dma_start(a4[:, s, :], io["a4"][row_of(g), :, :].rearrange("a p c -> (a p) c")).then_inc(in_[s], 16)
                sp.dma_start(a16[:, s, :], io["a16"][row_of(g), :, :].rearrange("a p c -> (a p) c")).then_inc(in_[s], 16)
                sp.dma_start(dme[:, s, :], scr["dm"][row_of(g), :, :].rearrange("a p c -> (a p) c")).then_inc(in_[s], 16)
                sp.dma_start(d16r[:, s, :], scr["dst16"].rearrange("(g n) -> g n", n=GE)[row_of(g), :]
                             .broadcast_to([P, GE])).then_inc(in_[s], 16)
                sp.dma_start(penr[:, s, :], scr["pen"][row_of(g * GE, GE + 1)].rearrange("(a n) -> a n", a=1)
                             .broadcast_to([H, GE + 1])).then_inc(in_[s], 16)
                sp.dma_start(er3[:, s, :], scr["er"][row_of(t), :, :].rearrange("a p c -> (a p) c")).then_inc(in_[s], 16)

            def store(t, v, before):
                before()
                sp.dma_start(scr["acc"][row_of(t), :, :].rearrange("a p c -> (a p) c"),
                             acc[:, v, :]).then_inc(acc_out[v], 16)

            def of_visit(table, v, most):
                return sp.value_load(table[0:1, row_of(v)], min_val=0, max_val=most)

            for v in range(SLOTS):
                loads(of_visit(vg, v, G - 1), of_visit(vt, v, NT - 1), v, lambda: None)

            def step(v, s):
                g = of_visit(vg, v + SLOTS, G - 1)
                t = of_visit(vt, v + SLOTS, NT - 1)
                t_now = of_visit(vt, v, NT - 1)

                def slot_free():
                    sp.wait_ge(msg_ok, v + 1)
                    sp.wait_ge(z_mm, v + 1)

                def summed():
                    sp.wait_ge(acc_ok, v + 1)
                    settle(sp)
                    if not (isinstance(v, int) and v == 0):
                        sp.wait_ge(acc_out[(s + 1) % 2], (v + (0 if s % 2 == 0 else 1)) * 8)

                loads(g, t, s, slot_free)
                store(t_now, s % 2, summed)

            step(0, 0)
            step(1, 1)
            with sp.Fori(0, (V - 2) // SLOTS - 1) as k:
                for u in range(SLOTS):
                    step(k * SLOTS + (2 + u), (2 + u) % SLOTS)
            for v in range(V - SLOTS, V):
                t_now = of_visit(vt, v, NT - 1)
                sp.wait_ge(acc_ok, v + 1)
                sp.wait_ge(acc_out[(v + 1) % 2], 16 * ((v + 1) // 2))
                sp.dma_start(scr["acc"][row_of(t_now), :, :].rearrange("a p c -> (a p) c"),
                             acc[:, v % 2, :]).then_inc(acc_out[v % 2], 16)
            sp.wait_ge(acc_out[0], 16 * (V // 2))
            sp.wait_ge(acc_out[1], 16 * (V // 2))

        @block.gpsimd
        def _(pool):
            pool.memset(bdm[:, :], 0.0).then_inc(zeroed, 1)
            pool.memset(ident[:, :], 0.0).then_inc(pool_step, 1)
            pool.iota(iota_i[:, :], pattern=[[1, P]], base=0, channel_multiplier=0).then_inc(pool_ok, 1)
            pool.iota(pcol_i[:, :], pattern=[[0, 1]], base=0, channel_multiplier=1).then_inc(pool_ok, 1)
            pool.wait_ge(pool_step, 1)
            pool.affine_select(out=ident[:, :], in_=ident[:, :], compare_op=ALU.not_equal, fill=1.0,
                               base=0, pattern=[[-1, P]], channel_multiplier=1).then_inc(pool_ok, 1)

            def gather(v, s):
                pool.wait_ge(in_[s], (v - s) * (4 * LOADS) + 16 * LOADS)
                pool.wait_ge(pool_ok, 3)
                settle(pool)
                for c in range(C):
                    pool.indirect_dma_start(
                        out=gat[:, s, c, :], out_offset=None, in_=scr["table_rows"],
                        in_offset=bass.IndirectOffsetOnAxis(ap=idx[:, s, c:c + 1], axis=0),
                    ).then_inc(gathered[s], 16)

            tail(pool, gather, None)

        @block.scalar
        def _(act):
            def step(v, s):
                b = s % 2
                act.wait_ge(dlt_ok, v + 1)
                act.activation(msg[:, b, :, 0:H * HW].rearrange("p c (h w) -> p c h w", w=HW)[:, :, :, DH],
                               dlt[:, b, :].rearrange("p (c h) -> p c h", h=H), ACT.Exp).then_inc(p_ok, 1)

            def merge_scale(v, b):
                act.wait_ge(dd_ok, v * 2 + 2)
                act.activation(sc[:, b, :, :], dd[:, b, :, :], ACT.Exp).then_inc(sc_ok, 1)

            def both(v, s):
                step(v, s)
                if not (isinstance(v, int) and v == 0):
                    merge_scale(v - 1, (s + 1) % 2)

            tail(act, both, lambda: merge_scale(V - 1, (V - 1) % 2))

        @block.vector
        def _(dve):
            dve.memset(acc[:, :, :], 0.0).then_inc(setup, 1)
            dve.memset(tvb[:, 0:1], -1.0).then_inc(setup, 1)
            dve.wait_ge(pool_ok, 3)
            dve.wait_ge(tables_in, 48)
            dve.tensor_copy(iota_f[:, :], iota_i[:, :]).then_inc(setup, 1)
            dve.tensor_copy(pcol[:, :], pcol_i[:, :]).then_inc(setup, 1)
            dve.tensor_scalar(tbase[:, :], tvb[:, 1:VP + 1], float(P), None, ALU.mult).then_inc(setup, 1)
            dve.wait_ge(setup, 5)
            dve.tensor_scalar(nodeid[:, :], tbase[:, :], pcol[:, 0:1], None, ALU.add).then_inc(setup, 1)
            dve.tensor_tensor(fresh[:, :], tvb[:, 1:VP + 1], tvb[:, 0:VP], ALU.not_equal).then_inc(setup, 1)
            dve.wait_ge(setup, 7)
            dve.tensor_scalar(fresh[:, :], fresh[:, :], 2.0 * NEG, None, ALU.mult).then_inc(setup_ok, 1)
            dve.wait_ge(setup_ok, 1)

            def select(v, s):
                b = s % 2
                dve.wait_ge(in_[s], (v - s) * (4 * LOADS) + 16 * LOADS)
                dve.tensor_scalar(iotat[:, b, :], iota_f[:, :], tbase[:, row_of(v)], None,
                                  ALU.add).then_inc(iotat_ok, 1)
                if not (isinstance(v, int) and v < 2):
                    dve.wait_ge(z_mm, v - 1)
                dve.tensor_scalar(ohT[:, b, :], d16r[:, s, :], nodeid[:, row_of(v)], None,
                                  ALU.is_equal).then_inc(ohT_ok, 1)
                dve.wait_ge(iotat_ok, v + 1)
                if not (isinstance(v, int) and v < 2):
                    dve.wait_ge(sums, v - 1)
                dve.tensor_tensor(oh[:, b, :, :], iotat[:, b, :].unsqueeze(1).broadcast_to([P, C, P]),
                                  dme[:, s, 0:C].unsqueeze(2).broadcast_to([P, C, P]),
                                  ALU.is_equal).then_inc(oh_ok, 1)

            def logits(v, s):
                b = s % 2
                dve.wait_ge(z_mm, v + 1)
                dve.wait_ge(gathered[s], (v - s) * (4 * C) + 16 * C)
                dve.tensor_tensor(z[:, b, :].rearrange("p (c n) -> p c n", c=C),
                                  ps_z[b][:, 0:C * HT].rearrange("p (c n) -> p c n", c=C),
                                  gat[:, s, :, D:ROW], ALU.add).then_inc(z_ok, 1)
                dve.wait_ge(z_ok, v + 1)
                dve.tensor_tensor(
                    zm[:, b, :].rearrange("p (c h t) -> p c h t", c=C, h=H),
                    z[:, b, :].rearrange("p (c h t) -> p c h t", c=C, h=H),
                    a4[:, s, :].rearrange("p (c t) -> p c t", c=C).unsqueeze(2).broadcast_to([P, C, H, T]),
                    ALU.mult).then_inc(zm_ok, 1)
                dve.wait_ge(zm_ok, v + 1)
                dve.tensor_reduce(lg[:, b, :], zm[:, b, :].rearrange("p (q t) -> p q t", t=T),
                                  AX_X, ALU.add).then_inc(lg_ok, 1)
                dve.wait_ge(lg_ok, v + 1)
                dve.tensor_scalar(lg3[:, b, :], lg[:, b, :], 1.0 / 3.0, None, ALU.mult).then_inc(lg3_ok, 1)
                dve.wait_ge(lg3_ok, v + 1)
                dve.scalar_tensor_tensor(e[:, b, :], lg3[:, b, :], SLOPE, lg3[:, b, :], ALU.mult,
                                         ALU.max).then_inc(e_ok, 1)

            def maxima(v, s):
                b = s % 2
                dve.wait_ge(eT_ps, v + 1)
                if not (isinstance(v, int) and v < 2):
                    dve.wait_ge(m_ps, v - 1)
                dve.tensor_tensor_scan(runf[:, b, :], penr[:, s, 0:GE], ps_e[0:H, :], NEG,
                                       ALU.add, ALU.max).then_inc(runf_ok, 1)
                dve.wait_ge(runf_ok, v + 1)
                dve.tensor_tensor_scan(runm[:, b, ::-1], penr[:, s, GE:0:-1], runf[:, b, ::-1], NEG,
                                       ALU.add, ALU.max).then_inc(runm_ok, 1)

            def shift(v, s):
                b = s % 2
                dve.wait_ge(m_ps, v + 1)
                if not (isinstance(v, int) and v < 2):
                    dve.wait_ge(sums, v - 1)
                dve.tensor_tensor(dlt[:, b, :], e[:, b, :], ps_m[:, 0:C * H], ALU.subtract).then_inc(dlt_ok, 1)
                dve.tensor_tensor(msg[:, b, :, H * HW:SUMS],
                                  ps_m[:, 0:C * H].rearrange("p (c h) -> p c h", c=C),
                                  dme[:, s, C:2 * C].unsqueeze(2).broadcast_to([P, C, H]),
                                  ALU.mult).then_inc(mend_ok, 1)

            def messages(v, s):
                b = s % 2
                dve.wait_ge(p_ok, v + 1)
                m4 = msg[:, b, :, 0:H * HW].rearrange("p c (h w) -> p c h w", w=HW)
                dve.tensor_tensor(m4[:, :, :, 0:DH],
                                  gat[:, s, :, 0:D].rearrange("p c (h d) -> p c h d", h=H),
                                  m4[:, :, :, DH:HW].broadcast_to([P, C, H, DH]),
                                  ALU.mult).then_inc(msg_ok, 1)

            def merge_maxima(v, s):
                b, o = s % 2, (s + 1) % 2
                dve.wait_ge(sums, v + 1)
                heads = ps_s[b][:, 0:H * HW].rearrange("p (h w) -> p h w", w=HW)
                dve.tensor_scalar(absn[:, b, :], heads[:, :, DH], 0.5, NEG, ALU.is_lt,
                                  ALU.mult).then_inc(small, 1)
                dve.tensor_scalar(ma[:, b, :], acc[:, o, H * HW:SUMS], fresh[:, row_of(v)], None,
                                  ALU.add).then_inc(small, 1)
                dve.wait_ge(small, v * 3 + 2)
                dve.tensor_tensor(mg[:, b, :], ps_s[b][:, H * HW:SUMS], absn[:, b, :],
                                  ALU.add).then_inc(small, 1)
                dve.wait_ge(small, v * 3 + 3)
                if not (isinstance(v, int) and v < 2):
                    dve.wait_ge(acc_out[b], (v - b) * 8)
                dve.tensor_tensor(acc[:, b, H * HW:SUMS], ma[:, b, :], mg[:, b, :], ALU.max).then_inc(merge, 1)
                dve.wait_ge(merge, v * 3 + 1)
                dve.tensor_tensor(dd[:, b, 0, :], ma[:, b, :], acc[:, b, H * HW:SUMS],
                                  ALU.subtract).then_inc(dd_ok, 1)
                dve.tensor_tensor(dd[:, b, 1, :], mg[:, b, :], acc[:, b, H * HW:SUMS],
                                  ALU.subtract).then_inc(dd_ok, 1)

            def merge_sums(v, s):
                b, o = s % 2, (s + 1) % 2
                dve.wait_ge(sc_ok, v + 1)

                def heads(ap):
                    return ap.rearrange("p (h w) -> p h w", w=HW)

                dve.tensor_tensor(heads(tmp[:, b, :]), heads(ps_s[b][:, 0:H * HW]),
                                  sc[:, b, 1, :].unsqueeze(2).broadcast_to([P, H, HW]),
                                  ALU.mult).then_inc(merge, 1)
                dve.tensor_tensor(heads(acc[:, b, 0:H * HW]), heads(acc[:, o, 0:H * HW]),
                                  sc[:, b, 0, :].unsqueeze(2).broadcast_to([P, H, HW]),
                                  ALU.mult).then_inc(merge, 1)
                dve.wait_ge(merge, v * 3 + 3)
                dve.tensor_tensor(acc[:, b, 0:H * HW], acc[:, b, 0:H * HW], tmp[:, b, :],
                                  ALU.add).then_inc(acc_ok, 1)

            select(0, 0)

            def step(v, s):
                first = isinstance(v, int) and v == 0
                o = (s - 1) % SLOTS
                logits(v, s)
                if not first:
                    messages(v - 1, o)
                maxima(v, s)
                select(v + 1, (s + 1) % SLOTS)
                if not first:
                    if not (isinstance(v, int) and v < 2):
                        dve.wait_ge(acc_ok, v - 1)
                    merge_maxima(v - 1, o)
                shift(v, s)
                if not first:
                    merge_sums(v - 1, o)

            step(0, 0)
            step(1, 1)
            with dve.Fori(0, (V - 2) // SLOTS - 1) as k:
                for u in range(SLOTS):
                    step(k * SLOTS + (2 + u), (2 + u) % SLOTS)
            for v in range(V - SLOTS, V):
                logits(v, v % SLOTS)
                messages(v - 1, (v - 1) % SLOTS)
                maxima(v, v % SLOTS)
                if v + 1 < V:
                    select(v + 1, (v + 1) % SLOTS)
                dve.wait_ge(acc_ok, v - 1)
                merge_maxima(v - 1, (v - 1) % SLOTS)
                shift(v, v % SLOTS)
                merge_sums(v - 1, (v - 1) % SLOTS)
            messages(V - 1, (V - 1) % SLOTS)
            dve.wait_ge(acc_ok, V - 1)
            merge_maxima(V - 1, (V - 1) % SLOTS)
            merge_sums(V - 1, (V - 1) % SLOTS)

        @block.tensor
        def _(pe):
            pe.wait_ge(blocks_in, 16 * C)
            pe.wait_ge(pool_ok, 3)

            def edge_terms(v, s):
                b = s % 2
                pe.wait_ge(in_[s], (v - s) * (4 * LOADS) + 16 * LOADS)
                if not (isinstance(v, int) and v < 2):
                    pe.wait_ge(z_ok, v - 1)
                pe.wait_ge(ohT_ok, v + 1)
                pe.matmul(ps_z[b][:, 0:C * HT], a16[:, s, :], bdm[:, :], start=True, stop=False,
                          skip_group_check=True)
                for c in range(C):
                    for part in range(3):
                        last = pe.matmul(ps_z[b][:, c * HT:(c + 1) * HT], ohT[:, b, c * P:(c + 1) * P],
                                         er3[:, s, part * HT:(part + 1) * HT], start=False,
                                         stop=(c == C - 1 and part == 2), skip_group_check=True)
                last.then_inc(z_mm, 1)

            def turn_logits(v, s):
                b = s % 2
                pe.wait_ge(e_ok, v + 1)
                if not (isinstance(v, int) and v < 1):
                    pe.wait_ge(runf_ok, v)
                for c in range(C):
                    last = pe.transpose(ps_e[0:H, c * P:(c + 1) * P], e[:, b, c * H:(c + 1) * H], ident[:, :])
                last.then_inc(eT_ps, 1)

            def turn_maxima(v, s):
                b = s % 2
                pe.wait_ge(runm_ok, v + 1)
                if not (isinstance(v, int) and v < 1):
                    pe.wait_ge(mend_ok, v)
                settle(pe)
                for c in range(C):
                    last = pe.transpose(ps_m[:, c * H:(c + 1) * H], runm[0:H, b, c * P:(c + 1) * P],
                                        ident[0:H, 0:H])
                last.then_inc(m_ps, 1)

            def segment_sums(v, s):
                b = s % 2
                pe.wait_ge(msg_ok, v + 1)
                pe.wait_ge(mend_ok, v + 1)
                pe.wait_ge(oh_ok, v + 1)
                if not (isinstance(v, int) and v < 2):
                    pe.wait_ge(acc_ok, v - 1)
                for c in range(C):
                    last = pe.matmul(ps_s[b][:, 0:SUMS], oh[:, b, c, :], msg[:, b, c, :],
                                     start=(c == 0), stop=(c == C - 1))
                last.then_inc(sums, 1)

            edge_terms(0, 0)

            def step(v, s):
                turn_logits(v, s)
                if not (isinstance(v, int) and v == 0):
                    segment_sums(v - 1, (s - 1) % SLOTS)
                turn_maxima(v, s)
                edge_terms(v + 1, (s + 1) % SLOTS)

            step(0, 0)
            step(1, 1)
            with pe.Fori(0, (V - 2) // SLOTS - 1) as k:
                for u in range(SLOTS):
                    step(k * SLOTS + (2 + u), (2 + u) % SLOTS)
            for v in range(V - SLOTS, V):
                turn_logits(v, v % SLOTS)
                segment_sums(v - 1, (v - 1) % SLOTS)
                turn_maxima(v, v % SLOTS)
                if v + 1 < V:
                    edge_terms(v + 1, (v + 1) % SLOTS)
            segment_sums(V - 1, (V - 1) % SLOTS)


def phase_ffn(nc, io, scr):
    B = 4
    NB = -(-NT // B)
    with ExitStack() as ctx:
        kit = Kit(nc, ctx)
        sb, ps, sem = kit.sb, kit.ps, kit.sem
        w1 = sb("w1", [P, X, KD, D])
        w2 = sb("w2", [P, X, KD, D])
        wo = sb("wo", [P, X, KD, D])
        wr = sb("wr", [P, KD, X])
        brb = sb("brb", [P, X])
        bo = sb("bo", [X, D])
        bn = sb("bn", [P, 10, X * KD])
        sc = sb("fsc", [P, 2, X * KD])
        sh = sb("fsh", [P, 2, X * KD])
        ident = sb("ident3", [P, P])
        eps = sb("feps", [P, 2])
        am = sb("am", [P, 2, B, SUMS])
        xm = sb("xm", [P, 2, B, D])
        rs = sb("rs", [P, B, H])
        x2 = sb("x2", [P, 2, B, D])
        st = sb("fst", [P, B, 6])
        mv = sb("fmv", [P, B, 2])
        sd = sb("fsd", [P, B])
        xn = sb("fxn", [P, B, D])
        xnT = sb("fxnT", [P, 2, KD, B * P])
        lo = sb("lo", [P, B, X])
        lm = sb("lm", [P, B])
        w = sb("w", [P, 2, B, X])
        wT = sb("wT", [X, B * P])
        h1 = sb("h1", [P, 2, KD, B * P])
        h2 = sb("h2", [P, 2, KD, B * P])
        y = sb("y", [P, 2, B, D])

        ps_t = ps("ps_t", [P, KD, B * P])
        ps_h = [ps(f"ps_h{i}", [P, B * P]) for i in range(4)]
        ps_y = ps("ps_y", [P, B, D])

        weights_in = sem("f_weights_in")
        bn_in = sem("f_bn_in")
        pool_step = sem("f_pool_step")
        pool_ok = sem("f_pool_ok")
        bn_sd = sem("f_bn_sd")
        bn_step = sem("f_bn_step")
        bn_ok = sem("f_bn_ok")
        in_ = [sem(f"f_in{i}") for i in range(2)]
        r0 = sem("f_r0")
        r1 = sem("f_r1")
        v_ok = sem("f_v_ok")
        x2_ok = sem("f_x2_ok")
        st_ok = sem("f_st_ok")
        mv_ok = sem("f_mv_ok")
        sd_ok = sem("f_sd_ok")
        rsd_ok = sem("f_rsd_ok")
        xn_ok = sem("f_xn_ok")
        xnT_ps = sem("f_xnT_ps")
        xnT_ok = sem("f_xnT_ok")
        rt_ps = sem("f_rt_ps")
        lo_ok = sem("f_lo_ok")
        lm_ok = sem("f_lm_ok")
        ls_ok = sem("f_ls_ok")
        le_ok = sem("f_le_ok")
        lsum_ok = sem("f_lsum_ok")
        lrec_ok = sem("f_lrec_ok")
        w_ok = sem("f_w_ok")
        wT_ps = sem("f_wT_ps")
        wT_ok = sem("f_wT_ok")
        bo_ps = sem("f_bo_ps")
        y0_ok = sem("f_y0_ok")
        h1_ps = sem("f_h1_ps")
        h1_ok = sem("f_h1_ok")
        h2_ps = sem("f_h2_ps")
        h2_ok = sem("f_h2_ok")
        y_ps = sem("f_y_ps")
        y_ok = sem("f_y_ok")
        y_out = [sem(f"f_y_out{i}") for i in range(2)]
        block = ctx.enter_context(nc.Block())

        def halves(n):
            return -(-n // 2)

        def blocks(eng, body):
            full = NT // B
            for b in range(2):
                body(b, b % 2, B)
            with eng.Fori(0, (full - 2) // 2) as k:
                for u in (0, 1):
                    body(k * 2 + (2 + u), u, B)
            body(full, full % 2, NT - full * B)

        assert (NT // B) % 2 == 0 and NB == NT // B + 1

        @block.sync
        def _(sp):
            sp.dma_start(bn[:, :, :], io["bn"].rearrange("p (k n) -> p k n", k=10)).then_inc(bn_in, 16)
            sp.dma_start(wr[:, :, :], io["Wr"].rearrange("(c p) n -> p c n", p=P)).then_inc(weights_in, 16)
            sp.dma_start(brb[:, :], io["br"].rearrange("(a n) -> a n", a=1).broadcast_to([P, X])).then_inc(weights_in, 16)
            sp.dma_start(bo[:, :], io["bo"]).then_inc(weights_in, 16)

            def load(b, s, n):
                if later(b):
                    sp.wait_ge(x2_ok, b - 1)
                sp.dma_start(am[:, s, 0:n, :], scr["acc"][row_of(b * B, n), :, :].rearrange("a p c -> p a c")).then_inc(in_[s], 16)
                sp.dma_start(xm[:, s, 0:n, :], scr["xmix"][row_of(b * B, n), :, :].rearrange("a p c -> p a c")).then_inc(in_[s], 16)

            load(0, 0, B)
            load(1, 1, B)
            for dst, name in ((w1, "W1"), (w2, "W2"), (wo, "Wo")):
                sp.dma_start(dst[:, :, :, :], io[name].rearrange("e (c p) n -> p e c n", p=P)).then_inc(weights_in, 16)
            with sp.Fori(0, (NT // B - 2) // 2) as k:
                for u in (0, 1):
                    load(k * 2 + (2 + u), u, B)
            load(NT // B, 0, NT - NT // B * B)

        @block.gpsimd
        def _(pool):
            pool.memset(ident[:, :], 0.0).then_inc(pool_step, 1)
            pool.memset(eps[:, 0:1], LN_EPS).then_inc(pool_ok, 1)
            pool.memset(eps[:, 1:2], BN_EPS).then_inc(pool_ok, 1)
            pool.wait_ge(pool_step, 1)
            pool.affine_select(out=ident[:, :], in_=ident[:, :], compare_op=ALU.not_equal, fill=1.0,
                               base=0, pattern=[[-1, P]], channel_multiplier=1).then_inc(pool_ok, 1)

            def store(b, s, n):
                pool.wait_ge(y_ok, b * (2 * X) + X * halves(n))
                pool.wait_ge(pool_ok, 3)
                if n == B:
                    pool.dma_start(io["out"][row_of(b * (B * P), B * P), :].rearrange("(a p) c -> p a c", p=P),
                                   y[:, s, :, :]).then_inc(y_out[s], 16)
                else:
                    pool.dma_start(io["out"][N - LAST:N, :], y[0:LAST, s, 0, :]).then_inc(y_out[s], 16)

            blocks(pool, store)
            pool.wait_ge(y_out[0], 16 * ((NB + 1) // 2))
            pool.wait_ge(y_out[1], 16 * (NB // 2))

        @block.scalar
        def _(act):
            act.wait_ge(bn_in, 16)
            act.wait_ge(pool_ok, 3)
            for layer in range(2):
                act.activation(sc[:, layer, :], bn[:, 5 * layer + 4, :], ACT.Sqrt, bias=eps[:, 1:2]).then_inc(bn_sd, 1)
            act.wait_ge(bn_ok, 2)

            def body(b, s, n):
                act.wait_ge(mv_ok, b + 1)
                act.activation(sd[:, 0:n], mv[:, 0:n, 1], ACT.Sqrt, bias=eps[:, 0:1]).then_inc(sd_ok, 1)
                act.wait_ge(xnT_ps, b + 1)
                act.copy(xnT[:, s, :, 0:n * P], ps_t[:, :, 0:n * P]).then_inc(xnT_ok, 1)
                act.wait_ge(ls_ok, b + 1)
                act.activation(lo[:, 0:n, :], lo[:, 0:n, :], ACT.Exp).then_inc(le_ok, 1)
                for x in range(X):
                    for layer, (hid, done, ok) in enumerate(((h1, h1_ps, h1_ok), (h2, h2_ps, h2_ok))):
                        act.wait_ge(done, b * X + (x + 1))
                        if not (isinstance(b, int) and b == 0 and x < 2) and layer == 1:
                            if x == 0:
                                act.wait_ge(y_ps, b * (2 * X) - 2)
                            else:
                                act.wait_ge(y_ps, b * (2 * X) + (x - 1) * halves(n))
                        for m in range(KD):
                            act.activation(hid[:, x % 2, m, 0:n * P], ps_h[2 * layer + m][:, 0:n * P], ACT.Relu,
                                           bias=sh[:, layer, x * KD + m:x * KD + m + 1],
                                           scale=sc[:, layer, x * KD + m:x * KD + m + 1]).then_inc(ok, 1)

            blocks(act, body)

        @block.vector
        def _(dve):
            dve.wait_ge(bn_sd, 2)
            dve.reciprocal(sc[:, :, :], sc[:, :, :]).then_inc(bn_step, 1)
            for layer in range(2):
                dve.tensor_tensor(sh[:, layer, :], bn[:, 5 * layer, :], bn[:, 5 * layer + 3, :],
                                  ALU.subtract).then_inc(bn_step, 1)
            dve.wait_ge(bn_step, 3)
            for layer in range(2):
                dve.tensor_tensor(sc[:, layer, :], sc[:, layer, :], bn[:, 5 * layer + 1, :], ALU.mult).then_inc(bn_step, 1)
            dve.wait_ge(bn_step, 5)
            dve.tensor_tensor(sh[:, :, :], sh[:, :, :], sc[:, :, :], ALU.mult).then_inc(bn_step, 1)
            dve.wait_ge(bn_step, 6)
            for layer in range(2):
                dve.tensor_tensor(sh[:, layer, :], sh[:, layer, :], bn[:, 5 * layer + 2, :], ALU.add).then_inc(bn_ok, 1)
            dve.wait_ge(weights_in, 16 * 6)

            def body(b, s, n):
                dve.wait_ge(in_[s], (b - s) * 16 + 32)
                heads = am[:, s, 0:n, 0:H * HW].rearrange("p a (h w) -> p a h w", w=HW)
                dve.tensor_scalar(rs[:, 0:n, :], heads[:, :, :, DH], 1e-30, None, ALU.max).then_inc(r0, 1)
                dve.wait_ge(r0, b + 1)
                dve.reciprocal(rs[:, 0:n, :], rs[:, 0:n, :]).then_inc(r1, 1)
                dve.wait_ge(r1, b + 1)
                for a in range(n):
                    dve.tensor_tensor(x2[:, s, a, :].rearrange("p (h d) -> p h d", h=H), heads[:, a, :, 0:DH],
                                      rs[:, a, :].unsqueeze(2).broadcast_to([P, H, DH]), ALU.mult).then_inc(v_ok, 1)
                dve.wait_ge(v_ok, b * B + n)
                dve.tensor_tensor(x2[:, s, 0:n, :], x2[:, s, 0:n, :], xm[:, s, 0:n, :], ALU.add).then_inc(x2_ok, 1)
                dve.wait_ge(x2_ok, b + 1)
                for a in range(n):
                    dve.bn_stats(st[:, a, :], x2[:, s, a, :]).then_inc(st_ok, 1)
                dve.wait_ge(st_ok, b * B + n)
                settle(dve)
                for a in range(n):
                    last = dve.bn_aggr(mv[:, a, :], st[:, a, :])
                last.then_inc(mv_ok, 1)
                dve.wait_ge(sd_ok, b + 1)
                dve.reciprocal(sd[:, 0:n], sd[:, 0:n]).then_inc(rsd_ok, 1)
                dve.wait_ge(rsd_ok, b + 1)
                for a in range(n):
                    dve.tensor_scalar(xn[:, a, :], x2[:, s, a, :], mv[:, a, 0:1], sd[:, a:a + 1],
                                      ALU.subtract, ALU.mult).then_inc(xn_ok, 1)
                dve.wait_ge(rt_ps, b + 1)
                dve.tensor_tensor(lo[:, 0:n, :], ps_y[:, 0:n, 0:X],
                                  brb[:, :].unsqueeze(1).broadcast_to([P, n, X]), ALU.add).then_inc(lo_ok, 1)
                dve.wait_ge(lo_ok, b + 1)
                dve.tensor_reduce(lm[:, 0:n], lo[:, 0:n, :], AX_X, ALU.max).then_inc(lm_ok, 1)
                dve.wait_ge(lm_ok, b + 1)
                dve.tensor_tensor(lo[:, 0:n, :], lo[:, 0:n, :], lm[:, 0:n].unsqueeze(2).broadcast_to([P, n, X]),
                                  ALU.subtract).then_inc(ls_ok, 1)
                dve.wait_ge(le_ok, b + 1)
                dve.tensor_reduce(lm[:, 0:n], lo[:, 0:n, :], AX_X, ALU.add).then_inc(lsum_ok, 1)
                dve.wait_ge(lsum_ok, b + 1)
                dve.reciprocal(lm[:, 0:n], lm[:, 0:n]).then_inc(lrec_ok, 1)
                dve.wait_ge(lrec_ok, b + 1)
                dve.tensor_tensor(w[:, s, 0:n, :], lo[:, 0:n, :], lm[:, 0:n].unsqueeze(2).broadcast_to([P, n, X]),
                                  ALU.mult).then_inc(w_ok, 1)
                dve.wait_ge(wT_ps, b + 1)
                dve.tensor_copy(wT[:, 0:n * P], ps_t[0:X, 0, 0:n * P]).then_inc(wT_ok, 1)
                dve.wait_ge(bo_ps, b + 1)
                if later(b):
                    dve.wait_ge(y_out[s], (b - s) * 8)
                dve.tensor_tensor(y[:, s, 0:n, :], ps_y[:, 0:n, :], x2[:, s, 0:n, :], ALU.add).then_inc(y0_ok, 1)
                dve.wait_ge(y0_ok, b + 1)
                for x in range(X):
                    for half in range(halves(n)):
                        dve.wait_ge(y_ps, b * (2 * X) + (x * halves(n) + half + 1))
                        if x > 0:
                            dve.wait_ge(y_ok, b * (2 * X) + ((x - 1) * halves(n) + half + 1))
                        for a in range(2 * half, min(2 * half + 2, n)):
                            ins = dve.scalar_tensor_tensor(y[:, s, a, :], ps_y[:, a, :], w[:, s, a, x:x + 1],
                                                           y[:, s, a, :], ALU.mult, ALU.add)
                        ins.then_inc(y_ok, 1)

            blocks(dve, body)

        @block.tensor
        def _(pe):
            pe.wait_ge(pool_ok, 3)
            pe.wait_ge(weights_in, 16 * 6)

            def body(b, s, n):
                pe.wait_ge(xn_ok, b * B + n)
                if not (isinstance(b, int) and b == 0):
                    pe.wait_ge(wT_ok, b)
                for k in range(KD):
                    for a in range(n):
                        last = pe.transpose(ps_t[:, k, a * P:(a + 1) * P], xn[:, a, k * P:(k + 1) * P], ident[:, :])
                last.then_inc(xnT_ps, 1)
                pe.wait_ge(xnT_ok, b + 1)
                if not (isinstance(b, int) and b == 0):
                    pe.wait_ge(y_ok, b * (2 * X))
                for a in range(n):
                    for k in range(KD):
                        last = pe.matmul(ps_y[:, a, 0:X], xnT[:, s, k, a * P:(a + 1) * P], wr[:, k, :],
                                         start=(k == 0), stop=(k == KD - 1), skip_group_check=True)
                last.then_inc(rt_ps, 1)

                def layer1(x):
                    if not (isinstance(b, int) and b == 0 and x == 0):
                        pe.wait_ge(h1_ok, (b * X + x) * 2)
                    for m in range(KD):
                        for k in range(KD):
                            last = pe.matmul(ps_h[m][:, 0:n * P], w1[:, x, k, m * P:(m + 1) * P],
                                             xnT[:, s, k, 0:n * P], start=(k == 0), stop=(k == KD - 1))
                    last.then_inc(h1_ps, 1)

                def layer2(x):
                    pe.wait_ge(h1_ok, (b * X + x) * 2 + 2)
                    if not (isinstance(b, int) and b == 0 and x == 0):
                        pe.wait_ge(h2_ok, (b * X + x) * 2)
                    for m in range(KD):
                        for k in range(KD):
                            last = pe.matmul(ps_h[2 + m][:, 0:n * P], w2[:, x, k, m * P:(m + 1) * P],
                                             h1[:, x % 2, k, 0:n * P], start=(k == 0), stop=(k == KD - 1))
                    last.then_inc(h2_ps, 1)

                def layer3(x):
                    pe.wait_ge(h2_ok, (b * X + x) * 2 + 2)
                    for half in range(halves(n)):
                        if x == 0:
                            pe.wait_ge(y0_ok, b + 1)
                        else:
                            pe.wait_ge(y_ok, b * (2 * X) + ((x - 1) * halves(n) + half + 1))
                        for a in range(2 * half, min(2 * half + 2, n)):
                            for k in range(KD):
                                last = pe.matmul(ps_y[:, a, :], h2[:, x % 2, k, a * P:(a + 1) * P],
                                                 wo[:, x, k, :], start=(k == 0), stop=(k == KD - 1))
                        last.then_inc(y_ps, 1)

                layer1(0)
                pe.wait_ge(w_ok, b + 1)
                for a in range(n):
                    last = pe.transpose(ps_t[0:X, 0, a * P:(a + 1) * P], w[:, s, a, :], ident[:, :])
                last.then_inc(wT_ps, 1)
                layer2(0)
                pe.wait_ge(wT_ok, b + 1)
                for a in range(n):
                    last = pe.matmul(ps_y[:, a, :], wT[:, a * P:(a + 1) * P], bo[:, :], start=True, stop=True)
                last.then_inc(bo_ps, 1)
                for x in range(1, X):
                    layer1(x)
                    layer3(x - 1)
                    layer2(x)
                layer3(X - 1)

            blocks(pe, body)


INPUTS = {
    "x": ((NT, P, D), F32), "W_n": ((D, D), F32), "W_nT": ((D, D), F32),
    "attn_l": ((H, DH, T), F32), "attn_r": ((H, DH, T), F32), "attn_m": ((H, F, T), F32),
    "Wqkv": ((D, 3 * D), F32), "Wout": ((D, D), F32), "gamma": ((D,), F32),
    "src": ((G, P, C), I32), "a4": ((G, P, C * T), F32), "a16": ((G, P, P), F32),
    "dst_em": ((EP,), I32), "dst_next_em": ((EP,), I32), "dst_lin": ((EP,), I32),
    "dst_prev_lin": ((EP,), I32), "group_first": ((G - 1,), I32),
    "Wr": ((D, X), F32), "br": ((X,), F32), "W1": ((X, D, D), F32), "W2": ((X, D, D), F32),
    "Wo": ((X, D, D), F32), "bo": ((X, D), F32), "bn": ((P, 10 * X * KD), F32),
}
SCRATCH = {
    "table": ((NT, P, ROW), F32), "er": ((NT, P, 3 * HT), BF16), "xmix": ((NT, P, D), F32),
    "dm": ((G, P, 2 * C), F32), "dst16": ((EP,), U16), "pen": ((EP + 1,), BF16),
    "visit_group": ((VP,), I32), "visit_tile": ((VP,), I32), "visit_tile_f": ((VP,), F32),
    "acc": ((NT, P, SUMS), F32),
}


def build(nc):
    io = {n: nc.dram_tensor(f"in_{n}", s, dt, kind="ExternalInput").ap() for n, (s, dt) in INPUTS.items()}
    io["out"] = nc.dram_tensor("out", (N, D), F32, kind="ExternalOutput").ap()
    scr = {n: nc.dram_tensor(f"scratch_{n}", s, dt).ap() for n, (s, dt) in SCRATCH.items()}
    scr["table_rows"] = scr["table"].rearrange("t p c -> (t p) c")
    phase_nodes(nc, io, scr)
    phase_edge_tables(nc, io, scr)
    phase_edges(nc, io, scr)
    phase_ffn(nc, io, scr)


def lay_out(i):
    import numpy as np

    def edges(a, fill=0):
        a = np.asarray(a)
        out = np.full((EP,) + a.shape[1:], fill, a.dtype)
        out[:E] = a
        return out

    def edge_major(a):
        return a.reshape(G, C, P).transpose(0, 2, 1)

    dst = edges(i["dst"], PAD_DST)
    following = np.full(EP, -1, dst.dtype)
    following[:-1] = dst[1:]
    following[GE - 1::GE] = -1
    before = np.full(EP, -1, dst.dtype)
    before[1:] = dst[:-1]
    x = np.asarray(i["x"])
    xp = np.zeros((NP, D), x.dtype)
    xp[:N] = x
    bn = np.stack([np.asarray(i["L0_ffn_" + n]).reshape(X, KD, P).transpose(2, 0, 1).reshape(P, X * KD)
                   for n in ("b1", "g1", "be1", "m1", "v1", "b2", "g2", "be2", "m2", "v2")], axis=1)
    laid = {
        "x": xp.reshape(NT, P, D), "W_nT": np.asarray(i["L0_gnn_W_n"]).T,
        "src": edge_major(edges(i["src"])),
        "a4": edges(i["edge_attr_4"]).reshape(G, C, P, T).transpose(0, 2, 1, 3).reshape(G, P, C * T),
        "a16": edges(i["edge_attr_16"]).reshape(G, C, P, F).transpose(0, 1, 3, 2).reshape(G, P, P),
        "dst_em": edge_major(dst).reshape(-1), "dst_next_em": edge_major(following).reshape(-1),
        "dst_lin": dst, "dst_prev_lin": before, "group_first": dst[GE::GE], "bn": bn.reshape(P, 10 * X * KD),
    }
    for n in ("W_n", "attn_l", "attn_r", "attn_m"):
        laid[n] = i["L0_gnn_" + n]
    for n in ("Wqkv", "Wout", "gamma"):
        laid[n] = i["L0_mix_" + n]
    for n in ("Wr", "br", "W1", "W2", "Wo", "bo"):
        laid[n] = i["L0_ffn_" + n]
    return {f"in_{n}": np.ascontiguousarray(laid[n]) for n in INPUTS}


def kernel(**inputs):
    import concourse.bacc as bacc
    from concourse.bass_utils import run_bass_kernel_spmd

    nc = bacc.Bacc("TRN2", target_bir_lowering=False, num_devices=1)
    build(nc)
    r = run_bass_kernel_spmd(nc, [lay_out(inputs)], core_ids=[0])
    return r.results[0]["out"]
```

```python
from contextlib import ExitStack

import concourse.bass as bass
from concourse import mybir

F32 = mybir.dt.float32
BF16 = mybir.dt.bfloat16
I32 = mybir.dt.int32
U16 = mybir.dt.uint16
ALU = mybir.AluOpType
ACT = mybir.ActivationFunctionType
AX_X = mybir.AxisListType.X
RMAX = bass.bass_isa.ReduceOp.max

P = 128
N = 6250
NT = -(-N // P)
NP = NT * P
LAST = N - (NT - 1) * P
D = 256
KD = D // P
H = 8
DH = D // H
T = 4
HT = H * T
F = 16
E = 206250
C = 8
GE = C * P
G = -(-E // GE)
EP = G * GE
PAD_DST = 8191
V = G + NT - 1
VP = 2 * P
ROW = D + HT
HW = DH + 1
SUMS = H * HW + H
SLOTS = 4
NEG = -1.0e30
SLOPE = 0.2
THIRD = 1.0 / 3.0
FIRST = 6
LN_EPS = 1e-5
BN_EPS = 1e-3
SCALE = DH ** -0.5
X = 8
EL = EP // P


class Kit:

    def __init__(self, nc, ctx):
        self.nc, self.ctx = nc, ctx

    def sb(self, name, shape, dt=F32):
        return self.ctx.enter_context(self.nc.sbuf_tensor(name, shape, dt))

    def ps(self, name, shape, dt=F32):
        return self.ctx.enter_context(self.nc.psum_tensor(name, shape, dt))

    def sem(self, name):
        return self.ctx.enter_context(self.nc.semaphore(name))


def row_of(t, n=1):
    return bass.ds(t, n)


def settle(eng):
    eng.nop(nofuse=True)


def later(t):
    return not (isinstance(t, int) and t < 2)


def tiles(eng, body, follow=None, lag=1):

    def step(t, s):
        body(t, s)
        if follow is not None and not (isinstance(t, int) and t < lag):
            follow(t - lag, (s + lag) % 2)

    for t in range(5):
        step(t, t % 2)
    with eng.Fori(0, (NT - 5) // 2) as k:
        for u in (0, 1):
            step(k * 2 + (5 + u), (5 + u) % 2)
    if follow is not None:
        for t in range(NT - lag, NT):
            follow(t, t % 2)


def phase_nodes(nc, io, scr):
    with ExitStack() as ctx:
        kit = Kit(nc, ctx)
        sb, ps, sem = kit.sb, kit.ps, kit.sem
        wcat = sb("wcat", [P, KD, D + 2 * HT])
        wqkv = sb("wqkv", [P, KD, 3 * D])
        wnT = sb("wnT", [P, KD, D])
        wout = sb("wout", [P, KD, D])
        bd = sb("bd", [P, KD, 2 * HT])
        gamma = sb("gamma", [P, D])
        ident = sb("ident", [P, P])
        eps = sb("eps", [P, 1])
        xin = sb("xin", [P, 2, D])
        st = sb("st", [P, 2, 6])
        mv = sb("mv", [P, 2, 2])
        rstd = sb("rstd", [P, 2, 1])
        xn = sb("xn", [P, 2, D])
        xnT = sb("xnT", [P, 2, KD, P])
        trow = sb("trow", [P, 2, D + 2 * HT])
        er3 = sb("er3", [P, 2, 3 * HT], BF16)
        er_a = sb("er_a", [P, 2, HT])
        er_b = sb("er_b", [P, 2, HT])
        ktile = sb("ktile", [P, NT, D])
        vtile = sb("vtile", [P, NT, D])
        qtile = sb("qtile", [P, NT, D])
        real = sb("real", [P, NT])
        kmax = sb("kmax", [P, D])
        kmaxb = sb("kmaxb", [P, D])
        kexp = sb("kexp", [P, 2, D])
        ctx_sb = sb("ctx_sb", [P, KD, P])
        ctxT = sb("ctxT", [P, KD, P])
        rsum = sb("rsum", [P, KD])
        mixw = sb("mixw", [P, KD, D])
        qmax = sb("qmax", [P, H])
        qsm = sb("qsm", [P, 2, D])
        qsum = sb("qsum", [P, H])
        qT = sb("qT", [P, 2, KD, P])
        xre = sb("xre", [P, 2, D])
        mixo = sb("mixo", [P, 2, D])
        mixf = sb("mixf", [P, 2, D])

        ps_tr = [ps(f"ps_tr{i}", [P, KD, P]) for i in range(2)]
        ps_ft = [ps(f"ps_ft{i}", [P, 512]) for i in range(2)]
        ps_qk = [ps(f"ps_qk{i}", [P, 512]) for i in range(2)]
        ps_v = [ps(f"ps_v{i}", [P, 512]) for i in range(2)]

        weights_in = sem("n_weights_in")
        blocks_in = sem("n_blocks_in")
        zeroed = sem("n_zeroed")
        ident_ok = sem("n_ident_ok")
        pool_step = sem("n_pool_step")
        eps_ok = sem("n_eps_ok")
        attn_w = sem("n_attn_w")
        attn_wc = sem("n_attn_wc")
        x_in = [sem(f"n_x_in{i}") for i in range(2)]
        stats = sem("n_stats")
        var_ok = sem("n_var_ok")
        std = sem("n_std")
        rstd_ok = sem("n_rstd_ok")
        xn_ok = sem("n_xn_ok")
        xnT_ps = sem("n_xnT_ps")
        xnT_ok = sem("n_xnT_ok")
        proj = sem("n_proj")
        trow_ok = sem("n_trow_ok")
        kept = sem("n_kept")
        ermax = sem("n_ermax")
        er_hi = sem("n_er_hi")
        er_r1 = sem("n_er_r1")
        er_mid = sem("n_er_mid")
        er_r2 = sem("n_er_r2")
        er_ok = sem("n_er_ok")
        table_out = [sem(f"n_table_out{i}") for i in range(2)]
        kmax_ok = sem("n_kmax_ok")
        kmaxb_ok = sem("n_kmaxb_ok")
        ksub = sem("n_ksub")
        kexp_ok = sem("n_kexp_ok")
        ctx_mm = sem("n_ctx_mm")
        ctx_z = sem("n_ctx_z")
        ctx_c = sem("n_ctx_c")
        ctxT_ps = sem("n_ctxT_ps")
        ctxT_ok = sem("n_ctxT_ok")
        mix_mm = sem("n_mix_mm")
        mixw_ok = sem("n_mixw_ok")
        rsum_ok = sem("n_rsum_ok")
        qmax_ok = sem("n_qmax_ok")
        qsub = sem("n_qsub")
        qexp = sem("n_qexp")
        qsum_ok = sem("n_qsum_ok")
        qrec = sem("n_qrec")
        qsm_ok = sem("n_qsm_ok")
        qT_ps = sem("n_qT_ps")
        qT_ok = sem("n_qT_ok")
        out_mm = sem("n_out_mm")
        xre_in = [sem(f"n_xre_in{i}") for i in range(2)]
        ln_st = sem("n_ln_st")
        ln_var = sem("n_ln_var")
        ln_std = sem("n_ln_std")
        ln_rstd = sem("n_ln_rstd")
        ln_n = sem("n_ln_n")
        ln_g = sem("n_ln_g")
        mixf_ok = sem("n_mixf_ok")
        mix_out = [sem(f"n_mix_out{i}") for i in range(2)]

        block = ctx.enter_context(nc.Block())

        @block.sync
        def _(sp):
            loads = [
                (wcat[:, :, 0:D], io["W_n"].rearrange("(c p) n -> p c n", p=P)),
                (wnT[:, :, :], io["W_nT"].rearrange("(c p) n -> p c n", p=P)),
                (wqkv[:, :, :], io["Wqkv"].rearrange("(c p) n -> p c n", p=P)),
                (wout[:, :, :], io["Wout"].rearrange("(c p) n -> p c n", p=P)),
                (gamma[:, :], io["gamma"].rearrange("(a n) -> a n", a=1).broadcast_to([P, D])),
            ]
            for dst, src in loads:
                sp.dma_start(dst, src).then_inc(weights_in, 16)
            sp.wait_ge(zeroed, 1)
            for h in range(H):
                rows = slice(DH * (h % 4), DH * (h % 4) + DH)
                for side, name in enumerate(("attn_l", "attn_r")):
                    sp.dma_start(bd[rows, h // 4, HT * side + T * h:HT * side + T * h + T],
                                 io[name][h]).then_inc(blocks_in, 16)

            def load_x(t, s):
                if later(t):
                    sp.wait_ge(xn_ok, t - 1)
                sp.dma_start(xin[:, s, :], io["x"][row_of(t), :, :].rearrange("a p n -> (a p) n")) \
                    .then_inc(x_in[s], 16)

            tiles(sp, load_x)

            def reload(t, s):
                if later(t):
                    sp.wait_ge(mixf_ok, t - 1)
                sp.dma_start(xre[:, s, :], io["x"][row_of(t), :, :].rearrange("a p n -> (a p) n")) \
                    .then_inc(xre_in[s], 16)

            tiles(sp, reload)

        @block.gpsimd
        def _(pool):
            pool.memset(bd[:, :, :], 0.0).then_inc(zeroed, 1)
            pool.memset(ident[:, :], 0.0).then_inc(pool_step, 1)
            pool.memset(real[:, :], 1.0).then_inc(pool_step, 1)
            pool.memset(eps[:, :], LN_EPS).then_inc(eps_ok, 1)
            pool.wait_ge(pool_step, 2)
            pool.affine_select(out=ident[:, :], in_=ident[:, :], compare_op=ALU.not_equal, fill=1.0,
                               base=0, pattern=[[-1, P]], channel_multiplier=1).then_inc(ident_ok, 1)
            pool.affine_select(out=real[:, NT - 1:NT], in_=real[:, NT - 1:NT], compare_op=ALU.is_ge,
                               fill=0.0, base=LAST - 1, pattern=[[0, 1]],
                               channel_multiplier=-1).then_inc(ident_ok, 1)

            def store_table(t, s):
                pool.wait_ge(trow_ok, t + 1)
                pool.wait_ge(er_ok, t + 1)
                pool.wait_ge(ident_ok, 2)
                pool.dma_start(scr["table"][row_of(t), :, :].rearrange("a p n -> (a p) n"),
                               trow[:, s, 0:ROW]).then_inc(table_out[s], 16)
                pool.dma_start(scr["er"][row_of(t), :, :].rearrange("a p n -> (a p) n"),
                               er3[:, s, :]).then_inc(table_out[s], 16)

            tiles(pool, store_table)
            pool.wait_ge(kmax_ok, NT)
            pool.partition_all_reduce(kmaxb[:, :], kmax[:, :], P, RMAX).then_inc(kmaxb_ok, 1)

            def store_mix(t, s):
                pool.wait_ge(mixf_ok, t + 1)
                pool.wait_ge(ident_ok, 2)
                pool.dma_start(scr["xmix"][row_of(t), :, :].rearrange("a p n -> (a p) n"),
                               mixf[:, s, :]).then_inc(mix_out[s], 16)

            tiles(pool, store_mix)
            pool.wait_ge(table_out[0], 32 * ((NT + 1) // 2))
            pool.wait_ge(table_out[1], 32 * (NT // 2))
            pool.wait_ge(mix_out[0], 16 * ((NT + 1) // 2))
            pool.wait_ge(mix_out[1], 16 * (NT // 2))

        @block.scalar
        def _(act):
            act.wait_ge(attn_w, 1)
            for k in range(KD):
                act.copy(wcat[:, k, D:D + 2 * HT], ps_ft[k][:, 0:2 * HT]).then_inc(attn_wc, 1)
            act.wait_ge(eps_ok, 1)

            def turn(t, s):
                act.wait_ge(var_ok, t + 1)
                act.activation(rstd[:, s, :], mv[:, s, 1:2], ACT.Sqrt, bias=eps[:, 0:1]).then_inc(std, 1)
                act.wait_ge(xnT_ps, t + 1)
                if later(t):
                    act.wait_ge(proj, t - 1)
                act.copy(xnT[:, s, :, :], ps_tr[s][:, :, :]).then_inc(xnT_ok, 1)

            def keep(t, s):
                act.wait_ge(proj, t + 1)
                if later(t):
                    act.wait_ge(er_ok, t - 1)
                    act.wait_ge(table_out[s], (t - s) * 16)
                act.copy(trow[:, s, :], ps_ft[s][:, 0:D + 2 * HT]).then_inc(trow_ok, 1)
                act.copy(qtile[:, row_of(t), :].rearrange("p a n -> p (a n)"),
                         ps_qk[s][:, 0:D]).then_inc(kept, 1)
                act.copy(ktile[:, row_of(t), :].rearrange("p a n -> p (a n)"),
                         ps_qk[s][:, D:2 * D]).then_inc(kept, 1)
                act.copy(vtile[:, row_of(t), :].rearrange("p a n -> p (a n)"),
                         ps_v[s][:, 0:D]).then_inc(kept, 1)

            tiles(act, turn, keep, 2)

            def exp_k(t, s):
                act.wait_ge(ksub, t + 1)
                act.activation(kexp[:, s, :], kexp[:, s, :], ACT.Exp).then_inc(kexp_ok, 1)

            tiles(act, exp_k)

            def soften(t, s):
                act.wait_ge(qsub, t + 1)
                act.activation(qsm[:, s, :], qsm[:, s, :], ACT.Exp).then_inc(qexp, 1)
                act.wait_ge(qT_ps, t + 1)
                if later(t):
                    act.wait_ge(out_mm, t - 1)
                act.copy(qT[:, s, :, :], ps_tr[s][:, :, :]).then_inc(qT_ok, 1)

            def deviate(t, s):
                act.wait_ge(ln_var, t + 1)
                act.activation(rstd[:, s, :], mv[:, s, 1:2], ACT.Sqrt, bias=eps[:, 0:1]).then_inc(ln_std, 1)

            tiles(act, soften, deviate, 2)

        @block.vector
        def _(dve):
            def norm(t, s):
                dve.wait_ge(x_in[s], (t - s) * 8 + 16)
                dve.bn_stats(st[:, s, :], xin[:, s, :]).then_inc(stats, 1)
                dve.wait_ge(stats, t + 1)
                settle(dve)
                dve.bn_aggr(mv[:, s, :], st[:, s, :]).then_inc(var_ok, 1)
                dve.wait_ge(std, t + 1)
                dve.reciprocal(rstd[:, s, :], rstd[:, s, :]).then_inc(rstd_ok, 1)
                dve.wait_ge(rstd_ok, t + 1)
                if later(t):
                    dve.wait_ge(xnT_ps, t - 1)
                dve.tensor_scalar(xn[:, s, :], xin[:, s, :], mv[:, s, 0:1], rstd[:, s, 0:1],
                                  ALU.subtract, ALU.mult).then_inc(xn_ok, 1)

            def split(t, s):
                dve.wait_ge(trow_ok, t + 1)
                if later(t):
                    dve.wait_ge(table_out[s], (t - s) * 16)
                er = trow[:, s, ROW:ROW + HT]
                dve.tensor_copy(er3[:, s, 0:HT], er).then_inc(er_hi, 1)
                dve.wait_ge(er_hi, t + 1)
                dve.tensor_tensor(er_a[:, s, :], er, er3[:, s, 0:HT], ALU.subtract).then_inc(er_r1, 1)
                dve.wait_ge(er_r1, t + 1)
                dve.tensor_copy(er3[:, s, HT:2 * HT], er_a[:, s, :]).then_inc(er_mid, 1)
                dve.wait_ge(er_mid, t + 1)
                dve.tensor_tensor(er_b[:, s, :], er_a[:, s, :], er3[:, s, HT:2 * HT],
                                  ALU.subtract).then_inc(er_r2, 1)
                dve.wait_ge(er_r2, t + 1)
                dve.tensor_copy(er3[:, s, 2 * HT:3 * HT], er_b[:, s, :]).then_inc(er_ok, 1)
                kk = ktile[:, row_of(t), :].rearrange("p a n -> p (a n)")
                dve.wait_ge(kept, t * 3 + 2)
                if isinstance(t, int) and t == 0:
                    dve.tensor_copy(kmax[:, :], kk).then_inc(kmax_ok, 1)
                else:
                    dve.wait_ge(kmax_ok, t)
                    dve.tensor_tensor(kmax[:, :], kmax[:, :], kk, ALU.max).then_inc(kmax_ok, 1)

            tiles(dve, norm, split, 2)
            dve.wait_ge(kmaxb_ok, 1)

            def sub_k(t, s):
                dve.wait_ge(kept, 3 * NT)
                if later(t):
                    dve.wait_ge(ctx_mm, t - 1)
                dve.tensor_tensor(kexp[:, s, :], ktile[:, row_of(t), :].rearrange("p a n -> p (a n)"),
                                  kmaxb[:, :], ALU.subtract).then_inc(ksub, 1)

            tiles(dve, sub_k)

            dve.memset(ctx_sb[:, :, :], 0.0).then_inc(ctx_z, 1)
            dve.wait_ge(ctx_mm, NT)
            dve.wait_ge(ctx_z, 1)
            for c in range(KD):
                for j in range(4):
                    r = slice(DH * j, DH * j + DH)
                    dve.tensor_copy(ctx_sb[r, c, DH * j:DH * j + DH],
                                    ps_ft[c][r, P * c + DH * j:P * c + DH * j + DH]).then_inc(ctx_c, 1)
                dve.reciprocal(rsum[:, c:c + 1], ps_ft[c][:, D:D + 1]).then_inc(rsum_ok, 1)
            dve.wait_ge(ctxT_ps, 1)
            dve.tensor_copy(ctxT[:, :, :], ps_tr[0][:, :, :]).then_inc(ctxT_ok, 1)
            dve.wait_ge(mix_mm, 1)
            dve.wait_ge(rsum_ok, 2)
            for c in range(KD):
                dve.tensor_scalar(mixw[:, c, :], ps_qk[c][:, 0:D], rsum[:, c:c + 1], SCALE,
                                  ALU.mult, ALU.mult).then_inc(mixw_ok, 1)

            def soften(t, s):
                q = qtile[:, row_of(t), :].rearrange("p a (h d) -> p (a h) d", h=H)
                qs = qsm[:, s, :].rearrange("p (h d) -> p h d", h=H)
                dve.tensor_reduce(qmax[:, :], q, AX_X, ALU.max).then_inc(qmax_ok, 1)
                dve.wait_ge(qmax_ok, t + 1)
                if later(t):
                    dve.wait_ge(qT_ps, t - 1)
                dve.tensor_tensor(qs, q, qmax[:, :].unsqueeze(2).broadcast_to([P, H, DH]),
                                  ALU.subtract).then_inc(qsub, 1)
                dve.wait_ge(qexp, t + 1)
                dve.tensor_reduce(qsum[:, :], qs, AX_X, ALU.add).then_inc(qsum_ok, 1)
                dve.wait_ge(qsum_ok, t + 1)
                dve.reciprocal(qsum[:, :], qsum[:, :]).then_inc(qrec, 1)
                dve.wait_ge(qrec, t + 1)
                dve.tensor_tensor(qs, qs, qsum[:, :].unsqueeze(2).broadcast_to([P, H, DH]),
                                  ALU.mult).then_inc(qsm_ok, 1)

            def finish(t, s):
                dve.wait_ge(out_mm, t + 1)
                dve.bn_stats(st[:, s, :], ps_v[s][:, 0:D]).then_inc(ln_st, 1)
                dve.wait_ge(ln_st, t + 1)
                settle(dve)
                dve.bn_aggr(mv[:, s, :], st[:, s, :]).then_inc(ln_var, 1)
                dve.wait_ge(ln_std, t + 1)
                dve.reciprocal(rstd[:, s, :], rstd[:, s, :]).then_inc(ln_rstd, 1)
                dve.wait_ge(ln_rstd, t + 1)
                dve.tensor_scalar(mixo[:, s, :], ps_v[s][:, 0:D], mv[:, s, 0:1], rstd[:, s, 0:1],
                                  ALU.subtract, ALU.mult).then_inc(ln_n, 1)
                dve.wait_ge(ln_n, t + 1)
                dve.tensor_tensor(mixo[:, s, :], mixo[:, s, :], gamma[:, :], ALU.mult).then_inc(ln_g, 1)
                dve.wait_ge(ln_g, t + 1)
                if later(t):
                    dve.wait_ge(mix_out[s], (t - s) * 8)
                dve.wait_ge(xre_in[s], (t - s) * 8 + 16)
                dve.tensor_tensor(mixf[:, s, :], mixo[:, s, :], xre[:, s, :],
                                  ALU.add).then_inc(mixf_ok, 1)

            tiles(dve, soften, finish, 2)

        @block.tensor
        def _(pe):
            pe.wait_ge(weights_in, 16 * 5)
            pe.wait_ge(blocks_in, 16 * 2 * H)
            for k in range(KD):
                for c in range(KD):
                    last = pe.matmul(ps_ft[k][:, 0:2 * HT], wnT[:, c, k * P:k * P + P], bd[:, c, :],
                                     start=(c == 0), stop=(c == KD - 1))
            last.then_inc(attn_w, 1)
            pe.wait_ge(attn_wc, KD)
            pe.wait_ge(ident_ok, 2)

            def turn(t, s):
                pe.wait_ge(xn_ok, t + 1)
                if later(t):
                    pe.wait_ge(xnT_ok, t - 1)
                for k in range(KD):
                    last = pe.transpose(ps_tr[s][:, k, :], xn[:, s, k * P:k * P + P], ident[:, :])
                last.then_inc(xnT_ps, 1)

            def project(t, s):
                pe.wait_ge(xnT_ok, t + 1)
                if later(t):
                    pe.wait_ge(kept, (t - 1) * 3)
                for k in range(KD):
                    pe.matmul(ps_ft[s][:, 0:D + 2 * HT], xnT[:, s, k, :], wcat[:, k, :],
                              start=(k == 0), stop=(k == KD - 1))
                for k in range(KD):
                    pe.matmul(ps_qk[s][:, :], xnT[:, s, k, :], wqkv[:, k, 0:2 * D],
                              start=(k == 0), stop=(k == KD - 1))
                for k in range(KD):
                    last = pe.matmul(ps_v[s][:, 0:D], xnT[:, s, k, :], wqkv[:, k, 2 * D:3 * D],
                                     start=(k == 0), stop=(k == KD - 1))
                last.then_inc(proj, 1)

            tiles(pe, turn, project)
            pe.wait_ge(kept, 3 * NT)
            pe.wait_ge(kmax_ok, NT)
            pe.wait_ge(trow_ok, NT)

            def context(t, s, start, stop):
                pe.wait_ge(kexp_ok, t + 1)
                for c in range(KD):
                    pe.matmul(ps_ft[c][:, 0:D], kexp[:, s, c * P:c * P + P],
                              vtile[:, row_of(t), :].rearrange("p a n -> p (a n)"),
                              start=start, stop=stop, skip_group_check=True)
                for c in range(KD):
                    last = pe.matmul(ps_ft[c][:, D:D + 1], kexp[:, s, c * P:c * P + P],
                                     real[:, row_of(t)], start=False, stop=stop, skip_group_check=True)
                last.then_inc(ctx_mm, 1)

            context(0, 0, True, False)
            with pe.Fori(0, (NT - 3) // 2) as k:
                for u in (0, 1):
                    context(k * 2 + (1 + u), (1 + u) % 2, False, False)
            context(NT - 2, 1, False, False)
            context(NT - 1, 0, False, True)

            pe.wait_ge(ctx_c, 2 * 4)
            for c in range(KD):
                last = pe.transpose(ps_tr[0][:, c, :], ctx_sb[:, c, :], ident[:, :])
            last.then_inc(ctxT_ps, 1)
            pe.wait_ge(ctxT_ok, 1)
            for c in range(KD):
                last = pe.matmul(ps_qk[c][:, 0:D], ctxT[:, c, :], wout[:, c, :], start=True, stop=True)
            last.then_inc(mix_mm, 1)
            pe.wait_ge(mixw_ok, KD)

            def turn_q(t, s):
                pe.wait_ge(qsm_ok, t + 1)
                if later(t):
                    pe.wait_ge(qT_ok, t - 1)
                for k in range(KD):
                    last = pe.transpose(ps_tr[s][:, k, :], qsm[:, s, k * P:k * P + P], ident[:, :])
                last.then_inc(qT_ps, 1)

            def attend(t, s):
                pe.wait_ge(qT_ok, t + 1)
                if later(t):
                    pe.wait_ge(ln_n, t - 1)
                for k in range(KD):
                    last = pe.matmul(ps_v[s][:, 0:D], qT[:, s, k, :], mixw[:, k, :],
                                     start=(k == 0), stop=(k == KD - 1))
                last.then_inc(out_mm, 1)

            tiles(pe, turn_q, attend)


def phase_edge_tables(nc, io, scr):
    with ExitStack() as ctx:
        kit = Kit(nc, ctx)
        sb, sem = kit.sb, kit.sem
        d_em = sb("d_em", [P, EL], I32)
        dn_em = sb("dn_em", [P, EL], I32)
        d_lin = sb("d_lin", [P, EL], I32)
        dp_lin = sb("dp_lin", [P, EL], I32)
        dm = sb("dm", [P, EL])
        d16 = sb("d16", [P, EL], U16)
        same = sb("same", [P, EL])
        pen = sb("pen", [P, EL], BF16)
        gf = sb("gf", [P, G - 1], I32)
        gt = sb("gt", [P, G - 1], I32)
        gidx = sb("gidx", [P, G - 1], I32)
        gb = sb("gb", [P, G - 1])
        vcol = sb("vcol", [P, 2], I32)
        vf = sb("vf", [P, 2])
        cmp = sb("cmp", [P, 2, G - 1])
        gt_f = sb("gt_f", [P, 2, 2])
        gt_i = sb("gt_i", [P, 2, 2], I32)
        loaded = sem("e_loaded")
        iotas = sem("e_iotas")
        step = sem("e_step")
        dm_ok = sem("e_dm_ok")
        d16_ok = sem("e_d16_ok")
        pen_ok = sem("e_pen_ok")
        visits_ok = sem("e_visits_ok")
        stored = sem("e_stored")
        block = ctx.enter_context(nc.Block())

        @block.sync
        def _(sp):
            for dst, name in ((d_em, "dst_em"), (dn_em, "dst_next_em"), (d_lin, "dst_lin"), (dp_lin, "dst_prev_lin")):
                sp.dma_start(dst[:, :], io[name].rearrange("(p n) -> p n", p=P)).then_inc(loaded, 16)
            sp.dma_start(gf[:, :], io["group_first"].rearrange("(a n) -> a n", a=1).broadcast_to([P, G - 1])) \
                .then_inc(loaded, 16)
            sp.wait_ge(dm_ok, 1)
            sp.dma_start(scr["dm"].rearrange("g p c -> (g p c)").rearrange("(q n) -> q n", q=P),
                         dm[:, :]).then_inc(stored, 16)
            sp.wait_ge(d16_ok, 1)
            sp.dma_start(scr["dst16"].rearrange("(p n) -> p n", p=P), d16[:, :]).then_inc(stored, 16)
            sp.wait_ge(pen_ok, 1)
            sp.dma_start(scr["pen"][0:EP].rearrange("(p n) -> p n", p=P), pen[:, :]).then_inc(stored, 16)
            sp.dma_start(scr["pen"][EP:EP + 1].rearrange("(p n) -> p n", p=1), pen[0:1, 0:1]).then_inc(stored, 16)
            sp.wait_ge(visits_ok, 1)
            for k in range(2):
                sp.dma_start(scr["visit_group"][k * P:(k + 1) * P].rearrange("(p a) -> p a", a=1),
                             gt_i[:, 0, k:k + 1]).then_inc(stored, 16)
                sp.dma_start(scr["visit_tile"][k * P:(k + 1) * P].rearrange("(p a) -> p a", a=1),
                             gt_i[:, 1, k:k + 1]).then_inc(stored, 16)
                sp.dma_start(scr["visit_tile_f"][k * P:(k + 1) * P].rearrange("(p a) -> p a", a=1),
                             gt_f[:, 1, k:k + 1]).then_inc(stored, 16)
            sp.wait_ge(stored, 16 * 10)

        @block.gpsimd
        def _(pool):
            pool.iota(gidx[:, :], pattern=[[1, G - 1]], base=1, channel_multiplier=0).then_inc(iotas, 1)
            pool.iota(vcol[:, :], pattern=[[P, 2]], base=0, channel_multiplier=1).then_inc(iotas, 1)

        @block.vector
        def _(dve):
            dve.wait_ge(loaded, 16 * 5)
            dve.tensor_tensor(dm[:, :], d_em[:, :], dn_em[:, :], ALU.not_equal).then_inc(dm_ok, 1)
            dve.tensor_copy(d16[:, :], d_lin[:, :]).then_inc(d16_ok, 1)
            dve.tensor_tensor(same[:, :], d_lin[:, :], dp_lin[:, :], ALU.not_equal).then_inc(step, 1)
            dve.wait_ge(step, 1)
            dve.tensor_scalar(pen[:, :], same[:, :], NEG, None, ALU.mult).then_inc(pen_ok, 1)
            dve.tensor_single_scalar(gt[:, :], gf[:, :], 7, ALU.arith_shift_right).then_inc(step, 1)
            dve.wait_ge(iotas, 2)
            dve.wait_ge(step, 2)
            dve.tensor_tensor(gb[:, :], gt[:, :], gidx[:, :], ALU.add).then_inc(step, 1)
            dve.tensor_copy(vf[:, :], vcol[:, :]).then_inc(step, 1)
            dve.wait_ge(step, 4)
            for k in range(2):
                dve.tensor_scalar(cmp[:, k, :], gb[:, :], vf[:, k:k + 1], None, ALU.is_le).then_inc(step, 1)
            dve.wait_ge(step, 6)
            dve.tensor_reduce(gt_f[:, 0, :], cmp[:, :, :], AX_X, ALU.add).then_inc(step, 1)
            dve.wait_ge(step, 7)
            dve.tensor_tensor(gt_f[:, 1, :], vf[:, :], gt_f[:, 0, :], ALU.subtract).then_inc(step, 1)
            dve.wait_ge(step, 8)
            dve.tensor_copy(gt_i[:, :, :], gt_f[:, :, :]).then_inc(visits_ok, 1)


def phase_edges(nc, io, scr):
    with ExitStack() as ctx:
        kit = Kit(nc, ctx)
        sb, ps, sem = kit.sb, kit.ps, kit.sem
        vg = sb("vg", [1, VP], I32)
        vt = sb("vt", [1, VP], I32)
        tvb = sb("tvb", [P, VP + 1])
        tbase = sb("tbase", [P, VP])
        nodeid = sb("nodeid", [P, VP])
        fresh = sb("fresh", [P, VP])
        pcol_i = sb("pcol_i", [P, 1], I32)
        pcol = sb("pcol", [P, 1])
        ident = sb("ident2", [P, P])
        bdm = sb("bdm", [P, C * HT])
        idx = sb("idx", [P, SLOTS, C], I32)
        a4 = sb("a4", [P, SLOTS, C * T])
        a16 = sb("a16", [P, SLOTS, P])
        dme = sb("dme", [P, SLOTS, C])
        d16r = sb("d16r", [P, SLOTS, GE], U16)
        penr = sb("penr", [H, SLOTS, GE + 1], BF16)
        er3 = sb("er3e", [P, SLOTS, 3 * HT], BF16)
        gat = sb("gat", [P, SLOTS, C, ROW])
        ohT = sb("ohT", [P, 2, GE], BF16)
        identb = sb("identb", [P, P], BF16)
        oh = sb("oh", [P, SLOTS, C, P])
        zm = sb("zm", [P, 2, C * HT])
        lg = sb("lg", [P, 2, C * H])
        e = sb("e", [P, 2, C * H])
        runf = sb("runf", [H, 2, GE])
        runm = sb("runm", [H, 2, GE])
        dlt = sb("dlt", [P, 2, C * H])
        msg = sb("msg", [P, 2, C, SUMS])
        acc = sb("acc", [P, 2, SUMS])
        absn = sb("absn", [P, 2, H])
        mg = sb("mg", [P, 2, H])
        ma = sb("ma", [P, 2, H])
        dd = sb("dd", [P, 2, 2, H])
        sc = sb("sc", [P, 2, 2, H])
        tmp = sb("tmp", [P, 2, H * HW])

        ps_z = [ps(f"ps_z{i}", [P, 512]) for i in range(2)]
        ps_e = ps("ps_e", [P, 1024])
        ps_m = ps("ps_m", [P, 512])
        ps_o = ps("ps_o", [P, C, P], BF16)
        ps_s = [ps(f"ps_s{i}", [P, 512]) for i in range(2)]

        tables_in = sem("g_tables_in")
        blocks_in = sem("g_blocks_in")
        pool_step = sem("g_pool_step")
        zeroed = sem("g_zeroed")
        pool_ok = sem("g_pool_ok")
        setup = sem("g_setup")
        setup_ok = sem("g_setup_ok")
        in_ = [sem(f"g_in{i}") for i in range(SLOTS)]
        gathered = [sem(f"g_gathered{i}") for i in range(SLOTS)]
        ohT_ok = sem("g_ohT_ok")
        oh_ps = sem("g_oh_ps")
        oh_ok = sem("g_oh_ok")
        z_mm = sem("g_z_mm")
        terms = sem("g_terms")
        zm_ok = sem("g_zm_ok")
        lg_ok = sem("g_lg_ok")
        e_ok = sem("g_e_ok")
        eT_ps = sem("g_eT_ps")
        runf_ok = sem("g_runf_ok")
        runm_ok = sem("g_runm_ok")
        m_ps = sem("g_m_ps")
        dlt_ok = sem("g_dlt_ok")
        mend_ok = sem("g_mend_ok")
        p_ok = sem("g_p_ok")
        msg_ok = sem("g_msg_ok")
        sums = sem("g_sums")
        small = sem("g_small")
        dd_ok = sem("g_dd_ok")
        sc_ok = sem("g_sc_ok")
        max_ok = sem("g_max_ok")
        scaled = sem("g_scaled")
        acc_ok = sem("g_acc_ok")
        acc_out = [sem(f"g_acc_out{i}") for i in range(2)]
        LOADS = 7

        block = ctx.enter_context(nc.Block())

        def visits(eng, step):
            for v in range(FIRST):
                step(v, v % SLOTS)
            with eng.Fori(0, (V - FIRST) // SLOTS - 1) as k:
                for u in range(SLOTS):
                    step(k * SLOTS + (FIRST + u), (FIRST + u) % SLOTS)
            for v in range(V - SLOTS, V):
                step(v, v % SLOTS)

        @block.sync
        def _(sp):
            sp.dma_start(vg[:, :], scr["visit_group"].rearrange("(a n) -> a n", a=1)).then_inc(tables_in, 16)
            sp.dma_start(vt[:, :], scr["visit_tile"].rearrange("(a n) -> a n", a=1)).then_inc(tables_in, 16)
            sp.dma_start(tvb[:, 1:VP + 1], scr["visit_tile_f"].rearrange("(a n) -> a n", a=1)
                         .broadcast_to([P, VP])).then_inc(tables_in, 16)
            sp.wait_ge(zeroed, 1)
            for c in range(C):
                sp.dma_start(bdm[F * c:F * c + F, HT * c:HT * c + HT].rearrange("f (h t) -> f h t", h=H),
                             io["attn_m"].rearrange("h f t -> f h t")).then_inc(blocks_in, 16)
            sp.wait_ge(tables_in, 48)

            def loads(g, t, s, before):
                before()
                sp.dma_start(idx[:, s, :], io["src"][row_of(g), :, :].rearrange("a p c -> (a p) c")).then_inc(in_[s], 16)
                sp.dma_start(a4[:, s, :], io["a4"][row_of(g), :, :].rearrange("a p c -> (a p) c")).then_inc(in_[s], 16)
                sp.dma_start(a16[:, s, :], io["a16"][row_of(g), :, :].rearrange("a p c -> (a p) c")).then_inc(in_[s], 16)
                sp.dma_start(dme[:, s, :], scr["dm"][row_of(g), :, :].rearrange("a p c -> (a p) c")).then_inc(in_[s], 16)
                sp.dma_start(d16r[:, s, :], scr["dst16"].rearrange("(g n) -> g n", n=GE)[row_of(g), :]
                             .broadcast_to([P, GE])).then_inc(in_[s], 16)
                sp.dma_start(penr[:, s, :], scr["pen"][row_of(g * GE, GE + 1)].rearrange("(a n) -> a n", a=1)
                             .broadcast_to([H, GE + 1])).then_inc(in_[s], 16)
                sp.dma_start(er3[:, s, :], scr["er"][row_of(t), :, :].rearrange("a p c -> (a p) c")).then_inc(in_[s], 16)

            def store(t, v, before):
                before()
                sp.dma_start(scr["acc"][row_of(t), :, :].rearrange("a p c -> (a p) c"),
                             acc[:, v, :]).then_inc(acc_out[v], 16)

            def of_visit(table, v, most):
                return sp.value_load(table[0:1, row_of(v)], min_val=0, max_val=most)

            for v in range(SLOTS):
                loads(of_visit(vg, v, G - 1), of_visit(vt, v, NT - 1), v, lambda: None)

            def step(v, s):
                g = of_visit(vg, v + SLOTS, G - 1)
                t = of_visit(vt, v + SLOTS, NT - 1)
                t_now = of_visit(vt, v, NT - 1)

                def slot_free():
                    sp.wait_ge(msg_ok, v + 1)
                    sp.wait_ge(z_mm, v + 1)

                def summed():
                    sp.wait_ge(acc_ok, v + 1)
                    settle(sp)
                    if not (isinstance(v, int) and v == 0):
                        sp.wait_ge(acc_out[(s + 1) % 2], (v + (0 if s % 2 == 0 else 1)) * 8)

                loads(g, t, s, slot_free)
                store(t_now, s % 2, summed)

            for v in range(FIRST):
                step(v, v % SLOTS)
            with sp.Fori(0, (V - FIRST) // SLOTS - 1) as k:
                for u in range(SLOTS):
                    step(k * SLOTS + (FIRST + u), (FIRST + u) % SLOTS)
            for v in range(V - SLOTS, V):
                t_now = of_visit(vt, v, NT - 1)
                sp.wait_ge(acc_ok, v + 1)
                sp.wait_ge(acc_out[(v + 1) % 2], 16 * ((v + 1) // 2))
                sp.dma_start(scr["acc"][row_of(t_now), :, :].rearrange("a p c -> (a p) c"),
                             acc[:, v % 2, :]).then_inc(acc_out[v % 2], 16)
            sp.wait_ge(acc_out[0], 16 * (V // 2))
            sp.wait_ge(acc_out[1], 16 * (V // 2))

        @block.gpsimd
        def _(pool):
            pool.memset(bdm[:, :], 0.0).then_inc(zeroed, 1)
            pool.memset(ident[:, :], 0.0).then_inc(pool_step, 1)
            pool.iota(pcol_i[:, :], pattern=[[0, 1]], base=0, channel_multiplier=1).then_inc(pool_ok, 1)
            pool.wait_ge(pool_step, 1)
            pool.affine_select(out=ident[:, :], in_=ident[:, :], compare_op=ALU.not_equal, fill=1.0,
                               base=0, pattern=[[-1, P]], channel_multiplier=1).then_inc(pool_ok, 1)
            pool.wait_ge(pool_ok, 2)
            pool.tensor_copy(identb[:, :], ident[:, :]).then_inc(pool_ok, 1)

            def gather(v, s):
                pool.wait_ge(in_[s], (v - s) * (4 * LOADS) + 16 * LOADS)
                pool.wait_ge(pool_ok, 3)
                settle(pool)
                for c in range(C):
                    pool.indirect_dma_start(
                        out=gat[:, s, c, :], out_offset=None, in_=scr["table_rows"],
                        in_offset=bass.IndirectOffsetOnAxis(ap=idx[:, s, c:c + 1], axis=0),
                    ).then_inc(gathered[s], 16)

            visits(pool, gather)

        @block.scalar
        def _(act):
            def weights(v, s):
                b = s % 2
                act.wait_ge(dlt_ok, v + 1)
                act.activation(msg[:, b, :, 0:H * HW].rearrange("p c (h w) -> p c h w", w=HW)[:, :, :, DH],
                               dlt[:, b, :].rearrange("p (c h) -> p c h", h=H), ACT.Exp,
                               scale=THIRD).then_inc(p_ok, 1)

            def one_hot(v, s):
                act.wait_ge(oh_ps, v + 1)
                if not (isinstance(v, int) and v < SLOTS):
                    act.wait_ge(sums, v - (SLOTS - 1))
                act.copy(oh[:, s, :, :], ps_o[:, :, :]).then_inc(oh_ok, 1)

            def rescale(v, s):
                b, o = s % 2, (s + 1) % 2
                act.wait_ge(dd_ok, v * 2 + 2)
                act.activation(sc[:, b, :, :], dd[:, b, :, :], ACT.Exp, scale=THIRD).then_inc(sc_ok, 1)
                act.wait_ge(sc_ok, v + 1)
                for h in range(H):
                    cols = slice(h * HW, h * HW + HW)
                    act.mul(tmp[:, b, cols], ps_s[b][:, cols], sc[:, b, 1, h:h + 1]).then_inc(scaled, 1)
                    act.mul(acc[:, b, cols], acc[:, o, cols], sc[:, b, 0, h:h + 1]).then_inc(scaled, 1)

            one_hot(0, 0)

            def step(v, s):
                if not (isinstance(v, int) and v == V - 1):
                    one_hot(v + 1, (s + 1) % SLOTS)
                if not (isinstance(v, int) and v < 2):
                    rescale(v - 2, (s - 2) % SLOTS)
                weights(v, s)

            visits(act, step)
            rescale(V - 2, (V - 2) % SLOTS)
            rescale(V - 1, (V - 1) % SLOTS)

        @block.vector
        def _(dve):
            dve.memset(acc[:, :, :], 0.0).then_inc(setup, 1)
            dve.memset(tvb[:, 0:1], -1.0).then_inc(setup, 1)
            dve.wait_ge(pool_ok, 3)
            dve.wait_ge(tables_in, 48)
            dve.tensor_copy(pcol[:, :], pcol_i[:, :]).then_inc(setup, 1)
            dve.tensor_scalar(tbase[:, :], tvb[:, 1:VP + 1], float(P), None, ALU.mult).then_inc(setup, 1)
            dve.wait_ge(setup, 4)
            dve.tensor_scalar(nodeid[:, :], tbase[:, :], pcol[:, 0:1], None, ALU.add).then_inc(setup, 1)
            dve.tensor_tensor(fresh[:, :], tvb[:, 1:VP + 1], tvb[:, 0:VP], ALU.not_equal).then_inc(setup, 1)
            dve.wait_ge(setup, 6)
            dve.tensor_scalar(fresh[:, :], fresh[:, :], 2.0 * NEG, None, ALU.mult).then_inc(setup_ok, 1)
            dve.wait_ge(setup_ok, 1)

            def select(v, s):
                b = s % 2
                dve.wait_ge(in_[s], (v - s) * (4 * LOADS) + 16 * LOADS)
                if not (isinstance(v, int) and v < 2):
                    dve.wait_ge(oh_ps, v - 1)
                dve.tensor_scalar(ohT[:, b, :], d16r[:, s, :], nodeid[:, row_of(v)], None,
                                  ALU.is_equal).then_inc(ohT_ok, 1)

            select(0, 0)
            select(1, 1)

            def step(v, s):
                number = isinstance(v, int)
                b, o = s % 2, (s + 1) % 2
                merging = not (number and v < 2)
                w, ps_w = v - 2, (s - 2) % SLOTS % 2
                assert ps_w == b
                mrg = ps_s[b][:, 0:H * HW].rearrange("p (h w) -> p h w", w=HW)

                dve.wait_ge(z_mm, v + 1)
                dve.tensor_tensor(
                    zm[:, b, :].rearrange("p (c h t) -> p c h t", c=C, h=H),
                    ps_z[b][:, 0:C * HT].rearrange("p (c h t) -> p c h t", c=C, h=H),
                    a4[:, s, :].rearrange("p (c t) -> p c t", c=C).unsqueeze(2).broadcast_to([P, C, H, T]),
                    ALU.mult).then_inc(zm_ok, 1)
                if merging:
                    dve.wait_ge(sums, w + 1)
                    dve.tensor_scalar(absn[:, b, :], mrg[:, :, DH], 0.5, NEG, ALU.is_lt,
                                      ALU.mult).then_inc(small, 1)
                    dve.tensor_scalar(ma[:, b, :], acc[:, o, H * HW:SUMS], fresh[:, row_of(w)], None,
                                      ALU.add).then_inc(small, 1)
                dve.wait_ge(zm_ok, v + 1)
                dve.tensor_reduce(lg[:, b, :], zm[:, b, :].rearrange("p (q t) -> p q t", t=T),
                                  AX_X, ALU.add).then_inc(lg_ok, 1)
                if merging:
                    dve.wait_ge(small, w * 3 + 2)
                    dve.tensor_tensor(mg[:, b, :], ps_s[b][:, H * HW:SUMS], absn[:, b, :],
                                      ALU.add).then_inc(small, 1)
                dve.wait_ge(lg_ok, v + 1)
                dve.scalar_tensor_tensor(e[:, b, :], lg[:, b, :], SLOPE, lg[:, b, :], ALU.mult,
                                         ALU.max).then_inc(e_ok, 1)
                if merging:
                    dve.wait_ge(small, w * 3 + 3)
                    if not (number and v < 4):
                        dve.wait_ge(acc_out[b], (w - b) * 8)
                    dve.tensor_tensor(acc[:, b, H * HW:SUMS], ma[:, b, :], mg[:, b, :],
                                      ALU.max).then_inc(max_ok, 1)
                if not (number and v == 0):
                    messages(v - 1, (s - 1) % SLOTS)
                if merging:
                    dve.wait_ge(max_ok, w + 1)
                    dve.tensor_tensor(dd[:, b, 0, :], ma[:, b, :], acc[:, b, H * HW:SUMS],
                                      ALU.subtract).then_inc(dd_ok, 1)
                    dve.tensor_tensor(dd[:, b, 1, :], mg[:, b, :], acc[:, b, H * HW:SUMS],
                                      ALU.subtract).then_inc(dd_ok, 1)

                dve.wait_ge(eT_ps, v + 1)
                if not (number and v < 2):
                    dve.wait_ge(m_ps, v - 1)
                dve.tensor_tensor_scan(runf[:, b, :], penr[:, s, 0:GE], ps_e[0:H, :], NEG,
                                       ALU.add, ALU.max).then_inc(runf_ok, 1)
                dve.wait_ge(runf_ok, v + 1)
                dve.tensor_tensor_scan(runm[:, b, ::-1], penr[:, s, GE:0:-1], runf[:, b, ::-1], NEG,
                                       ALU.add, ALU.max).then_inc(runm_ok, 1)
                if not (number and v >= V - 2):
                    select(v + 2, (s + 2) % SLOTS)

                dve.wait_ge(m_ps, v + 1)
                if merging:
                    dve.wait_ge(sums, v - 1)
                dve.tensor_tensor(dlt[:, b, :], e[:, b, :], ps_m[:, 0:C * H], ALU.subtract).then_inc(dlt_ok, 1)
                dve.tensor_tensor(msg[:, b, :, H * HW:SUMS],
                                  ps_m[:, 0:C * H].rearrange("p (c h) -> p c h", c=C),
                                  dme[:, s, :].unsqueeze(2).broadcast_to([P, C, H]),
                                  ALU.mult).then_inc(mend_ok, 1)
                if merging:
                    join(w, s)

            def messages(v, s):
                dve.wait_ge(p_ok, v + 1)
                dve.wait_ge(gathered[s], (v - s) * (4 * C) + 16 * C)
                m4 = msg[:, s % 2, :, 0:H * HW].rearrange("p c (h w) -> p c h w", w=HW)
                dve.tensor_tensor(m4[:, :, :, 0:DH],
                                  gat[:, s, :, 0:D].rearrange("p c (h d) -> p c h d", h=H),
                                  m4[:, :, :, DH:HW].broadcast_to([P, C, H, DH]),
                                  ALU.mult).then_inc(msg_ok, 1)

            def join(v, s):
                b = s % 2
                dve.wait_ge(scaled, v * (2 * H) + 2 * H)
                dve.tensor_tensor(acc[:, b, 0:H * HW], acc[:, b, 0:H * HW], tmp[:, b, :],
                                  ALU.add).then_inc(acc_ok, 1)

            def merge_alone(v, s):
                b, o = s % 2, (s + 1) % 2
                dve.wait_ge(sums, v + 1)
                dve.tensor_scalar(absn[:, b, :], ps_s[b][:, 0:H * HW].rearrange("p (h w) -> p h w", w=HW)[:, :, DH],
                                  0.5, NEG, ALU.is_lt, ALU.mult).then_inc(small, 1)
                dve.tensor_scalar(ma[:, b, :], acc[:, o, H * HW:SUMS], fresh[:, row_of(v)], None,
                                  ALU.add).then_inc(small, 1)
                dve.wait_ge(small, v * 3 + 2)
                dve.tensor_tensor(mg[:, b, :], ps_s[b][:, H * HW:SUMS], absn[:, b, :],
                                  ALU.add).then_inc(small, 1)
                dve.wait_ge(small, v * 3 + 3)
                dve.wait_ge(acc_out[b], (v - b) * 8)
                dve.tensor_tensor(acc[:, b, H * HW:SUMS], ma[:, b, :], mg[:, b, :], ALU.max).then_inc(max_ok, 1)
                dve.wait_ge(max_ok, v + 1)
                for side, m in enumerate((ma, mg)):
                    dve.tensor_tensor(dd[:, b, side, :], m[:, b, :], acc[:, b, H * HW:SUMS],
                                      ALU.subtract).then_inc(dd_ok, 1)
                join(v, s)

            visits(dve, step)
            messages(V - 1, (V - 1) % SLOTS)
            merge_alone(V - 2, (V - 2) % SLOTS)
            merge_alone(V - 1, (V - 1) % SLOTS)

        @block.tensor
        def _(pe):
            pe.wait_ge(blocks_in, 16 * C)
            pe.wait_ge(pool_ok, 3)

            def edge_terms(v, s):
                b = s % 2
                pe.wait_ge(in_[s], (v - s) * (4 * LOADS) + 16 * LOADS)
                if not (isinstance(v, int) and v < 2):
                    pe.wait_ge(zm_ok, v - 1)
                pe.matmul(ps_z[b][:, 0:C * HT], a16[:, s, :], bdm[:, :], start=True, stop=False,
                          skip_group_check=True)
                pe.wait_ge(ohT_ok, v + 1)
                for c in range(C):
                    for part in range(3):
                        last = pe.matmul(ps_z[b][:, c * HT:(c + 1) * HT], ohT[:, b, c * P:(c + 1) * P],
                                         er3[:, s, part * HT:(part + 1) * HT], start=False,
                                         stop=False, skip_group_check=True)
                last.then_inc(terms, 1)
                if not (isinstance(v, int) and v < 1):
                    pe.wait_ge(oh_ok, v)
                settle(pe)
                for c in range(C):
                    last = pe.transpose(ps_o[:, c, :], ohT[:, b, c * P:(c + 1) * P], identb[:, :])
                last.then_inc(oh_ps, 1)

            def source_terms(v, s):
                pe.wait_ge(gathered[s], (v - s) * (4 * C) + 16 * C)
                pe.matmul(ps_z[s % 2][:, 0:C * HT].rearrange("p (c n) -> p c n", c=C), ident[:, :],
                          gat[:, s, :, D:ROW], start=False, stop=True, skip_group_check=True).then_inc(z_mm, 1)

            def turn_logits(v, s):
                b = s % 2
                pe.wait_ge(e_ok, v + 1)
                if not (isinstance(v, int) and v < 1):
                    pe.wait_ge(runf_ok, v)
                for c in range(C):
                    last = pe.transpose(ps_e[0:H, c * P:(c + 1) * P], e[:, b, c * H:(c + 1) * H], ident[:, :])
                last.then_inc(eT_ps, 1)

            def turn_maxima(v, s):
                b = s % 2
                pe.wait_ge(runm_ok, v + 1)
                if not (isinstance(v, int) and v < 1):
                    pe.wait_ge(mend_ok, v)
                settle(pe)
                for c in range(C):
                    last = pe.transpose(ps_m[:, c * H:(c + 1) * H], runm[0:H, b, c * P:(c + 1) * P],
                                        ident[0:H, 0:H])
                last.then_inc(m_ps, 1)

            def segment_sums(v, s, chunks):
                b = s % 2
                if chunks[0] == 0:
                    pe.wait_ge(msg_ok, v + 1)
                    pe.wait_ge(mend_ok, v + 1)
                    pe.wait_ge(oh_ok, v + 1)
                    if not (isinstance(v, int) and v < 2):
                        pe.wait_ge(acc_ok, v - 1)
                for c in chunks:
                    last = pe.matmul(ps_s[b][:, 0:SUMS], oh[:, s, c, :], msg[:, b, c, :],
                                     start=(c == 0), stop=(c == C - 1), skip_group_check=True)
                if c == C - 1:
                    last.then_inc(sums, 1)

            edge_terms(0, 0)
            source_terms(0, 0)

            def step(v, s):
                more = not (isinstance(v, int) and v == V - 1)
                if more:
                    edge_terms(v + 1, (s + 1) % SLOTS)
                turn_logits(v, s)
                if not (isinstance(v, int) and v == 0):
                    segment_sums(v - 1, (s - 1) % SLOTS, range(0, 5))
                turn_maxima(v, s)
                if more:
                    source_terms(v + 1, (s + 1) % SLOTS)
                if not (isinstance(v, int) and v == 0):
                    segment_sums(v - 1, (s - 1) % SLOTS, range(5, C))

            visits(pe, step)
            segment_sums(V - 1, (V - 1) % SLOTS, range(C))


def phase_ffn(nc, io, scr):
    B = 4
    NB = -(-NT // B)
    with ExitStack() as ctx:
        kit = Kit(nc, ctx)
        sb, ps, sem = kit.sb, kit.ps, kit.sem
        w1 = sb("w1", [P, X, KD, D])
        w2 = sb("w2", [P, X, KD, D])
        wo = sb("wo", [P, X, KD, D])
        wr = sb("wr", [P, KD, X])
        brb = sb("brb", [P, X])
        bo = sb("bo", [X, D])
        bn = sb("bn", [P, 10, X * KD])
        sc = sb("fsc", [P, 2, X * KD])
        sh = sb("fsh", [P, 2, X * KD])
        ident = sb("ident3", [P, P])
        eps = sb("feps", [P, 2])
        am = sb("am", [P, 2, B, SUMS])
        xm = sb("xm", [P, 2, B, D])
        rs = sb("rs", [P, B, H])
        x2 = sb("x2", [P, 2, B, D])
        st = sb("fst", [P, B, 6])
        mv = sb("fmv", [P, B, 2])
        sd = sb("fsd", [P, B])
        xn = sb("fxn", [P, B, D])
        xnT = sb("fxnT", [P, 2, KD, B * P])
        lo = sb("lo", [P, B, X])
        lm = sb("lm", [P, B])
        w = sb("w", [P, 2, B, X])
        wT = sb("wT", [X, B * P])
        h1 = sb("h1", [P, 2, KD, B * P])
        h2 = sb("h2", [P, 2, KD, B * P])
        y = sb("y", [P, 2, B, D])

        ps_t = ps("ps_t", [P, KD, B * P])
        ps_h = [ps(f"ps_h{i}", [P, B * P]) for i in range(4)]
        ps_y = ps("ps_y", [P, B, D])
        bo_y = ps_t[:, :, :].rearrange("p k (a n) -> p (k a) n", n=D)

        weights_in = sem("f_weights_in")
        bn_in = sem("f_bn_in")
        pool_step = sem("f_pool_step")
        pool_ok = sem("f_pool_ok")
        bn_sd = sem("f_bn_sd")
        bn_step = sem("f_bn_step")
        bn_ok = sem("f_bn_ok")
        in_ = [sem(f"f_in{i}") for i in range(2)]
        r0 = sem("f_r0")
        r1 = sem("f_r1")
        v_ok = sem("f_v_ok")
        x2_ok = sem("f_x2_ok")
        st_ok = sem("f_st_ok")
        mv_ok = sem("f_mv_ok")
        sd_ok = sem("f_sd_ok")
        rsd_ok = sem("f_rsd_ok")
        xn_ok = sem("f_xn_ok")
        xnT_ps = sem("f_xnT_ps")
        xnT_ok = sem("f_xnT_ok")
        rt_ps = sem("f_rt_ps")
        lo_ok = sem("f_lo_ok")
        lm_ok = sem("f_lm_ok")
        ls_ok = sem("f_ls_ok")
        le_ok = sem("f_le_ok")
        lsum_ok = sem("f_lsum_ok")
        lrec_ok = sem("f_lrec_ok")
        w_ok = sem("f_w_ok")
        wT_ps = sem("f_wT_ps")
        wT_ok = sem("f_wT_ok")
        bo_ps = sem("f_bo_ps")
        y0_ok = sem("f_y0_ok")
        h1_ps = sem("f_h1_ps")
        h1_ok = sem("f_h1_ok")
        h2_ps = sem("f_h2_ps")
        h2_ok = sem("f_h2_ok")
        y_ps = sem("f_y_ps")
        y_ok = sem("f_y_ok")
        y_out = [sem(f"f_y_out{i}") for i in range(2)]
        block = ctx.enter_context(nc.Block())

        def halves(n):
            return -(-n // 2)

        FULL = NT // B
        assert FULL % 2 == 0 and NB == FULL + 1

        def blocks(prepare, expert, eng):

            def block_of(b, s, n, following):
                for x in range(X):
                    expert(b, s, n, x)
                    if following:
                        prepare(b + 1, 1 - s, following, x)

            for x in range(X):
                prepare(0, 0, B, x)
            for b in range(2):
                block_of(b, b % 2, B, B)
            with eng.Fori(0, (FULL - 4) // 2) as k:
                for u in (0, 1):
                    block_of(k * 2 + (2 + u), u, B, B)
            block_of(FULL - 2, 0, B, B)
            block_of(FULL - 1, 1, B, NT - FULL * B)
            block_of(FULL, 0, NT - FULL * B, 0)

        @block.sync
        def _(sp):
            sp.dma_start(bn[:, :, :], io["bn"].rearrange("p (k n) -> p k n", k=10)).then_inc(bn_in, 16)
            sp.dma_start(wr[:, :, :], io["Wr"].rearrange("(c p) n -> p c n", p=P)).then_inc(weights_in, 16)
            sp.dma_start(brb[:, :], io["br"].rearrange("(a n) -> a n", a=1).broadcast_to([P, X])).then_inc(weights_in, 16)
            sp.dma_start(bo[:, :], io["bo"]).then_inc(weights_in, 16)

            def load(b, s, n):
                if later(b):
                    sp.wait_ge(x2_ok, b - 1)
                sp.dma_start(am[:, s, 0:n, :], scr["acc"][row_of(b * B, n), :, :].rearrange("a p c -> p a c")).then_inc(in_[s], 16)
                sp.dma_start(xm[:, s, 0:n, :], scr["xmix"][row_of(b * B, n), :, :].rearrange("a p c -> p a c")).then_inc(in_[s], 16)

            load(0, 0, B)
            load(1, 1, B)
            for dst, name in ((w1, "W1"), (w2, "W2"), (wo, "Wo")):
                sp.dma_start(dst[:, :, :, :], io[name].rearrange("e (c p) n -> p e c n", p=P)).then_inc(weights_in, 16)
            with sp.Fori(0, (NT // B - 2) // 2) as k:
                for u in (0, 1):
                    load(k * 2 + (2 + u), u, B)
            load(NT // B, 0, NT - NT // B * B)

        @block.gpsimd
        def _(pool):
            pool.memset(ident[:, :], 0.0).then_inc(pool_step, 1)
            pool.memset(eps[:, 0:1], LN_EPS).then_inc(pool_ok, 1)
            pool.memset(eps[:, 1:2], BN_EPS).then_inc(pool_ok, 1)
            pool.wait_ge(pool_step, 1)
            pool.affine_select(out=ident[:, :], in_=ident[:, :], compare_op=ALU.not_equal, fill=1.0,
                               base=0, pattern=[[-1, P]], channel_multiplier=1).then_inc(pool_ok, 1)

            def store(b, s, n):
                pool.wait_ge(y_ok, b * (2 * X) + X * halves(n))
                pool.wait_ge(pool_ok, 3)
                if n == B:
                    pool.dma_start(io["out"][row_of(b * (B * P), B * P), :].rearrange("(a p) c -> p a c", p=P),
                                   y[:, s, :, :]).then_inc(y_out[s], 16)
                else:
                    pool.dma_start(io["out"][N - LAST:N, :], y[0:LAST, s, 0, :]).then_inc(y_out[s], 16)

            for b in range(2):
                store(b, b % 2, B)
            with pool.Fori(0, (FULL - 2) // 2) as k:
                for u in (0, 1):
                    store(k * 2 + (2 + u), u, B)
            store(FULL, 0, NT - FULL * B)
            pool.wait_ge(y_out[0], 16 * ((NB + 1) // 2))
            pool.wait_ge(y_out[1], 16 * (NB // 2))

        @block.scalar
        def _(act):
            act.wait_ge(bn_in, 16)
            act.wait_ge(pool_ok, 3)
            for layer in range(2):
                act.activation(sc[:, layer, :], bn[:, 5 * layer + 4, :], ACT.Sqrt, bias=eps[:, 1:2]).then_inc(bn_sd, 1)
            act.wait_ge(bn_ok, 2)

            def prepare(b, s, n, x):
                if x == 1:
                    act.wait_ge(mv_ok, b + 1)
                    act.activation(sd[:, 0:n], mv[:, 0:n, 1], ACT.Sqrt, bias=eps[:, 0:1]).then_inc(sd_ok, 1)
                elif x == 2:
                    act.wait_ge(xnT_ps, b + 1)
                    act.copy(xnT[:, s, :, 0:n * P], ps_t[:, :, 0:n * P]).then_inc(xnT_ok, 1)
                elif x == 5:
                    act.wait_ge(ls_ok, b + 1)
                    act.activation(lo[:, 0:n, :], lo[:, 0:n, :], ACT.Exp).then_inc(le_ok, 1)

            def expert(b, s, n, x):
                for layer, (hid, done, ok) in enumerate(((h1, h1_ps, h1_ok), (h2, h2_ps, h2_ok))):
                    act.wait_ge(done, b * X + (x + 1))
                    if not (isinstance(b, int) and b == 0 and x < 2) and layer == 1:
                        if x < 2:
                            act.wait_ge(y_ps, b * (2 * X) + (2 * x - 2))
                        else:
                            act.wait_ge(y_ps, b * (2 * X) + (x - 1) * halves(n))
                    for m in range(KD):
                        act.activation(hid[:, x % 2, m, 0:n * P], ps_h[2 * layer + m][:, 0:n * P], ACT.Relu,
                                       bias=sh[:, layer, x * KD + m:x * KD + m + 1],
                                       scale=sc[:, layer, x * KD + m:x * KD + m + 1]).then_inc(ok, 1)

            blocks(prepare, expert, act)

        @block.vector
        def _(dve):
            dve.wait_ge(bn_sd, 2)
            dve.reciprocal(sc[:, :, :], sc[:, :, :]).then_inc(bn_step, 1)
            for layer in range(2):
                dve.tensor_tensor(sh[:, layer, :], bn[:, 5 * layer, :], bn[:, 5 * layer + 3, :],
                                  ALU.subtract).then_inc(bn_step, 1)
            dve.wait_ge(bn_step, 3)
            for layer in range(2):
                dve.tensor_tensor(sc[:, layer, :], sc[:, layer, :], bn[:, 5 * layer + 1, :], ALU.mult).then_inc(bn_step, 1)
            dve.wait_ge(bn_step, 5)
            dve.tensor_tensor(sh[:, :, :], sh[:, :, :], sc[:, :, :], ALU.mult).then_inc(bn_step, 1)
            dve.wait_ge(bn_step, 6)
            for layer in range(2):
                dve.tensor_tensor(sh[:, layer, :], sh[:, layer, :], bn[:, 5 * layer + 2, :], ALU.add).then_inc(bn_ok, 1)
            dve.wait_ge(weights_in, 16 * 6)

            def prepare(b, s, n, x):
                heads = am[:, s, 0:n, 0:H * HW].rearrange("p a (h w) -> p a h w", w=HW)
                if x == 0:
                    dve.wait_ge(in_[s], (b - s) * 16 + 32)
                    dve.tensor_scalar(rs[:, 0:n, :], heads[:, :, :, DH], 1e-30, None, ALU.max).then_inc(r0, 1)
                    dve.wait_ge(r0, b + 1)
                    dve.reciprocal(rs[:, 0:n, :], rs[:, 0:n, :]).then_inc(r1, 1)
                    dve.wait_ge(r1, b + 1)
                    for a in range(n):
                        dve.tensor_tensor(x2[:, s, a, :].rearrange("p (h d) -> p h d", h=H), heads[:, a, :, 0:DH],
                                          rs[:, a, :].unsqueeze(2).broadcast_to([P, H, DH]), ALU.mult).then_inc(v_ok, 1)
                    dve.wait_ge(v_ok, b * B + n)
                    dve.tensor_tensor(x2[:, s, 0:n, :], x2[:, s, 0:n, :], xm[:, s, 0:n, :], ALU.add).then_inc(x2_ok, 1)
                    dve.wait_ge(x2_ok, b + 1)
                    for a in range(n):
                        dve.bn_stats(st[:, a, :], x2[:, s, a, :]).then_inc(st_ok, 1)
                    dve.wait_ge(st_ok, b * B + n)
                    settle(dve)
                    for a in range(n):
                        last = dve.bn_aggr(mv[:, a, :], st[:, a, :])
                    last.then_inc(mv_ok, 1)
                elif x == 1:
                    dve.wait_ge(sd_ok, b + 1)
                    dve.reciprocal(sd[:, 0:n], sd[:, 0:n]).then_inc(rsd_ok, 1)
                    dve.wait_ge(rsd_ok, b + 1)
                    for a in range(n):
                        dve.tensor_scalar(xn[:, a, :], x2[:, s, a, :], mv[:, a, 0:1], sd[:, a:a + 1],
                                          ALU.subtract, ALU.mult).then_inc(xn_ok, 1)
                elif x == 4:
                    dve.wait_ge(rt_ps, b + 1)
                    dve.tensor_tensor(lo[:, 0:n, :], ps_t[:, 0, 0:n * X].rearrange("p (a x) -> p a x", x=X),
                                      brb[:, :].unsqueeze(1).broadcast_to([P, n, X]), ALU.add).then_inc(lo_ok, 1)
                    dve.wait_ge(lo_ok, b + 1)
                    dve.tensor_reduce(lm[:, 0:n], lo[:, 0:n, :], AX_X, ALU.max).then_inc(lm_ok, 1)
                    dve.wait_ge(lm_ok, b + 1)
                    dve.tensor_tensor(lo[:, 0:n, :], lo[:, 0:n, :], lm[:, 0:n].unsqueeze(2).broadcast_to([P, n, X]),
                                      ALU.subtract).then_inc(ls_ok, 1)
                elif x == 5:
                    dve.wait_ge(le_ok, b + 1)
                    dve.tensor_reduce(lm[:, 0:n], lo[:, 0:n, :], AX_X, ALU.add).then_inc(lsum_ok, 1)
                    dve.wait_ge(lsum_ok, b + 1)
                    dve.reciprocal(lm[:, 0:n], lm[:, 0:n]).then_inc(lrec_ok, 1)
                    dve.wait_ge(lrec_ok, b + 1)
                    dve.tensor_tensor(w[:, s, 0:n, :], lo[:, 0:n, :], lm[:, 0:n].unsqueeze(2).broadcast_to([P, n, X]),
                                      ALU.mult).then_inc(w_ok, 1)
                elif x == 6:
                    dve.wait_ge(wT_ps, b + 1)
                    dve.tensor_copy(wT[:, 0:n * P], ps_t[0:X, 1, 0:n * P]).then_inc(wT_ok, 1)
                elif x == 7:
                    dve.wait_ge(bo_ps, b + 1)
                    if later(b):
                        dve.wait_ge(y_out[s], (b - s) * 8)
                    dve.tensor_tensor(y[:, s, 0:n, :], bo_y[:, 0:n, :], x2[:, s, 0:n, :], ALU.add).then_inc(y0_ok, 1)

            def expert(b, s, n, x):
                for half in range(halves(n)):
                    dve.wait_ge(y_ps, b * (2 * X) + (x * halves(n) + half + 1))
                    if x == 0:
                        dve.wait_ge(y0_ok, b + 1)
                    else:
                        dve.wait_ge(y_ok, b * (2 * X) + ((x - 1) * halves(n) + half + 1))
                    for a in range(2 * half, min(2 * half + 2, n)):
                        ins = dve.scalar_tensor_tensor(y[:, s, a, :], ps_y[:, a, :], w[:, s, a, x:x + 1],
                                                       y[:, s, a, :], ALU.mult, ALU.add)
                    ins.then_inc(y_ok, 1)

            blocks(prepare, expert, dve)

        @block.tensor
        def _(pe):
            pe.wait_ge(pool_ok, 3)
            pe.wait_ge(weights_in, 16 * 6)

            def prepare(b, s, n, x):
                if x == 2:
                    pe.wait_ge(xn_ok, b * B + n)
                    if not (isinstance(b, int) and b == 0):
                        pe.wait_ge(y0_ok, b)
                    settle(pe)
                    for k in range(KD):
                        for a in range(n):
                            last = pe.transpose(ps_t[:, k, a * P:(a + 1) * P], xn[:, a, k * P:(k + 1) * P], ident[:, :])
                    last.then_inc(xnT_ps, 1)
                elif x == 3:
                    pe.wait_ge(xnT_ok, b + 1)
                    for a in range(n):
                        for k in range(KD):
                            last = pe.matmul(ps_t[:, 0, a * X:(a + 1) * X], xnT[:, s, k, a * P:(a + 1) * P],
                                             wr[:, k, :], start=(k == 0), stop=(k == KD - 1), skip_group_check=True)
                    last.then_inc(rt_ps, 1)
                elif x == 6:
                    pe.wait_ge(w_ok, b + 1)
                    for a in range(n):
                        last = pe.transpose(ps_t[0:X, 1, a * P:(a + 1) * P], w[:, s, a, :], ident[:, :])
                    last.then_inc(wT_ps, 1)
                elif x == 7:
                    pe.wait_ge(wT_ok, b + 1)
                    for a in range(n):
                        last = pe.matmul(bo_y[:, a, :], wT[:, a * P:(a + 1) * P], bo[:, :], start=True, stop=True)
                    last.then_inc(bo_ps, 1)

            def layer(hid, src, wts, first, x, n):
                for m in range(KD):
                    for k in range(KD):
                        last = pe.matmul(ps_h[first + m][:, 0:n * P], wts[:, x, k, m * P:(m + 1) * P],
                                         src[:, k, 0:n * P], start=(k == 0), stop=(k == KD - 1))
                last.then_inc(hid, 1)

            def up(b, s, n, x):
                if not (isinstance(b, int) and b == 0 and x == 0):
                    pe.wait_ge(h1_ok, b * (2 * X) + 2 * x)
                pe.wait_ge(xnT_ok, b + 1)
                layer(h1_ps, xnT[:, s, :, :], w1, 0, x, n)
                if x > 0:
                    down(b, s, n, x - 1)
                pe.wait_ge(h1_ok, b * (2 * X) + (2 * x + 2))
                if not (isinstance(b, int) and b == 0 and x == 0):
                    pe.wait_ge(h2_ok, b * (2 * X) + 2 * x)
                layer(h2_ps, h1[:, x % 2, :, :], w2, 2, x, n)
                if x == X - 1:
                    down(b, s, n, x)

            def down(b, s, n, x):
                pe.wait_ge(h2_ok, b * (2 * X) + (2 * x + 2))
                for half in range(halves(n)):
                    if x > 0:
                        pe.wait_ge(y_ok, b * (2 * X) + ((x - 1) * halves(n) + half + 1))
                    elif not (isinstance(b, int) and b == 0):
                        pe.wait_ge(y_ok, b * (2 * X) - (1 - half))
                    for a in range(2 * half, min(2 * half + 2, n)):
                        for k in range(KD):
                            last = pe.matmul(ps_y[:, a, :], h2[:, x % 2, k, a * P:(a + 1) * P], wo[:, x, k, :],
                                             start=(k == 0), stop=(k == KD - 1))
                    last.then_inc(y_ps, 1)

            blocks(prepare, up, pe)


INPUTS = {
    "x": ((NT, P, D), F32), "W_n": ((D, D), F32), "W_nT": ((D, D), F32),
    "attn_l": ((H, DH, T), F32), "attn_r": ((H, DH, T), F32), "attn_m": ((H, F, T), F32),
    "Wqkv": ((D, 3 * D), F32), "Wout": ((D, D), F32), "gamma": ((D,), F32),
    "src": ((G, P, C), I32), "a4": ((G, P, C * T), F32), "a16": ((G, P, P), F32),
    "dst_em": ((EP,), I32), "dst_next_em": ((EP,), I32), "dst_lin": ((EP,), I32),
    "dst_prev_lin": ((EP,), I32), "group_first": ((G - 1,), I32),
    "Wr": ((D, X), F32), "br": ((X,), F32), "W1": ((X, D, D), F32), "W2": ((X, D, D), F32),
    "Wo": ((X, D, D), F32), "bo": ((X, D), F32), "bn": ((P, 10 * X * KD), F32),
}
SCRATCH = {
    "table": ((NT, P, ROW), F32), "er": ((NT, P, 3 * HT), BF16), "xmix": ((NT, P, D), F32),
    "dm": ((G, P, C), F32), "dst16": ((EP,), U16), "pen": ((EP + 1,), BF16),
    "visit_group": ((VP,), I32), "visit_tile": ((VP,), I32), "visit_tile_f": ((VP,), F32),
    "acc": ((NT, P, SUMS), F32),
}


def build(nc):
    io = {n: nc.dram_tensor(f"in_{n}", s, dt, kind="ExternalInput").ap() for n, (s, dt) in INPUTS.items()}
    io["out"] = nc.dram_tensor("out", (N, D), F32, kind="ExternalOutput").ap()
    scr = {n: nc.dram_tensor(f"scratch_{n}", s, dt).ap() for n, (s, dt) in SCRATCH.items()}
    scr["table_rows"] = scr["table"].rearrange("t p c -> (t p) c")
    phase_nodes(nc, io, scr)
    phase_edge_tables(nc, io, scr)
    phase_edges(nc, io, scr)
    phase_ffn(nc, io, scr)


def lay_out(i):
    import numpy as np

    def edges(a, fill=0):
        a = np.asarray(a)
        out = np.full((EP,) + a.shape[1:], fill, a.dtype)
        out[:E] = a
        return out

    def edge_major(a):
        return a.reshape(G, C, P).transpose(0, 2, 1)

    dst = edges(i["dst"], PAD_DST)
    following = np.full(EP, -1, dst.dtype)
    following[:-1] = dst[1:]
    following[GE - 1::GE] = -1
    before = np.full(EP, -1, dst.dtype)
    before[1:] = dst[:-1]
    x = np.asarray(i["x"])
    xp = np.zeros((NP, D), x.dtype)
    xp[:N] = x
    bn = np.stack([np.asarray(i["L0_ffn_" + n]).reshape(X, KD, P).transpose(2, 0, 1).reshape(P, X * KD)
                   for n in ("b1", "g1", "be1", "m1", "v1", "b2", "g2", "be2", "m2", "v2")], axis=1)
    laid = {
        "x": xp.reshape(NT, P, D), "W_nT": np.asarray(i["L0_gnn_W_n"]).T,
        "src": edge_major(edges(i["src"])),
        "a4": edges(i["edge_attr_4"]).reshape(G, C, P, T).transpose(0, 2, 1, 3).reshape(G, P, C * T),
        "a16": edges(i["edge_attr_16"]).reshape(G, C, P, F).transpose(0, 1, 3, 2).reshape(G, P, P),
        "dst_em": edge_major(dst).reshape(-1), "dst_next_em": edge_major(following).reshape(-1),
        "dst_lin": dst, "dst_prev_lin": before, "group_first": dst[GE::GE], "bn": bn.reshape(P, 10 * X * KD),
    }
    for n in ("W_n", "attn_l", "attn_r", "attn_m"):
        laid[n] = i["L0_gnn_" + n]
    for n in ("Wqkv", "Wout", "gamma"):
        laid[n] = i["L0_mix_" + n]
    for n in ("Wr", "br", "W1", "W2", "Wo", "bo"):
        laid[n] = i["L0_ffn_" + n]
    return {f"in_{n}": np.ascontiguousarray(laid[n]) for n in INPUTS}


def kernel(**inputs):
    import concourse.bacc as bacc
    from concourse.bass_utils import run_bass_kernel_spmd

    nc = bacc.Bacc("TRN2", target_bir_lowering=False, num_devices=1)
    build(nc)
    r = run_bass_kernel_spmd(nc, [lay_out(inputs)], core_ids=[0])
    return r.results[0]["out"]
```

```python
from contextlib import ExitStack

import concourse.bass as bass
from concourse import mybir

F32 = mybir.dt.float32
BF16 = mybir.dt.bfloat16
I32 = mybir.dt.int32
U16 = mybir.dt.uint16
F32R = mybir.dt.float32r
ALU = mybir.AluOpType
ACT = mybir.ActivationFunctionType
AX_X = mybir.AxisListType.X
RMAX = bass.bass_isa.ReduceOp.max

P = 128
N = 6250
NT = -(-N // P)
NP = NT * P
LAST = N - (NT - 1) * P
D = 256
KD = D // P
H = 8
DH = D // H
T = 4
HT = H * T
F = 16
E = 206250
C = 8
GE = C * P
G = -(-E // GE)
EP = G * GE
PAD_DST = 8191
V = G + NT - 1
VK = -(-V // P)
VP = VK * P
ROW = D + HT
HW = DH + 1
SUMS = H * HW + H
SLOTS = 4
EARLY = 6
NEG = -1.0e30
SLOPE = 0.2
THIRD = 1.0 / 3.0
FIRST = 6
LN_EPS = 1e-5
BN_EPS = 1e-3
SCALE = DH ** -0.5
X = 8
EL = EP // P


class Kit:

    def __init__(self, nc, ctx):
        self.nc, self.ctx = nc, ctx

    def sb(self, name, shape, dt=F32):
        return self.ctx.enter_context(self.nc.sbuf_tensor(name, shape, dt))

    def ps(self, name, shape, dt=F32):
        return self.ctx.enter_context(self.nc.psum_tensor(name, shape, dt))

    def sem(self, name):
        return self.ctx.enter_context(self.nc.semaphore(name))


def row_of(t, n=1):
    return bass.ds(t, n)


def settle(eng):
    eng.nop(nofuse=True)


def later(t):
    return not (isinstance(t, int) and t < 2)


def tiles(eng, *stages):

    def step(t, s):
        for body, lag in stages:
            if isinstance(t, int) and not 0 <= t - lag < NT:
                continue
            body(t - lag, (s + lag) % 2)

    for t in range(5):
        step(t, t % 2)
    with eng.Fori(0, (NT - 5) // 2) as k:
        for u in (0, 1):
            step(k * 2 + (5 + u), (5 + u) % 2)
    for t in range(NT, NT + max(lag for _, lag in stages)):
        step(t, t % 2)


def phase_nodes(nc, io, scr):
    with ExitStack() as ctx:
        kit = Kit(nc, ctx)
        sb, ps, sem = kit.sb, kit.ps, kit.sem
        wcat = sb("wcat", [P, KD, D + 2 * HT])
        wqkv = sb("wqkv", [P, KD, 3 * D])
        wnT = sb("wnT", [P, KD, D])
        wout = sb("wout", [P, KD, D])
        bd = sb("bd", [P, KD, 2 * HT])
        gamma = sb("gamma", [P, D])
        ident = sb("ident", [P, P])
        eps = sb("eps", [P, 1])
        xin = sb("xin", [P, 2, D])
        st = sb("st", [P, 2, 6])
        mv = sb("mv", [P, 2, 2])
        rstd = sb("rstd", [P, 2, 1])
        xn = sb("xn", [P, 2, D])
        xnT = sb("xnT", [P, 2, KD, P])
        trow = sb("trow", [P, 2, D + 2 * HT])
        er3 = sb("er3", [P, 2, 3 * HT], BF16)
        er_a = sb("er_a", [P, 2, HT])
        er_b = sb("er_b", [P, 2, HT])
        ktile = sb("ktile", [P, NT, D])
        vtile = sb("vtile", [P, NT, D])
        qtile = sb("qtile", [P, NT, D])
        real = sb("real", [P, NT])
        kmax = sb("kmax", [P, D])
        kmaxb = sb("kmaxb", [P, D])
        kexp = sb("kexp", [P, 2, D])
        ctx_sb = sb("ctx_sb", [P, KD, P])
        ctxT = sb("ctxT", [P, KD, P])
        rsum = sb("rsum", [P, KD])
        mixw = sb("mixw", [P, KD, D])
        qmax = sb("qmax", [P, 2, H])
        qsm = sb("qsm", [P, 2, D])
        qsum = sb("qsum", [P, 2, H])
        qrs = sb("qrs", [P, NT, H])
        qT = sb("qT", [P, 2, KD, P])
        xre = sb("xre", [P, 2, D])
        mixo = sb("mixo", [P, 2, D])
        mixf = sb("mixf", [P, 2, D])

        ps_tr = [ps(f"ps_tr{i}", [P, KD, P]) for i in range(2)]
        ps_ft = [ps(f"ps_ft{i}", [P, 512]) for i in range(2)]
        ps_qk = [ps(f"ps_qk{i}", [P, 512]) for i in range(2)]
        ps_v = [ps(f"ps_v{i}", [P, 512]) for i in range(2)]

        weights_in = sem("n_weights_in")
        blocks_in = sem("n_blocks_in")
        zeroed = sem("n_zeroed")
        ident_ok = sem("n_ident_ok")
        pool_step = sem("n_pool_step")
        eps_ok = sem("n_eps_ok")
        attn_w = sem("n_attn_w")
        attn_wc = sem("n_attn_wc")
        x_in = [sem(f"n_x_in{i}") for i in range(2)]
        stats = sem("n_stats")
        var_ok = sem("n_var_ok")
        std = sem("n_std")
        rstd_ok = sem("n_rstd_ok")
        xn_ok = sem("n_xn_ok")
        xnT_ps = sem("n_xnT_ps")
        xnT_ok = sem("n_xnT_ok")
        proj = sem("n_proj")
        trow_ok = sem("n_trow_ok")
        kept = sem("n_kept")
        er_hi = sem("n_er_hi")
        er_r1 = sem("n_er_r1")
        er_mid = sem("n_er_mid")
        er_r2 = sem("n_er_r2")
        er_ok = sem("n_er_ok")
        table_out = [sem(f"n_table_out{i}") for i in range(2)]
        kmax_ok = sem("n_kmax_ok")
        kmaxb_ok = sem("n_kmaxb_ok")
        ksub = sem("n_ksub")
        kexp_ok = sem("n_kexp_ok")
        ctx_mm = sem("n_ctx_mm")
        ctx_z = sem("n_ctx_z")
        ctx_c = sem("n_ctx_c")
        ctxT_ps = sem("n_ctxT_ps")
        ctxT_ok = sem("n_ctxT_ok")
        mix_mm = sem("n_mix_mm")
        mixw_ok = sem("n_mixw_ok")
        rsum_ok = sem("n_rsum_ok")
        qmax_ok = sem("n_qmax_ok")
        qsub = sem("n_qsub")
        qexp = sem("n_qexp")
        qsum_ok = sem("n_qsum_ok")
        qrec = sem("n_qrec")
        qsm_ok = sem("n_qsm_ok")
        qT_ps = sem("n_qT_ps")
        qT_ok = sem("n_qT_ok")
        out_mm = sem("n_out_mm")
        xre_in = [sem(f"n_xre_in{i}") for i in range(2)]
        ln_st = sem("n_ln_st")
        ln_var = sem("n_ln_var")
        ln_std = sem("n_ln_std")
        ln_rstd = sem("n_ln_rstd")
        ln_n = sem("n_ln_n")
        mixf_ok = sem("n_mixf_ok")
        mix_out = [sem(f"n_mix_out{i}") for i in range(2)]

        block = ctx.enter_context(nc.Block())

        @block.sync
        def _(sp):
            loads = [
                (wcat[:, :, 0:D], io["W_n"].rearrange("(c p) n -> p c n", p=P)),
                (wnT[:, :, :], io["W_nT"].rearrange("(c p) n -> p c n", p=P)),
                (wqkv[:, :, :], io["Wqkv"].rearrange("(c p) n -> p c n", p=P)),
                (wout[:, :, :], io["Wout"].rearrange("(c p) n -> p c n", p=P)),
                (gamma[:, :], io["gamma"].rearrange("(a n) -> a n", a=1).broadcast_to([P, D])),
            ]
            for dst, src in loads:
                sp.dma_start(dst, src).then_inc(weights_in, 16)
            sp.wait_ge(zeroed, 1)
            for h in range(H):
                rows = slice(DH * (h % 4), DH * (h % 4) + DH)
                for side, name in enumerate(("attn_l", "attn_r")):
                    sp.dma_start(bd[rows, h // 4, HT * side + T * h:HT * side + T * h + T],
                                 io[name][h]).then_inc(blocks_in, 16)

            def load_x(t, s):
                if later(t):
                    sp.wait_ge(xn_ok, t - 1)
                sp.dma_start(xin[:, s, :], io["x"][row_of(t), :, :].rearrange("a p n -> (a p) n")) \
                    .then_inc(x_in[s], 16)

            tiles(sp, (load_x, 0))

            def reload(t, s):
                if later(t):
                    sp.wait_ge(mixf_ok, t - 1)
                sp.dma_start(xre[:, s, :], io["x"][row_of(t), :, :].rearrange("a p n -> (a p) n")) \
                    .then_inc(xre_in[s], 16)

            tiles(sp, (reload, 0))

        @block.gpsimd
        def _(pool):
            pool.memset(bd[:, :, :], 0.0).then_inc(zeroed, 1)
            pool.memset(ident[:, :], 0.0).then_inc(pool_step, 1)
            pool.memset(real[:, :], 1.0).then_inc(pool_step, 1)
            pool.memset(eps[:, :], LN_EPS).then_inc(eps_ok, 1)
            pool.wait_ge(pool_step, 2)
            pool.affine_select(out=ident[:, :], in_=ident[:, :], compare_op=ALU.not_equal, fill=1.0,
                               base=0, pattern=[[-1, P]], channel_multiplier=1).then_inc(ident_ok, 1)
            pool.affine_select(out=real[:, NT - 1:NT], in_=real[:, NT - 1:NT], compare_op=ALU.is_ge,
                               fill=0.0, base=LAST - 1, pattern=[[0, 1]],
                               channel_multiplier=-1).then_inc(ident_ok, 1)

            def store_table(t, s):
                pool.wait_ge(trow_ok, t + 1)
                pool.wait_ge(er_ok, t + 1)
                pool.wait_ge(ident_ok, 2)
                pool.dma_start(scr["table"][row_of(t), :, :].rearrange("a p n -> (a p) n"),
                               trow[:, s, 0:ROW]).then_inc(table_out[s], 16)
                pool.dma_start(scr["er"][row_of(t), :, :].rearrange("a p n -> (a p) n"),
                               er3[:, s, :]).then_inc(table_out[s], 16)

            tiles(pool, (store_table, 0))
            pool.wait_ge(kmax_ok, NT)
            pool.partition_all_reduce(kmaxb[:, :], kmax[:, :], P, RMAX).then_inc(kmaxb_ok, 1)

            def store_mix(t, s):
                pool.wait_ge(mixf_ok, t + 1)
                pool.wait_ge(ident_ok, 2)
                pool.dma_start(scr["xmix"][row_of(t), :, :].rearrange("a p n -> (a p) n"),
                               mixf[:, s, :]).then_inc(mix_out[s], 16)

            tiles(pool, (store_mix, 0))
            pool.wait_ge(table_out[0], 32 * ((NT + 1) // 2))
            pool.wait_ge(table_out[1], 32 * (NT // 2))
            pool.wait_ge(mix_out[0], 16 * ((NT + 1) // 2))
            pool.wait_ge(mix_out[1], 16 * (NT // 2))

        @block.scalar
        def _(act):
            act.wait_ge(attn_w, 1)
            for k in range(KD):
                act.copy(wcat[:, k, D:D + 2 * HT], ps_ft[k][:, 0:2 * HT]).then_inc(attn_wc, 1)
            act.wait_ge(eps_ok, 1)

            def spread(t, s):
                act.wait_ge(var_ok, t + 1)
                act.activation(rstd[:, s, :], mv[:, s, 1:2], ACT.Sqrt, bias=eps[:, 0:1]).then_inc(std, 1)

            def turn(t, s):
                act.wait_ge(xnT_ps, t + 1)
                if later(t):
                    act.wait_ge(proj, t - 1)
                act.copy(xnT[:, s, :, :], ps_tr[s][:, :, :]).then_inc(xnT_ok, 1)

            def keep(t, s):
                act.wait_ge(proj, t + 1)
                if later(t):
                    act.wait_ge(er_ok, t - 1)
                    act.wait_ge(table_out[s], (t - s) * 16)
                act.copy(trow[:, s, :], ps_ft[s][:, 0:D + 2 * HT]).then_inc(trow_ok, 1)
                act.copy(qtile[:, row_of(t), :].rearrange("p a n -> p (a n)"),
                         ps_qk[s][:, 0:D]).then_inc(kept, 1)
                act.copy(ktile[:, row_of(t), :].rearrange("p a n -> p (a n)"),
                         ps_qk[s][:, D:2 * D]).then_inc(kept, 1)
                act.copy(vtile[:, row_of(t), :].rearrange("p a n -> p (a n)"),
                         ps_v[s][:, 0:D]).then_inc(kept, 1)

            tiles(act, (spread, 0), (turn, 1), (keep, 2))

            def exp_kq(t, s):
                act.wait_ge(ksub, t + 1)
                act.activation(kexp[:, s, :], kexp[:, s, :], ACT.Exp).then_inc(kexp_ok, 1)
                q = qtile[:, row_of(t), :].rearrange("p a n -> p (a n)")
                act.wait_ge(qsub, t + 1)
                act.activation(q, q, ACT.Exp).then_inc(qexp, 1)

            tiles(act, (exp_kq, 0))

            def turn_q(t, s):
                act.wait_ge(qT_ps, t + 1)
                if later(t):
                    act.wait_ge(out_mm, t - 1)
                act.copy(qT[:, s, :, :], ps_tr[s][:, :, :]).then_inc(qT_ok, 1)

            def deviate(t, s):
                act.wait_ge(ln_var, t + 1)
                act.activation(rstd[:, s, :], mv[:, s, 1:2], ACT.Sqrt, bias=eps[:, 0:1]).then_inc(ln_std, 1)

            tiles(act, (turn_q, 0), (deviate, 2))

        @block.vector
        def _(dve):
            def measure(t, s):
                dve.wait_ge(x_in[s], (t - s) * 8 + 16)
                dve.bn_stats(st[:, s, :], xin[:, s, :]).then_inc(stats, 1)
                dve.wait_ge(stats, t + 1)
                settle(dve)
                dve.bn_aggr(mv[:, s, :], st[:, s, :]).then_inc(var_ok, 1)

            def norm(t, s):
                dve.wait_ge(std, t + 1)
                dve.reciprocal(rstd[:, s, :], rstd[:, s, :]).then_inc(rstd_ok, 1)
                dve.wait_ge(rstd_ok, t + 1)
                if later(t):
                    dve.wait_ge(xnT_ps, t - 1)
                dve.tensor_scalar(xn[:, s, :], xin[:, s, :], mv[:, s, 0:1], rstd[:, s, 0:1],
                                  ALU.subtract, ALU.mult).then_inc(xn_ok, 1)

            def split(t, s):
                dve.wait_ge(trow_ok, t + 1)
                if later(t):
                    dve.wait_ge(table_out[s], (t - s) * 16)
                er = trow[:, s, ROW:ROW + HT]
                dve.tensor_copy(er3[:, s, 0:HT], er).then_inc(er_hi, 1)
                dve.wait_ge(er_hi, t + 1)
                dve.tensor_tensor(er_a[:, s, :], er, er3[:, s, 0:HT], ALU.subtract).then_inc(er_r1, 1)
                dve.wait_ge(er_r1, t + 1)
                dve.tensor_copy(er3[:, s, HT:2 * HT], er_a[:, s, :]).then_inc(er_mid, 1)
                dve.wait_ge(er_mid, t + 1)
                dve.tensor_tensor(er_b[:, s, :], er_a[:, s, :], er3[:, s, HT:2 * HT],
                                  ALU.subtract).then_inc(er_r2, 1)
                dve.wait_ge(er_r2, t + 1)
                dve.tensor_copy(er3[:, s, 2 * HT:3 * HT], er_b[:, s, :]).then_inc(er_ok, 1)
                kk = ktile[:, row_of(t), :].rearrange("p a n -> p (a n)")
                dve.wait_ge(kept, t * 3 + 2)
                if isinstance(t, int) and t == 0:
                    dve.tensor_copy(kmax[:, :], kk).then_inc(kmax_ok, 1)
                else:
                    dve.wait_ge(kmax_ok, t)
                    dve.tensor_tensor(kmax[:, :], kmax[:, :], kk, ALU.max).then_inc(kmax_ok, 1)

            tiles(dve, (measure, 0), (norm, 1), (split, 3))
            dve.wait_ge(kmaxb_ok, 1)

            def shift(t, s):
                dve.wait_ge(kept, 3 * NT)
                if later(t):
                    dve.wait_ge(ctx_mm, t - 1)
                dve.tensor_tensor(kexp[:, s, :], ktile[:, row_of(t), :].rearrange("p a n -> p (a n)"),
                                  kmaxb[:, :], ALU.subtract).then_inc(ksub, 1)
                q = qtile[:, row_of(t), :].rearrange("p a (h d) -> p (a h) d", h=H)
                dve.tensor_reduce(qmax[:, s, :], q, AX_X, ALU.max).then_inc(qmax_ok, 1)
                dve.wait_ge(qmax_ok, t + 1)
                dve.tensor_tensor(q, q, qmax[:, s, :].unsqueeze(2).broadcast_to([P, H, DH]),
                                  ALU.subtract).then_inc(qsub, 1)

            def sum_q(t, s):
                dve.wait_ge(qexp, t + 1)
                settle(dve)
                dve.tensor_reduce(qsum[:, s, :], qtile[:, row_of(t), :].rearrange("p a (h d) -> p (a h) d", h=H),
                                  AX_X, ALU.add).then_inc(qsum_ok, 1)
                dve.wait_ge(qsum_ok, t + 1)
                dve.reciprocal(qrs[:, row_of(t), :].rearrange("p a h -> p (a h)"), qsum[:, s, :]).then_inc(qrec, 1)

            tiles(dve, (shift, 0), (sum_q, 1))

            dve.memset(ctx_sb[:, :, :], 0.0).then_inc(ctx_z, 1)
            dve.wait_ge(ctx_mm, NT)
            dve.wait_ge(ctx_z, 1)
            for c in range(KD):
                for j in range(4):
                    r = slice(DH * j, DH * j + DH)
                    dve.tensor_copy(ctx_sb[r, c, DH * j:DH * j + DH],
                                    ps_ft[c][r, P * c + DH * j:P * c + DH * j + DH]).then_inc(ctx_c, 1)
                dve.reciprocal(rsum[:, c:c + 1], ps_ft[c][:, D:D + 1]).then_inc(rsum_ok, 1)
            dve.wait_ge(ctxT_ps, 1)
            dve.tensor_copy(ctxT[:, :, :], ps_tr[0][:, :, :]).then_inc(ctxT_ok, 1)
            dve.wait_ge(mix_mm, 1)
            dve.wait_ge(rsum_ok, 2)
            for c in range(KD):
                dve.tensor_scalar(mixw[:, c, :], ps_qk[c][:, 0:D], rsum[:, c:c + 1], SCALE,
                                  ALU.mult, ALU.mult).then_inc(mixw_ok, 1)

            def soften(t, s):
                dve.wait_ge(qrec, NT)
                if later(t):
                    dve.wait_ge(qT_ps, t - 1)
                dve.tensor_tensor(qsm[:, s, :].rearrange("p (h d) -> p h d", h=H),
                                  qtile[:, row_of(t), :].rearrange("p a (h d) -> p (a h) d", h=H),
                                  qrs[:, row_of(t), :].rearrange("p a h -> p (a h)").unsqueeze(2)
                                  .broadcast_to([P, H, DH]), ALU.mult).then_inc(qsm_ok, 1)

            def measure_out(t, s):
                dve.wait_ge(out_mm, t + 1)
                dve.bn_stats(st[:, s, :], ps_v[s][:, 0:D]).then_inc(ln_st, 1)
                dve.wait_ge(ln_st, t + 1)
                settle(dve)
                dve.bn_aggr(mv[:, s, :], st[:, s, :]).then_inc(ln_var, 1)

            def finish(t, s):
                dve.wait_ge(ln_var, t + 1)
                dve.scalar_tensor_tensor(mixo[:, s, :], ps_v[s][:, 0:D], mv[:, s, 0:1], gamma[:, :],
                                         ALU.subtract, ALU.mult).then_inc(ln_n, 1)
                dve.wait_ge(ln_std, t + 1)
                dve.reciprocal(rstd[:, s, :], rstd[:, s, :]).then_inc(ln_rstd, 1)
                dve.wait_ge(ln_rstd, t + 1)
                dve.wait_ge(ln_n, t + 1)
                if later(t):
                    dve.wait_ge(mix_out[s], (t - s) * 8)
                dve.wait_ge(xre_in[s], (t - s) * 8 + 16)
                dve.scalar_tensor_tensor(mixf[:, s, :], mixo[:, s, :], rstd[:, s, 0:1], xre[:, s, :],
                                         ALU.mult, ALU.add).then_inc(mixf_ok, 1)

            tiles(dve, (soften, 0), (finish, 3), (measure_out, 2))

        @block.tensor
        def _(pe):
            pe.wait_ge(weights_in, 16 * 5)
            pe.wait_ge(blocks_in, 16 * 2 * H)
            for k in range(KD):
                for c in range(KD):
                    last = pe.matmul(ps_ft[k][:, 0:2 * HT], wnT[:, c, k * P:k * P + P], bd[:, c, :],
                                     start=(c == 0), stop=(c == KD - 1))
            last.then_inc(attn_w, 1)
            pe.wait_ge(attn_wc, KD)
            pe.wait_ge(ident_ok, 2)

            def turn(t, s):
                pe.wait_ge(xn_ok, t + 1)
                if later(t):
                    pe.wait_ge(xnT_ok, t - 1)
                for k in range(KD):
                    last = pe.transpose(ps_tr[s][:, k, :], xn[:, s, k * P:k * P + P], ident[:, :])
                last.then_inc(xnT_ps, 1)

            def project(t, s):
                pe.wait_ge(xnT_ok, t + 1)
                if later(t):
                    pe.wait_ge(kept, (t - 1) * 3)
                for k in range(KD):
                    pe.matmul(ps_ft[s][:, 0:D + 2 * HT], xnT[:, s, k, :], wcat[:, k, :],
                              start=(k == 0), stop=(k == KD - 1))
                for k in range(KD):
                    pe.matmul(ps_qk[s][:, :], xnT[:, s, k, :], wqkv[:, k, 0:2 * D],
                              start=(k == 0), stop=(k == KD - 1))
                for k in range(KD):
                    last = pe.matmul(ps_v[s][:, 0:D], xnT[:, s, k, :], wqkv[:, k, 2 * D:3 * D],
                                     start=(k == 0), stop=(k == KD - 1))
                last.then_inc(proj, 1)

            tiles(pe, (turn, 0), (project, 1))
            pe.wait_ge(kept, 3 * NT)
            pe.wait_ge(kmax_ok, NT)
            pe.wait_ge(trow_ok, NT)

            def context(t, s, start, stop):
                pe.wait_ge(kexp_ok, t + 1)
                for c in range(KD):
                    pe.matmul(ps_ft[c][:, 0:D], kexp[:, s, c * P:c * P + P],
                              vtile[:, row_of(t), :].rearrange("p a n -> p (a n)"),
                              start=start, stop=stop, skip_group_check=True)
                for c in range(KD):
                    last = pe.matmul(ps_ft[c][:, D:D + 1], kexp[:, s, c * P:c * P + P],
                                     real[:, row_of(t)], start=False, stop=stop, skip_group_check=True)
                last.then_inc(ctx_mm, 1)

            context(0, 0, True, False)
            with pe.Fori(0, (NT - 3) // 2) as k:
                for u in (0, 1):
                    context(k * 2 + (1 + u), (1 + u) % 2, False, False)
            context(NT - 2, 1, False, False)
            context(NT - 1, 0, False, True)

            pe.wait_ge(ctx_c, 2 * 4)
            for c in range(KD):
                last = pe.transpose(ps_tr[0][:, c, :], ctx_sb[:, c, :], ident[:, :])
            last.then_inc(ctxT_ps, 1)
            pe.wait_ge(ctxT_ok, 1)
            for c in range(KD):
                last = pe.matmul(ps_qk[c][:, 0:D], ctxT[:, c, :], wout[:, c, :], start=True, stop=True)
            last.then_inc(mix_mm, 1)
            pe.wait_ge(mixw_ok, KD)

            def turn_q(t, s):
                pe.wait_ge(qsm_ok, t + 1)
                if later(t):
                    pe.wait_ge(qT_ok, t - 1)
                for k in range(KD):
                    last = pe.transpose(ps_tr[s][:, k, :], qsm[:, s, k * P:k * P + P], ident[:, :])
                last.then_inc(qT_ps, 1)

            def attend(t, s):
                pe.wait_ge(qT_ok, t + 1)
                if later(t):
                    pe.wait_ge(ln_n, t - 1)
                for k in range(KD):
                    last = pe.matmul(ps_v[s][:, 0:D], qT[:, s, k, :], mixw[:, k, :],
                                     start=(k == 0), stop=(k == KD - 1))
                last.then_inc(out_mm, 1)

            tiles(pe, (turn_q, 0), (attend, 1))


def phase_edge_tables(nc, io, scr):
    with ExitStack() as ctx:
        kit = Kit(nc, ctx)
        sb, sem = kit.sb, kit.sem
        d_em = sb("d_em", [P, EL], I32)
        dn_em = sb("dn_em", [P, EL], I32)
        d_lin = sb("d_lin", [P, EL], I32)
        dp_lin = sb("dp_lin", [P, EL], I32)
        dm = sb("dm", [P, EL])
        d16 = sb("d16", [P, EL], U16)
        same = sb("same", [P, EL])
        pen = sb("pen", [P, EL], BF16)
        gf = sb("gf", [P, G - 1], I32)
        gt = sb("gt", [P, G - 1], I32)
        gidx = sb("gidx", [P, G - 1], I32)
        gb = sb("gb", [P, G - 1])
        vcol = sb("vcol", [P, VK], I32)
        vf = sb("vf", [P, VK])
        cmp = sb("cmp", [P, VK, G - 1])
        gt_f = sb("gt_f", [P, 2, VK])
        gt_i = sb("gt_i", [P, 2, VK], I32)
        loaded = sem("e_loaded")
        iotas = sem("e_iotas")
        step = sem("e_step")
        dm_ok = sem("e_dm_ok")
        d16_ok = sem("e_d16_ok")
        pen_ok = sem("e_pen_ok")
        visits_ok = sem("e_visits_ok")
        stored = sem("e_stored")
        block = ctx.enter_context(nc.Block())

        @block.sync
        def _(sp):
            for dst, name in ((d_em, "dst_em"), (dn_em, "dst_next_em"), (d_lin, "dst_lin"), (dp_lin, "dst_prev_lin")):
                sp.dma_start(dst[:, :], io[name].rearrange("(p n) -> p n", p=P)).then_inc(loaded, 16)
            sp.dma_start(gf[:, :], io["group_first"].rearrange("(a n) -> a n", a=1).broadcast_to([P, G - 1])) \
                .then_inc(loaded, 16)
            sp.wait_ge(dm_ok, 1)
            sp.dma_start(scr["dm"].rearrange("g p c -> (g p c)").rearrange("(q n) -> q n", q=P),
                         dm[:, :]).then_inc(stored, 16)
            sp.wait_ge(d16_ok, 1)
            sp.dma_start(scr["dst16"].rearrange("(p n) -> p n", p=P), d16[:, :]).then_inc(stored, 16)
            sp.wait_ge(pen_ok, 1)
            sp.dma_start(scr["pen"][0:EP].rearrange("(p n) -> p n", p=P), pen[:, :]).then_inc(stored, 16)
            sp.dma_start(scr["pen"][EP:EP + 1].rearrange("(p n) -> p n", p=1), pen[0:1, 0:1]).then_inc(stored, 16)
            sp.wait_ge(visits_ok, 1)
            for k in range(VK):
                sp.dma_start(scr["visit_group"][k * P:(k + 1) * P].rearrange("(p a) -> p a", a=1),
                             gt_i[:, 0, k:k + 1]).then_inc(stored, 16)
                sp.dma_start(scr["visit_tile"][k * P:(k + 1) * P].rearrange("(p a) -> p a", a=1),
                             gt_i[:, 1, k:k + 1]).then_inc(stored, 16)
                sp.dma_start(scr["visit_tile_f"][k * P:(k + 1) * P].rearrange("(p a) -> p a", a=1),
                             gt_f[:, 1, k:k + 1]).then_inc(stored, 16)
            sp.wait_ge(stored, 16 * (4 + 3 * VK))

        @block.gpsimd
        def _(pool):
            pool.iota(gidx[:, :], pattern=[[1, G - 1]], base=1, channel_multiplier=0).then_inc(iotas, 1)
            pool.iota(vcol[:, :], pattern=[[P, VK]], base=0, channel_multiplier=1).then_inc(iotas, 1)

        @block.vector
        def _(dve):
            dve.wait_ge(loaded, 16 * 5)
            dve.tensor_tensor(dm[:, :], d_em[:, :], dn_em[:, :], ALU.not_equal).then_inc(dm_ok, 1)
            dve.tensor_copy(d16[:, :], d_lin[:, :]).then_inc(d16_ok, 1)
            dve.tensor_tensor(same[:, :], d_lin[:, :], dp_lin[:, :], ALU.not_equal).then_inc(step, 1)
            dve.wait_ge(step, 1)
            dve.tensor_scalar(pen[:, :], same[:, :], NEG, None, ALU.mult).then_inc(pen_ok, 1)
            dve.tensor_single_scalar(gt[:, :], gf[:, :], 7, ALU.arith_shift_right).then_inc(step, 1)
            dve.wait_ge(iotas, 2)
            dve.wait_ge(step, 2)
            dve.tensor_tensor(gb[:, :], gt[:, :], gidx[:, :], ALU.add).then_inc(step, 1)
            dve.tensor_copy(vf[:, :], vcol[:, :]).then_inc(step, 1)
            dve.wait_ge(step, 4)
            for k in range(VK):
                dve.tensor_scalar(cmp[:, k, :], gb[:, :], vf[:, k:k + 1], None, ALU.is_le).then_inc(step, 1)
            dve.wait_ge(step, 4 + VK)
            dve.tensor_reduce(gt_f[:, 0, :], cmp[:, :, :], AX_X, ALU.add).then_inc(step, 1)
            dve.wait_ge(step, 5 + VK)
            dve.tensor_tensor(gt_f[:, 1, :], vf[:, :], gt_f[:, 0, :], ALU.subtract).then_inc(step, 1)
            dve.wait_ge(step, 6 + VK)
            dve.tensor_copy(gt_i[:, :, :], gt_f[:, :, :]).then_inc(visits_ok, 1)


def phase_edges(nc, io, scr):
    with ExitStack() as ctx:
        kit = Kit(nc, ctx)
        sb, ps, sem = kit.sb, kit.ps, kit.sem
        vg = sb("vg", [1, VP], I32)
        vt = sb("vt", [1, VP], I32)
        tvb = sb("tvb", [P, VP + 1])
        tbase = sb("tbase", [P, VP])
        nodeid = sb("nodeid", [P, VP])
        fresh = sb("fresh", [P, VP])
        pcol_i = sb("pcol_i", [P, 1], I32)
        pcol = sb("pcol", [P, 1])
        ident = sb("ident2", [P, P])
        bdm = sb("bdm", [C * F, C * HT])
        idx = sb("idx", [P, SLOTS, C], I32)
        a4 = sb("a4", [P, SLOTS, C * T])
        a16 = sb("a16", [C * F, SLOTS, P])
        dme = sb("dme", [P, SLOTS, C])
        d16r = sb("d16r", [P, SLOTS, GE], U16)
        penr = sb("penr", [H, SLOTS, GE + 1], BF16)
        er3 = sb("er3e", [P, SLOTS, 3 * HT], BF16)
        gat = sb("gat", [P, SLOTS, C, ROW])
        ohT = sb("ohT", [P, 2, GE], BF16)
        identb = sb("identb", [P, P], BF16)
        oh = sb("oh", [P, SLOTS, C, P])
        zm = sb("zm", [P, 2, C * HT])
        lg = sb("lg", [P, 2, C * H])
        e = sb("e", [P, 2, C * H])
        runf = sb("runf", [H, 2, GE])
        runm = sb("runm", [H, 2, GE])
        dlt = sb("dlt", [P, 2, C * H])
        msg = sb("msg", [P, 2, C, SUMS])
        acc = sb("acc", [P, 2, SUMS])
        absn = sb("absn", [P, 2, H])
        mm = sb("mm", [P, 2, 2, H])
        dd = sb("dd", [P, 2, 2, H])
        sc = sb("sc", [P, 2, 2, H])
        tmp = sb("tmp", [P, 2, H * HW])

        ps_z = [ps(f"ps_z{i}", [P, 512]) for i in range(2)]
        ps_e = ps("ps_e", [P, 1024])
        ps_m = ps("ps_m", [P, 512])
        ps_o = ps("ps_o", [P, C, P], BF16)
        ps_s = [ps(f"ps_s{i}", [P, 512]) for i in range(2)]

        tables_in = sem("g_tables_in")
        blocks_in = sem("g_blocks_in")
        pool_step = sem("g_pool_step")
        zeroed = sem("g_zeroed")
        pool_ok = sem("g_pool_ok")
        setup = sem("g_setup")
        setup_ok = sem("g_setup_ok")
        in_ = [sem(f"g_in{i}") for i in range(SLOTS)]
        gathered = [sem(f"g_gathered{i}") for i in range(SLOTS)]
        ohT_ok = sem("g_ohT_ok")
        oh_ps = sem("g_oh_ps")
        oh_ok = sem("g_oh_ok")
        z_mm = sem("g_z_mm")
        zm_ok = sem("g_zm_ok")
        lg_ok = sem("g_lg_ok")
        e_ok = sem("g_e_ok")
        eT_ps = sem("g_eT_ps")
        runf_ok = sem("g_runf_ok")
        runm_ok = sem("g_runm_ok")
        m_ps = sem("g_m_ps")
        dlt_ok = sem("g_dlt_ok")
        mend_ok = sem("g_mend_ok")
        p_ok = sem("g_p_ok")
        msg_ok = sem("g_msg_ok")
        sums = sem("g_sums")
        small = sem("g_small")
        dd_ok = sem("g_dd_ok")
        sc_ok = sem("g_sc_ok")
        max_ok = sem("g_max_ok")
        scaled = sem("g_scaled")
        acc_ok = sem("g_acc_ok")
        acc_out = [sem(f"g_acc_out{i}") for i in range(2)]
        LOADS = 7

        block = ctx.enter_context(nc.Block())

        def visits(eng, step):
            for v in range(FIRST):
                step(v, v % SLOTS)
            with eng.Fori(0, (V - FIRST) // SLOTS - 1) as k:
                for u in range(SLOTS):
                    step(k * SLOTS + (FIRST + u), (FIRST + u) % SLOTS)
            for v in range(V - SLOTS, V):
                step(v, v % SLOTS)

        @block.sync
        def _(sp):
            sp.dma_start(vg[:, :], scr["visit_group"].rearrange("(a n) -> a n", a=1)).then_inc(tables_in, 16)
            sp.dma_start(vt[:, :], scr["visit_tile"].rearrange("(a n) -> a n", a=1)).then_inc(tables_in, 16)
            sp.dma_start(tvb[:, 1:VP + 1], scr["visit_tile_f"].rearrange("(a n) -> a n", a=1)
                         .broadcast_to([P, VP])).then_inc(tables_in, 16)
            sp.wait_ge(zeroed, 1)
            for c in range(C):
                sp.dma_start(bdm[F * c:F * c + F, HT * c:HT * c + HT].rearrange("f (h t) -> f h t", h=H),
                             io["attn_m"].rearrange("h f t -> f h t")).then_inc(blocks_in, 16)
            sp.wait_ge(tables_in, 48)

            def loads(g, t, s, before):
                before()
                sp.dma_start(idx[:, s, :], io["src"][row_of(g), :, :].rearrange("a p c -> (a p) c")).then_inc(in_[s], 16)
                sp.dma_start(a4[:, s, :], io["a4"][row_of(g), :, :].rearrange("a p c -> (a p) c")).then_inc(in_[s], 16)
                sp.dma_start(a16[:, s, :], io["a16"][row_of(g), :, :].rearrange("a p c -> (a p) c")).then_inc(in_[s], 16)
                sp.dma_start(dme[:, s, :], scr["dm"][row_of(g), :, :].rearrange("a p c -> (a p) c")).then_inc(in_[s], 16)
                sp.dma_start(d16r[:, s, :], scr["dst16"].rearrange("(g n) -> g n", n=GE)[row_of(g), :]
                             .broadcast_to([P, GE])).then_inc(in_[s], 16)
                sp.dma_start(penr[:, s, :], scr["pen"][row_of(g * GE, GE + 1)].rearrange("(a n) -> a n", a=1)
                             .broadcast_to([H, GE + 1])).then_inc(in_[s], 16)
                sp.dma_start(er3[:, s, :], scr["er"][row_of(t), :, :].rearrange("a p c -> (a p) c")).then_inc(in_[s], 16)

            def store(t, v, before):
                before()
                sp.dma_start(scr["acc"][row_of(t), :, :].rearrange("a p c -> (a p) c"),
                             acc[:, v, :]).then_inc(acc_out[v], 16)

            def of_visit(table, v, most):
                return sp.value_load(table[0:1, row_of(v)], min_val=0, max_val=most)

            for v in range(SLOTS):
                loads(of_visit(vg, v, G - 1), of_visit(vt, v, NT - 1), v, lambda: None)

            def step(v, s):
                g = of_visit(vg, v + SLOTS, G - 1)
                t = of_visit(vt, v + SLOTS, NT - 1)
                storing = not (isinstance(v, int) and v < 2)
                if storing:
                    t_before = of_visit(vt, v - 2, NT - 1)

                def slot_free():
                    sp.wait_ge(msg_ok, v + 1)
                    sp.wait_ge(z_mm, v + 1)
                    settle(sp)

                def summed():
                    sp.wait_ge(acc_ok, v - 1)
                    settle(sp)
                    if not (isinstance(v, int) and v == 2):
                        sp.wait_ge(acc_out[(s + 1) % 2], (v - 2 + (0 if s % 2 == 0 else 1)) * 8)
                    settle(sp)

                if storing:
                    store(t_before, s % 2, summed)
                loads(g, t, s, slot_free)

            for v in range(FIRST):
                step(v, v % SLOTS)
            with sp.Fori(0, (V - FIRST) // SLOTS - 1) as k:
                for u in range(SLOTS):
                    step(k * SLOTS + (FIRST + u), (FIRST + u) % SLOTS)
            for v in range(V - SLOTS - 2, V):
                t_now = of_visit(vt, v, NT - 1)
                sp.wait_ge(acc_ok, v + 1)
                sp.wait_ge(acc_out[(v + 1) % 2], 16 * ((v + 1) // 2))
                sp.dma_start(scr["acc"][row_of(t_now), :, :].rearrange("a p c -> (a p) c"),
                             acc[:, v % 2, :]).then_inc(acc_out[v % 2], 16)
            sp.wait_ge(acc_out[0], 16 * (V // 2))
            sp.wait_ge(acc_out[1], 16 * (V // 2))

        @block.gpsimd
        def _(pool):
            pool.memset(bdm[:, :], 0.0).then_inc(zeroed, 1)
            pool.memset(ident[:, :], 0.0).then_inc(pool_step, 1)
            pool.iota(pcol_i[:, :], pattern=[[0, 1]], base=0, channel_multiplier=1).then_inc(pool_ok, 1)
            pool.wait_ge(pool_step, 1)
            pool.affine_select(out=ident[:, :], in_=ident[:, :], compare_op=ALU.not_equal, fill=1.0,
                               base=0, pattern=[[-1, P]], channel_multiplier=1).then_inc(pool_ok, 1)
            pool.wait_ge(pool_ok, 2)
            pool.tensor_copy(identb[:, :], ident[:, :]).then_inc(pool_ok, 1)

            def gather(v, s):
                pool.wait_ge(in_[s], (v - s) * (4 * LOADS) + 16 * LOADS)
                pool.wait_ge(pool_ok, 3)
                settle(pool)
                for c in range(C):
                    pool.indirect_dma_start(
                        out=gat[:, s, c, :], out_offset=None, in_=scr["table_rows"],
                        in_offset=bass.IndirectOffsetOnAxis(ap=idx[:, s, c:c + 1], axis=0),
                    ).then_inc(gathered[s], 16)

            visits(pool, gather)

        @block.scalar
        def _(act):
            def weights(v, s):
                b = s % 2
                act.wait_ge(dlt_ok, v + 1)
                act.activation(msg[:, b, :, 0:H * HW].rearrange("p c (h w) -> p c h w", w=HW)[:, :, :, DH],
                               dlt[:, b, :].rearrange("p (c h) -> p c h", h=H), ACT.Exp,
                               scale=THIRD).then_inc(p_ok, 1)

            def one_hot(v, s):
                act.wait_ge(oh_ps, v + 1)
                if not (isinstance(v, int) and v < SLOTS):
                    act.wait_ge(sums, v - (SLOTS - 1))
                act.copy(oh[:, s, :, :], ps_o[:, 0:C, :]).then_inc(oh_ok, 1)

            def rescale(v, s):
                b, o = s % 2, (s + 1) % 2
                act.wait_ge(dd_ok, v + 1)
                act.activation(sc[:, b, :, :], dd[:, b, :, :], ACT.Exp, scale=THIRD).then_inc(sc_ok, 1)
                act.wait_ge(sc_ok, v + 1)
                for h in range(H):
                    cols = slice(h * HW, h * HW + HW)
                    act.mul(tmp[:, b, cols], ps_s[b][:, cols], sc[:, b, 1, h:h + 1]).then_inc(scaled, 1)
                    act.mul(acc[:, b, cols], acc[:, o, cols], sc[:, b, 0, h:h + 1]).then_inc(scaled, 1)

            one_hot(0, 0)

            def step(v, s):
                if not (isinstance(v, int) and v == V - 1):
                    one_hot(v + 1, (s + 1) % SLOTS)
                if not (isinstance(v, int) and v < 2):
                    rescale(v - 2, (s - 2) % SLOTS)
                weights(v, s)

            visits(act, step)
            rescale(V - 2, (V - 2) % SLOTS)
            rescale(V - 1, (V - 1) % SLOTS)

        @block.vector
        def _(dve):
            dve.memset(acc[:, :, :], 0.0).then_inc(setup, 1)
            dve.memset(tvb[:, 0:1], -1.0).then_inc(setup, 1)
            dve.wait_ge(pool_ok, 3)
            dve.wait_ge(tables_in, 48)
            dve.tensor_copy(pcol[:, :], pcol_i[:, :]).then_inc(setup, 1)
            dve.tensor_scalar(tbase[:, :], tvb[:, 1:VP + 1], float(P), None, ALU.mult).then_inc(setup, 1)
            dve.wait_ge(setup, 4)
            dve.tensor_scalar(nodeid[:, :], tbase[:, :], pcol[:, 0:1], None, ALU.add).then_inc(setup, 1)
            dve.tensor_tensor(fresh[:, :], tvb[:, 1:VP + 1], tvb[:, 0:VP], ALU.not_equal).then_inc(setup, 1)
            dve.wait_ge(setup, 6)
            dve.tensor_scalar(fresh[:, :], fresh[:, :], 2.0 * NEG, None, ALU.mult).then_inc(setup_ok, 1)
            dve.wait_ge(setup_ok, 1)

            def select(v, s):
                b = s % 2
                dve.wait_ge(in_[s], (v - s) * (4 * LOADS) + 16 * LOADS)
                if not (isinstance(v, int) and v < 2):
                    dve.wait_ge(oh_ps, v - 1)
                dve.tensor_scalar(ohT[:, b, :], d16r[:, s, :], nodeid[:, row_of(v)], None,
                                  ALU.is_equal).then_inc(ohT_ok, 1)

            select(0, 0)
            select(1, 1)

            def step(v, s):
                number = isinstance(v, int)
                b, o = s % 2, (s + 1) % 2
                merging = not (number and v < 2)
                w, ps_w = v - 2, (s - 2) % SLOTS % 2
                assert ps_w == b
                mrg = ps_s[b][:, 0:H * HW].rearrange("p (h w) -> p h w", w=HW)

                dve.wait_ge(z_mm, v + 1)
                dve.tensor_tensor(
                    zm[:, b, :].rearrange("p (c h t) -> p c h t", c=C, h=H),
                    ps_z[b][:, 0:C * HT].rearrange("p (c h t) -> p c h t", c=C, h=H),
                    a4[:, s, :].rearrange("p (c t) -> p c t", c=C).unsqueeze(2).broadcast_to([P, C, H, T]),
                    ALU.mult).then_inc(zm_ok, 1)
                if merging:
                    dve.wait_ge(sums, w + 1)
                    dve.tensor_scalar(absn[:, b, :], mrg[:, :, DH], 0.5, NEG, ALU.is_lt,
                                      ALU.mult).then_inc(small, 1)
                    dve.tensor_scalar(mm[:, b, 0, :], acc[:, o, H * HW:SUMS], fresh[:, row_of(w)], None,
                                      ALU.add).then_inc(small, 1)
                dve.wait_ge(zm_ok, v + 1)
                dve.tensor_reduce(lg[:, b, :], zm[:, b, :].rearrange("p (q t) -> p q t", t=T),
                                  AX_X, ALU.add).then_inc(lg_ok, 1)
                if merging:
                    dve.wait_ge(small, w * 3 + 2)
                    dve.tensor_tensor(mm[:, b, 1, :], ps_s[b][:, H * HW:SUMS], absn[:, b, :],
                                      ALU.add).then_inc(small, 1)
                dve.wait_ge(lg_ok, v + 1)
                dve.scalar_tensor_tensor(e[:, b, :], lg[:, b, :], SLOPE, lg[:, b, :], ALU.mult,
                                         ALU.max).then_inc(e_ok, 1)
                if merging:
                    dve.wait_ge(small, w * 3 + 3)
                    if not (number and v < 4):
                        dve.wait_ge(acc_out[b], (w - b) * 8)
                    dve.tensor_tensor(acc[:, b, H * HW:SUMS], mm[:, b, 0, :], mm[:, b, 1, :],
                                      ALU.max).then_inc(max_ok, 1)
                if not (number and v == 0):
                    messages(v - 1, (s - 1) % SLOTS)
                if merging:
                    dve.wait_ge(max_ok, w + 1)
                    below_new_maximum(b)

                dve.wait_ge(eT_ps, v + 1)
                if not (number and v < 2):
                    dve.wait_ge(m_ps, v - 1)
                dve.tensor_tensor_scan(runf[:, b, :], penr[:, s, 0:GE], ps_e[0:H, 0:GE], NEG,
                                       ALU.add, ALU.max).then_inc(runf_ok, 1)
                dve.wait_ge(runf_ok, v + 1)
                dve.tensor_tensor_scan(runm[:, b, ::-1], penr[:, s, GE:0:-1], runf[:, b, ::-1], NEG,
                                       ALU.add, ALU.max).then_inc(runm_ok, 1)
                if not (number and v >= V - 2):
                    select(v + 2, (s + 2) % SLOTS)

                dve.wait_ge(m_ps, v + 1)
                if merging:
                    dve.wait_ge(sums, v - 1)
                dve.tensor_tensor(dlt[:, b, :], e[:, b, :], ps_m[:, 0:C * H], ALU.subtract).then_inc(dlt_ok, 1)
                dve.tensor_tensor(msg[:, b, :, H * HW:SUMS],
                                  ps_m[:, 0:C * H].rearrange("p (c h) -> p c h", c=C),
                                  dme[:, s, :].unsqueeze(2).broadcast_to([P, C, H]),
                                  ALU.mult).then_inc(mend_ok, 1)
                if merging:
                    join(w, s)

            def messages(v, s):
                dve.wait_ge(p_ok, v + 1)
                dve.wait_ge(gathered[s], (v - s) * (4 * C) + 16 * C)
                m4 = msg[:, s % 2, :, 0:H * HW].rearrange("p c (h w) -> p c h w", w=HW)
                dve.tensor_tensor(m4[:, :, :, 0:DH],
                                  gat[:, s, :, 0:D].rearrange("p c (h d) -> p c h d", h=H),
                                  m4[:, :, :, DH:HW].broadcast_to([P, C, H, DH]),
                                  ALU.mult).then_inc(msg_ok, 1)

            def below_new_maximum(b):
                dve.tensor_tensor(dd[:, b, :, :], mm[:, b, :, :],
                                  acc[:, b, H * HW:SUMS].unsqueeze(1).broadcast_to([P, 2, H]),
                                  ALU.subtract).then_inc(dd_ok, 1)

            def join(v, s):
                b = s % 2
                dve.wait_ge(scaled, v * (2 * H) + 2 * H)
                dve.tensor_tensor(acc[:, b, 0:H * HW], acc[:, b, 0:H * HW], tmp[:, b, :],
                                  ALU.add).then_inc(acc_ok, 1)

            def merge_alone(v, s):
                b, o = s % 2, (s + 1) % 2
                dve.wait_ge(sums, v + 1)
                dve.tensor_scalar(absn[:, b, :], ps_s[b][:, 0:H * HW].rearrange("p (h w) -> p h w", w=HW)[:, :, DH],
                                  0.5, NEG, ALU.is_lt, ALU.mult).then_inc(small, 1)
                dve.tensor_scalar(mm[:, b, 0, :], acc[:, o, H * HW:SUMS], fresh[:, row_of(v)], None,
                                  ALU.add).then_inc(small, 1)
                dve.wait_ge(small, v * 3 + 2)
                dve.tensor_tensor(mm[:, b, 1, :], ps_s[b][:, H * HW:SUMS], absn[:, b, :],
                                  ALU.add).then_inc(small, 1)
                dve.wait_ge(small, v * 3 + 3)
                dve.wait_ge(acc_out[b], (v - b) * 8)
                dve.tensor_tensor(acc[:, b, H * HW:SUMS], mm[:, b, 0, :], mm[:, b, 1, :], ALU.max).then_inc(max_ok, 1)
                dve.wait_ge(max_ok, v + 1)
                below_new_maximum(b)
                join(v, s)

            visits(dve, step)
            messages(V - 1, (V - 1) % SLOTS)
            merge_alone(V - 2, (V - 2) % SLOTS)
            merge_alone(V - 1, (V - 1) % SLOTS)

        @block.tensor
        def _(pe):
            pe.wait_ge(blocks_in, 16 * C)
            pe.wait_ge(pool_ok, 3)

            def edge_terms(v, s):
                b = s % 2
                pe.wait_ge(in_[s], (v - s) * (4 * LOADS) + 16 * LOADS)
                if not (isinstance(v, int) and v < 2):
                    pe.wait_ge(zm_ok, v - 1)
                pe.matmul(ps_z[b][:, 0:C * HT], a16[:, s, :], bdm[:, :], start=True, stop=False,
                          skip_group_check=True)
                pe.wait_ge(ohT_ok, v + 1)
                for c in range(C):
                    for part in range(3):
                        pe.matmul(ps_z[b][:, c * HT:(c + 1) * HT], ohT[:, b, c * P:(c + 1) * P],
                                  er3[:, s, part * HT:(part + 1) * HT], start=False,
                                  stop=False, skip_group_check=True)
                if not (isinstance(v, int) and v < 1):
                    pe.wait_ge(oh_ok, v)
                settle(pe)
                for c in range(C):
                    last = pe.transpose(ps_o[:, c, :], ohT[:, b, c * P:(c + 1) * P], identb[:, :])
                last.then_inc(oh_ps, 1)

            def source_terms(v, s):
                pe.wait_ge(gathered[s], (v - s) * (4 * C) + 16 * C)
                pe.matmul(ps_z[s % 2][:, 0:C * HT].rearrange("p (c n) -> p c n", c=C), ident[:, :],
                          gat[:, s, :, D:ROW], start=False, stop=True, skip_group_check=True).then_inc(z_mm, 1)

            def turn_logits(v, s):
                b = s % 2
                pe.wait_ge(e_ok, v + 1)
                if not (isinstance(v, int) and v < 1):
                    pe.wait_ge(runf_ok, v)
                for c in range(C):
                    last = pe.transpose(ps_e[0:H, c * P:(c + 1) * P], e[:, b, c * H:(c + 1) * H], ident[:, :])
                last.then_inc(eT_ps, 1)

            def turn_maxima(v, s):
                b = s % 2
                pe.wait_ge(runm_ok, v + 1)
                if not (isinstance(v, int) and v < 1):
                    pe.wait_ge(mend_ok, v)
                settle(pe)
                for c in range(C):
                    last = pe.transpose(ps_m[:, c * H:(c + 1) * H], runm[0:H, b, c * P:(c + 1) * P],
                                        ident[0:H, 0:H])
                last.then_inc(m_ps, 1)

            def segment_sums(v, s, chunks):
                b = s % 2
                if chunks[0] == 0:
                    pe.wait_ge(msg_ok, v + 1)
                    pe.wait_ge(mend_ok, v + 1)
                    pe.wait_ge(oh_ok, v + 1)
                    if not (isinstance(v, int) and v < 2):
                        pe.wait_ge(acc_ok, v - 1)
                for c in chunks:
                    last = pe.matmul(ps_s[b][:, 0:SUMS], oh[:, s, c, :], msg[:, b, c, :],
                                     start=(c == 0), stop=(c == C - 1), skip_group_check=True)
                if c == C - 1:
                    last.then_inc(sums, 1)

            edge_terms(0, 0)
            source_terms(0, 0)

            def step(v, s):
                more = not (isinstance(v, int) and v == V - 1)
                if more:
                    edge_terms(v + 1, (s + 1) % SLOTS)
                turn_logits(v, s)
                if not (isinstance(v, int) and v == 0):
                    segment_sums(v - 1, (s - 1) % SLOTS, range(0, EARLY))
                turn_maxima(v, s)
                if more:
                    source_terms(v + 1, (s + 1) % SLOTS)
                if not (isinstance(v, int) and v == 0):
                    segment_sums(v - 1, (s - 1) % SLOTS, range(EARLY, C))

            visits(pe, step)
            segment_sums(V - 1, (V - 1) % SLOTS, range(C))


def phase_ffn(nc, io, scr):
    B = 4
    NB = -(-NT // B)
    with ExitStack() as ctx:
        kit = Kit(nc, ctx)
        sb, ps, sem = kit.sb, kit.ps, kit.sem
        w_raw = sb("w_raw", [P, 2, 3, KD, D])
        w_lo = [sb(f"w_lo{i}", [P, X, KD, D], F32R) for i in range(3)]
        w_hi = [sb(f"w_hi{i}", [P, X, KD, D], F32R) for i in range(3)]
        wr = sb("wr", [P, KD, X])
        brb = sb("brb", [P, X])
        bo = sb("bo", [X, D])
        bn = sb("bn", [P, 10, X * KD])
        sc = sb("fsc", [P, 2, X * KD])
        sh = sb("fsh", [P, 2, X * KD])
        ident = sb("ident3", [P, P])
        eps = sb("feps", [P, 2])
        am = sb("am", [P, B, SUMS])
        xm = sb("xm", [P, B, D])
        rs = sb("rs", [P, B, H])
        x2 = sb("x2", [P, 2, B, D])
        st = sb("fst", [P, B, 6])
        mv = sb("fmv", [P, B, 2])
        sd = sb("fsd", [P, B])
        xn = sb("fxn", [P, B, D])
        xnT = sb("fxnT", [P, KD, B * P])
        xnT_lo = sb("fxnT_lo", [P, 2, KD, B * P], F32R)
        xnT_hi = sb("fxnT_hi", [P, 2, KD, B * P], F32R)
        lo = sb("lo", [P, B, X])
        lm = sb("lm", [P, B])
        w = sb("w", [P, 2, B, X])
        wT = sb("wT", [X, B * P])
        h1 = sb("h1", [P, KD, B * P])
        h1_lo = sb("h1_lo", [P, 2, KD, B * P], F32R)
        h1_hi = sb("h1_hi", [P, 2, KD, B * P], F32R)
        h2 = sb("h2", [P, KD, B * P])
        h2_lo = sb("h2_lo", [P, 2, KD, B * P], F32R)
        h2_hi = sb("h2_hi", [P, 2, KD, B * P], F32R)
        y = sb("y", [P, 2, B, D])

        ps_t = ps("ps_t", [P, KD, B * P])
        ps_h = [ps(f"ps_h{i}", [P, B * P]) for i in range(4)]
        ps_y = ps("ps_y", [P, B, D])
        bo_y = ps_t[:, :, :].rearrange("p k (a n) -> p (k a) n", n=D)

        weights_in = sem("f_weights_in")
        bn_in = sem("f_bn_in")
        pool_step = sem("f_pool_step")
        pool_ok = sem("f_pool_ok")
        bn_sd = sem("f_bn_sd")
        bn_step = sem("f_bn_step")
        bn_ok = sem("f_bn_ok")
        in_ = sem("f_in")
        w_in = [sem(f"f_w_in{i}") for i in range(2)]
        r0 = sem("f_r0")
        r1 = sem("f_r1")
        v_ok = sem("f_v_ok")
        x2_ok = sem("f_x2_ok")
        st_ok = sem("f_st_ok")
        mv_ok = sem("f_mv_ok")
        sd_ok = sem("f_sd_ok")
        rsd_ok = sem("f_rsd_ok")
        xn_ok = sem("f_xn_ok")
        xnT_ps = sem("f_xnT_ps")
        xnT_ok = sem("f_xnT_ok")
        rt_ps = sem("f_rt_ps")
        lo_ok = sem("f_lo_ok")
        lm_ok = sem("f_lm_ok")
        ls_ok = sem("f_ls_ok")
        le_ok = sem("f_le_ok")
        lsum_ok = sem("f_lsum_ok")
        lrec_ok = sem("f_lrec_ok")
        w_ok = sem("f_w_ok")
        wT_ps = sem("f_wT_ps")
        wT_ok = sem("f_wT_ok")
        bo_ps = sem("f_bo_ps")
        y0_ok = sem("f_y0_ok")
        w_top = sem("f_w_top")
        w_parts = sem("f_w_parts")
        xnT_top = sem("f_xnT_top")
        xnT_parts = sem("f_xnT_parts")
        h1_raw = sem("f_h1_raw")
        h1_top = sem("f_h1_top")
        h2_raw = sem("f_h2_raw")
        h2_top = sem("f_h2_top")
        h1_ps = sem("f_h1_ps")
        h1_ok = sem("f_h1_ok")
        h2_ps = sem("f_h2_ps")
        h2_ok = sem("f_h2_ok")
        y_ps = sem("f_y_ps")
        y_ok = sem("f_y_ok")
        y_out = [sem(f"f_y_out{i}") for i in range(2)]
        block = ctx.enter_context(nc.Block())

        def halves(n):
            return -(-n // 2)

        FULL = NT // B
        assert FULL % 2 == 0 and NB == FULL + 1

        def blocks(eng, prepare, up, middle, down):

            def block_of(b, s, n, following):
                for x in range(X):
                    if x < X - 1:
                        up(b, s, n, x + 1)
                    elif following:
                        up(b + 1, 1 - s, following, 0)
                    middle(b, s, n, x)
                    if x > 0:
                        down(b, s, n, x - 1)
                    elif not (isinstance(b, int) and b == 0):
                        down(b - 1, 1 - s, B, X - 1)
                    if following:
                        prepare(b + 1, 1 - s, following, x)

            for x in range(X):
                prepare(0, 0, B, x)
            up(0, 0, B, 0)
            for b in range(2):
                block_of(b, b % 2, B, B)
            with eng.Fori(0, (FULL - 4) // 2) as k:
                for u in (0, 1):
                    block_of(k * 2 + (2 + u), u, B, B)
            block_of(FULL - 2, 0, B, B)
            block_of(FULL - 1, 1, B, NT - FULL * B)
            block_of(FULL, 0, NT - FULL * B, 0)
            down(FULL, 0, NT - FULL * B, X - 1)

        @block.sync
        def _(sp):
            sp.dma_start(bn[:, :, :], io["bn"].rearrange("p (k n) -> p k n", k=10)).then_inc(bn_in, 16)
            sp.dma_start(wr[:, :, :], io["Wr"].rearrange("(c p) n -> p c n", p=P)).then_inc(weights_in, 16)
            sp.dma_start(brb[:, :], io["br"].rearrange("(a n) -> a n", a=1).broadcast_to([P, X])).then_inc(weights_in, 16)
            sp.dma_start(bo[:, :], io["bo"]).then_inc(weights_in, 16)

            def load(b, n):
                if not (isinstance(b, int) and b == 0):
                    sp.wait_ge(x2_ok, b)
                sp.dma_start(am[:, 0:n, :], scr["acc"][row_of(b * B, n), :, :].rearrange("a p c -> p a c")).then_inc(in_, 16)
                sp.dma_start(xm[:, 0:n, :], scr["xmix"][row_of(b * B, n), :, :].rearrange("a p c -> p a c")).then_inc(in_, 16)

            def load_weights(x):
                if x >= 2:
                    sp.wait_ge(w_parts, 3 * (x - 1))
                for i, name in enumerate(("W1", "W2", "Wo")):
                    sp.dma_start(w_raw[:, x % 2, i, :, :],
                                 io[name][x].rearrange("(c p) n -> p c n", p=P)).then_inc(w_in[x % 2], 16)

            load(0, B)
            load_weights(0)
            load_weights(1)
            load(1, B)
            for x in range(2, X):
                load_weights(x)
            with sp.Fori(0, FULL - 2) as k:
                load(k + 2, B)
            load(FULL, NT - FULL * B)

        @block.gpsimd
        def _(pool):
            pool.memset(ident[:, :], 0.0).then_inc(pool_step, 1)
            pool.memset(eps[:, 0:1], LN_EPS).then_inc(pool_ok, 1)
            pool.memset(eps[:, 1:2], BN_EPS).then_inc(pool_ok, 1)
            pool.wait_ge(pool_step, 1)
            pool.affine_select(out=ident[:, :], in_=ident[:, :], compare_op=ALU.not_equal, fill=1.0,
                               base=0, pattern=[[-1, P]], channel_multiplier=1).then_inc(pool_ok, 1)

            def store(b, s, n):
                pool.wait_ge(y_ok, b * (2 * X) + X * halves(n))
                pool.wait_ge(pool_ok, 3)
                if n == B:
                    pool.dma_start(io["out"][row_of(b * (B * P), B * P), :].rearrange("(a p) c -> p a c", p=P),
                                   y[:, s, :, :]).then_inc(y_out[s], 16)
                else:
                    pool.dma_start(io["out"][N - LAST:N, :], y[0:LAST, s, 0, :]).then_inc(y_out[s], 16)

            for b in range(2):
                store(b, b % 2, B)
            with pool.Fori(0, (FULL - 2) // 2) as k:
                for u in (0, 1):
                    store(k * 2 + (2 + u), u, B)
            store(FULL, 0, NT - FULL * B)
            pool.wait_ge(y_out[0], 16 * ((NB + 1) // 2))
            pool.wait_ge(y_out[1], 16 * (NB // 2))

        @block.scalar
        def _(act):
            act.wait_ge(bn_in, 16)
            act.wait_ge(pool_ok, 3)
            for layer in range(2):
                act.activation(sc[:, layer, :], bn[:, 5 * layer + 4, :], ACT.Sqrt, bias=eps[:, 1:2]).then_inc(bn_sd, 1)
            act.wait_ge(bn_ok, 2)

            def prepare(b, s, n, x):
                if x == 1:
                    act.wait_ge(mv_ok, b + 1)
                    act.activation(sd[:, 0:n], mv[:, 0:n, 1], ACT.Sqrt, bias=eps[:, 0:1]).then_inc(sd_ok, 1)
                elif x == 2:
                    act.wait_ge(xnT_ps, b + 1)
                    act.copy(xnT[:, :, 0:n * P], ps_t[:, :, 0:n * P]).then_inc(xnT_ok, 1)
                elif x == 5:
                    act.wait_ge(ls_ok, b + 1)
                    act.activation(lo[:, 0:n, :], lo[:, 0:n, :], ACT.Exp).then_inc(le_ok, 1)

            def relu(b, n, x, layer, hid, raw):
                for m in range(KD):
                    act.activation(hid[:, m, 0:n * P], ps_h[2 * layer + m][:, 0:n * P], ACT.Relu,
                                   bias=sh[:, layer, x * KD + m:x * KD + m + 1],
                                   scale=sc[:, layer, x * KD + m:x * KD + m + 1]).then_inc(raw, 1)

            def up(b, s, n, x):
                act.wait_ge(h1_ps, b * X + (x + 1))
                if not (isinstance(b, int) and b == 0 and x == 0):
                    act.wait_ge(h1_ok, b * X + x)
                relu(b, n, x, 0, h1, h1_raw)

            def middle(b, s, n, x):
                act.wait_ge(h2_ps, b * X + (x + 1))
                if not (isinstance(b, int) and b == 0 and x == 0):
                    act.wait_ge(h2_ok, b * X + x)
                relu(b, n, x, 1, h2, h2_raw)

            blocks(act, prepare, up, middle, lambda b, s, n, x: None)

        @block.vector
        def _(dve):
            dve.wait_ge(bn_sd, 2)
            dve.reciprocal(sc[:, :, :], sc[:, :, :]).then_inc(bn_step, 1)
            for layer in range(2):
                dve.tensor_tensor(sh[:, layer, :], bn[:, 5 * layer, :], bn[:, 5 * layer + 3, :],
                                  ALU.subtract).then_inc(bn_step, 1)
            dve.wait_ge(bn_step, 3)
            for layer in range(2):
                dve.tensor_tensor(sc[:, layer, :], sc[:, layer, :], bn[:, 5 * layer + 1, :], ALU.mult).then_inc(bn_step, 1)
            dve.wait_ge(bn_step, 5)
            dve.tensor_tensor(sh[:, :, :], sh[:, :, :], sc[:, :, :], ALU.mult).then_inc(bn_step, 1)
            dve.wait_ge(bn_step, 6)
            for layer in range(2):
                dve.tensor_tensor(sh[:, layer, :], sh[:, layer, :], bn[:, 5 * layer + 2, :], ALU.add).then_inc(bn_ok, 1)
            dve.wait_ge(weights_in, 16 * 3)

            def split(hi, lo, whole, top, of, parts):
                dve.tensor_copy(hi, whole).then_inc(top, 1)
                dve.wait_ge(top, of)
                dve.tensor_tensor(lo, whole, hi.bitcast(F32), ALU.subtract).then_inc(parts, 1)

            def split_weights(x):
                dve.wait_ge(w_in[x % 2], 48 * (x // 2 + 1))
                for i in range(3):
                    split(w_hi[i][:, x, :, :], w_lo[i][:, x, :, :], w_raw[:, x % 2, i, :, :], w_top, 3 * x + i + 1, w_parts)

            def prepare(b, s, n, x):
                heads = am[:, 0:n, 0:H * HW].rearrange("p a (h w) -> p a h w", w=HW)
                if x == 0:
                    dve.wait_ge(in_, b * 32 + 32)
                    dve.tensor_scalar(rs[:, 0:n, :], heads[:, :, :, DH], 1e-30, None, ALU.max).then_inc(r0, 1)
                    dve.wait_ge(r0, b + 1)
                    dve.reciprocal(rs[:, 0:n, :], rs[:, 0:n, :]).then_inc(r1, 1)
                    dve.wait_ge(r1, b + 1)
                    for a in range(n):
                        dve.tensor_tensor(x2[:, s, a, :].rearrange("p (h d) -> p h d", h=H), heads[:, a, :, 0:DH],
                                          rs[:, a, :].unsqueeze(2).broadcast_to([P, H, DH]), ALU.mult).then_inc(v_ok, 1)
                    dve.wait_ge(v_ok, b * B + n)
                    dve.tensor_tensor(x2[:, s, 0:n, :], x2[:, s, 0:n, :], xm[:, 0:n, :], ALU.add).then_inc(x2_ok, 1)
                    dve.wait_ge(x2_ok, b + 1)
                    for a in range(n):
                        dve.bn_stats(st[:, a, :], x2[:, s, a, :]).then_inc(st_ok, 1)
                    dve.wait_ge(st_ok, b * B + n)
                    settle(dve)
                    for a in range(n):
                        last = dve.bn_aggr(mv[:, a, :], st[:, a, :])
                    last.then_inc(mv_ok, 1)
                elif x == 2 and isinstance(b, int) and b == 0:
                    split_weights(0)
                    split_weights(1)
                elif x == 1:
                    dve.wait_ge(sd_ok, b + 1)
                    dve.reciprocal(sd[:, 0:n], sd[:, 0:n]).then_inc(rsd_ok, 1)
                    dve.wait_ge(rsd_ok, b + 1)
                    for a in range(n):
                        dve.tensor_scalar(xn[:, a, :], x2[:, s, a, :], mv[:, a, 0:1], sd[:, a:a + 1],
                                          ALU.subtract, ALU.mult).then_inc(xn_ok, 1)
                elif x == 4:
                    dve.wait_ge(rt_ps, b + 1)
                    dve.tensor_tensor(lo[:, 0:n, :], ps_t[:, 0, 0:n * X].rearrange("p (a x) -> p a x", x=X),
                                      brb[:, :].unsqueeze(1).broadcast_to([P, n, X]), ALU.add).then_inc(lo_ok, 1)
                    dve.wait_ge(lo_ok, b + 1)
                    dve.tensor_reduce(lm[:, 0:n], lo[:, 0:n, :], AX_X, ALU.max).then_inc(lm_ok, 1)
                    dve.wait_ge(lm_ok, b + 1)
                    dve.tensor_tensor(lo[:, 0:n, :], lo[:, 0:n, :], lm[:, 0:n].unsqueeze(2).broadcast_to([P, n, X]),
                                      ALU.subtract).then_inc(ls_ok, 1)
                    split(xnT_hi[:, s, :, 0:n * P], xnT_lo[:, s, :, 0:n * P], xnT[:, :, 0:n * P], xnT_top, b + 1, xnT_parts)
                elif x == 5:
                    dve.wait_ge(le_ok, b + 1)
                    dve.tensor_reduce(lm[:, 0:n], lo[:, 0:n, :], AX_X, ALU.add).then_inc(lsum_ok, 1)
                    dve.wait_ge(lsum_ok, b + 1)
                    dve.reciprocal(lm[:, 0:n], lm[:, 0:n]).then_inc(lrec_ok, 1)
                    dve.wait_ge(lrec_ok, b + 1)
                    dve.tensor_tensor(w[:, s, 0:n, :], lo[:, 0:n, :], lm[:, 0:n].unsqueeze(2).broadcast_to([P, n, X]),
                                      ALU.mult).then_inc(w_ok, 1)
                elif x == 6:
                    dve.wait_ge(wT_ps, b + 1)
                    dve.tensor_copy(wT[:, 0:n * P], ps_t[0:X, 1, 0:n * P]).then_inc(wT_ok, 1)
                elif x == 7:
                    dve.wait_ge(bo_ps, b + 1)
                    if later(b):
                        dve.wait_ge(y_out[s], (b - s) * 8)
                    dve.tensor_tensor(y[:, s, 0:n, :], bo_y[:, 0:n, :], x2[:, s, 0:n, :], ALU.add).then_inc(y0_ok, 1)

            def up(b, s, n, x):
                dve.wait_ge(h1_raw, b * (2 * X) + (2 * x + 2))
                if not (isinstance(b, int) and b == 0 and x < 2):
                    dve.wait_ge(h2_ps, b * X + (x - 1))
                split(h1_hi[:, x % 2, :, 0:n * P], h1_lo[:, x % 2, :, 0:n * P], h1[:, :, 0:n * P],
                      h1_top, b * X + (x + 1), h1_ok)

            def middle(b, s, n, x):
                dve.wait_ge(h2_raw, b * (2 * X) + (2 * x + 2))
                if not (isinstance(b, int) and b == 0 and x < 2):
                    if x < 2:
                        dve.wait_ge(y_ps, b * (2 * X) + (2 * x - 2))
                    else:
                        dve.wait_ge(y_ps, b * (2 * X) + (x - 1) * halves(n))
                split(h2_hi[:, x % 2, :, 0:n * P], h2_lo[:, x % 2, :, 0:n * P], h2[:, :, 0:n * P],
                      h2_top, b * X + (x + 1), h2_ok)
                if isinstance(b, int) and b == 0 and x + 2 < X:
                    split_weights(x + 2)

            def down(b, s, n, x):
                for half in range(halves(n)):
                    dve.wait_ge(y_ps, b * (2 * X) + (x * halves(n) + half + 1))
                    if x == 0:
                        dve.wait_ge(y0_ok, b + 1)
                    else:
                        dve.wait_ge(y_ok, b * (2 * X) + ((x - 1) * halves(n) + half + 1))
                    for a in range(2 * half, min(2 * half + 2, n)):
                        ins = dve.scalar_tensor_tensor(y[:, s, a, :], ps_y[:, a, :], w[:, s, a, x:x + 1],
                                                       y[:, s, a, :], ALU.mult, ALU.add)
                    ins.then_inc(y_ok, 1)

            blocks(dve, prepare, up, middle, down)

        @block.tensor
        def _(pe):
            pe.wait_ge(pool_ok, 3)
            pe.wait_ge(weights_in, 16 * 3)

            def prepare(b, s, n, x):
                if x == 2:
                    pe.wait_ge(xn_ok, b * B + n)
                    if not (isinstance(b, int) and b == 0):
                        pe.wait_ge(y0_ok, b)
                    settle(pe)
                    for k in range(KD):
                        for a in range(n):
                            last = pe.transpose(ps_t[:, k, a * P:(a + 1) * P], xn[:, a, k * P:(k + 1) * P], ident[:, :])
                    last.then_inc(xnT_ps, 1)
                elif x == 3:
                    pe.wait_ge(xnT_ok, b + 1)
                    for a in range(n):
                        for k in range(KD):
                            last = pe.matmul(ps_t[:, 0, a * X:(a + 1) * X], xnT[:, k, a * P:(a + 1) * P],
                                             wr[:, k, :], start=(k == 0), stop=(k == KD - 1), skip_group_check=True)
                    last.then_inc(rt_ps, 1)
                elif x == 6:
                    pe.wait_ge(w_ok, b + 1)
                    for a in range(n):
                        last = pe.transpose(ps_t[0:X, 1, a * P:(a + 1) * P], w[:, s, a, :], ident[:, :])
                    last.then_inc(wT_ps, 1)
                elif x == 7:
                    pe.wait_ge(wT_ok, b + 1)
                    for a in range(n):
                        last = pe.matmul(bo_y[:, a, :], wT[:, a * P:(a + 1) * P], bo[:, :], start=True, stop=True)
                    last.then_inc(bo_ps, 1)

            def in_parts(out, a_hi, a_lo, b_hi, b_lo, start, stop):
                pe.matmul(out, a_hi, b_hi, start=start, stop=False)
                pe.matmul(out, a_hi, b_lo, start=False, stop=False)
                return pe.matmul(out, a_lo, b_hi, start=False, stop=stop)

            def layer(done, src_hi, src_lo, i, x, n):
                for m in range(KD):
                    for k in range(KD):
                        cols = slice(m * P, (m + 1) * P)
                        last = in_parts(ps_h[2 * i + m][:, 0:n * P], w_hi[i][:, x, k, cols], w_lo[i][:, x, k, cols],
                                        src_hi[:, k, 0:n * P], src_lo[:, k, 0:n * P], k == 0, k == KD - 1)
                last.then_inc(done, 1)

            def up(b, s, n, x):
                if isinstance(b, int) and b == 0:
                    pe.wait_ge(w_parts, 3 * x + 1)
                if not (isinstance(b, int) and b == 0 and x == 0):
                    pe.wait_ge(h1_raw, b * (2 * X) + 2 * x)
                pe.wait_ge(xnT_parts, b + 1)
                layer(h1_ps, xnT_hi[:, s, :, :], xnT_lo[:, s, :, :], 0, x, n)

            def middle(b, s, n, x):
                if isinstance(b, int) and b == 0:
                    pe.wait_ge(w_parts, 3 * x + 2)
                pe.wait_ge(h1_ok, b * X + (x + 1))
                if not (isinstance(b, int) and b == 0 and x == 0):
                    pe.wait_ge(h2_raw, b * (2 * X) + 2 * x)
                layer(h2_ps, h1_hi[:, x % 2, :, :], h1_lo[:, x % 2, :, :], 1, x, n)

            def down(b, s, n, x):
                if isinstance(b, int) and b == 0:
                    pe.wait_ge(w_parts, 3 * x + 3)
                pe.wait_ge(h2_ok, b * X + (x + 1))
                for half in range(halves(n)):
                    if x > 0:
                        pe.wait_ge(y_ok, b * (2 * X) + ((x - 1) * halves(n) + half + 1))
                    elif not (isinstance(b, int) and b == 0):
                        pe.wait_ge(y_ok, b * (2 * X) - (1 - half))
                    for a in range(2 * half, min(2 * half + 2, n)):
                        rows = slice(a * P, (a + 1) * P)
                        for k in range(KD):
                            last = in_parts(ps_y[:, a, :], h2_hi[:, x % 2, k, rows], h2_lo[:, x % 2, k, rows],
                                            w_hi[2][:, x, k, :], w_lo[2][:, x, k, :], k == 0, k == KD - 1)
                    last.then_inc(y_ps, 1)

            blocks(pe, prepare, up, middle, down)


INPUTS = {
    "x": ((NT, P, D), F32), "W_n": ((D, D), F32), "W_nT": ((D, D), F32),
    "attn_l": ((H, DH, T), F32), "attn_r": ((H, DH, T), F32), "attn_m": ((H, F, T), F32),
    "Wqkv": ((D, 3 * D), F32), "Wout": ((D, D), F32), "gamma": ((D,), F32),
    "src": ((G, P, C), I32), "a4": ((G, P, C * T), F32), "a16": ((G, C * F, P), F32),
    "dst_em": ((EP,), I32), "dst_next_em": ((EP,), I32), "dst_lin": ((EP,), I32),
    "dst_prev_lin": ((EP,), I32), "group_first": ((G - 1,), I32),
    "Wr": ((D, X), F32), "br": ((X,), F32), "W1": ((X, D, D), F32), "W2": ((X, D, D), F32),
    "Wo": ((X, D, D), F32), "bo": ((X, D), F32), "bn": ((P, 10 * X * KD), F32),
}
SCRATCH = {
    "table": ((NT, P, ROW), F32), "er": ((NT, P, 3 * HT), BF16), "xmix": ((NT, P, D), F32),
    "dm": ((G, P, C), F32), "dst16": ((EP,), U16), "pen": ((EP + 1,), BF16),
    "visit_group": ((VP,), I32), "visit_tile": ((VP,), I32), "visit_tile_f": ((VP,), F32),
    "acc": ((NT, P, SUMS), F32),
}


def build(nc):
    io = {n: nc.dram_tensor(f"in_{n}", s, dt, kind="ExternalInput").ap() for n, (s, dt) in INPUTS.items()}
    io["out"] = nc.dram_tensor("out", (N, D), F32, kind="ExternalOutput").ap()
    scr = {n: nc.dram_tensor(f"scratch_{n}", s, dt).ap() for n, (s, dt) in SCRATCH.items()}
    scr["table_rows"] = scr["table"].rearrange("t p c -> (t p) c")
    phase_nodes(nc, io, scr)
    phase_edge_tables(nc, io, scr)
    phase_edges(nc, io, scr)
    phase_ffn(nc, io, scr)


def lay_out(i):
    import numpy as np

    def edges(a, fill=0):
        a = np.asarray(a)
        out = np.full((EP,) + a.shape[1:], fill, a.dtype)
        out[:E] = a
        return out

    def edge_major(a):
        return a.reshape(G, C, P).transpose(0, 2, 1)

    dst = edges(i["dst"], PAD_DST)
    following = np.full(EP, -1, dst.dtype)
    following[:-1] = dst[1:]
    following[GE - 1::GE] = -1
    before = np.full(EP, -1, dst.dtype)
    before[1:] = dst[:-1]
    x = np.asarray(i["x"])
    xp = np.zeros((NP, D), x.dtype)
    xp[:N] = x
    bn = np.stack([np.asarray(i["L0_ffn_" + n]).reshape(X, KD, P).transpose(2, 0, 1).reshape(P, X * KD)
                   for n in ("b1", "g1", "be1", "m1", "v1", "b2", "g2", "be2", "m2", "v2")], axis=1)
    laid = {
        "x": xp.reshape(NT, P, D), "W_nT": np.asarray(i["L0_gnn_W_n"]).T,
        "src": edge_major(edges(i["src"])),
        "a4": edges(i["edge_attr_4"]).reshape(G, C, P, T).transpose(0, 2, 1, 3).reshape(G, P, C * T),
        "a16": edges(i["edge_attr_16"]).reshape(G, C, P, F).transpose(0, 1, 3, 2).reshape(G, C * F, P),
        "dst_em": edge_major(dst).reshape(-1), "dst_next_em": edge_major(following).reshape(-1),
        "dst_lin": dst, "dst_prev_lin": before, "group_first": dst[GE::GE], "bn": bn.reshape(P, 10 * X * KD),
    }
    for n in ("W_n", "attn_l", "attn_r", "attn_m"):
        laid[n] = i["L0_gnn_" + n]
    for n in ("Wqkv", "Wout", "gamma"):
        laid[n] = i["L0_mix_" + n]
    for n in ("Wr", "br", "W1", "W2", "Wo", "bo"):
        laid[n] = i["L0_ffn_" + n]
    return {f"in_{n}": np.ascontiguousarray(laid[n]) for n in INPUTS}


def kernel(**inputs):
    import concourse.bacc as bacc
    from concourse.bass_utils import run_bass_kernel_spmd

    nc = bacc.Bacc("TRN2", target_bir_lowering=False, num_devices=1)
    build(nc)
    r = run_bass_kernel_spmd(nc, [lay_out(inputs)], core_ids=[0])
    return r.results[0]["out"]
```
